# Optimizing a Trainium2 kernel written in Bass

```python
import numpy as np
import jax
import jax.numpy as jnp

def _softmax(x, axis=-1):
    return jax.nn.softmax(x, axis=axis)

def _gelu(x):
    return jax.nn.gelu(x, approximate=True)

def _silu(x):
    return jax.nn.silu(x)

def _sigmoid(x):
    return jax.nn.sigmoid(x)

def _layernorm(x, axis=-1, eps=1e-05):
    m = jnp.mean(x, axis=axis, keepdims=True)
    v = jnp.var(x, axis=axis, keepdims=True)
    return (x - m) / jnp.sqrt(v + eps)

def _scatter_add(tgt, idx, src, axis=0):
    return tgt.at[idx].add(src)

def _segment_sum(src, seg, n):
    return jax.ops.segment_sum(src, seg, n)
kernel_name = 'mk_sandwich_d1_jaxref_r8_21e0ab'

def setup_inputs(seed: int=0):
    np.random.seed(seed)
    _w = jnp.asarray

    def _L0_attn_setup():
        import jax, jax.numpy as jnp
        import numpy as np
        import math
        D_MODEL = 128
        N_HEADS = 16
        HEAD_DIM = D_MODEL // N_HEADS

        def alibi_slopes(n_heads: int) -> jnp.ndarray:

            def pow2_slopes(n):
                start = 2 ** (-2 ** (-(math.log2(n) - 3)))
                return [start * start ** i for i in range(n)]
            if math.log2(n_heads).is_integer():
                s = pow2_slopes(n_heads)
            else:
                c = 2 ** math.floor(math.log2(n_heads))
                s = pow2_slopes(c)
                s.extend(pow2_slopes(2 * c)[0::2][:n_heads - c])
            return jnp.array(s, dtype=jnp.float32)
        key = jax.random.key(seed)
        ks = jax.random.split(key, 5)
        B, T, C = (2, 256, D_MODEL)
        std = 1.0 / math.sqrt(C)
        return {'x': jax.random.normal(ks[0], (B, T, C), dtype=jnp.float32), 'Wq': jax.random.normal(ks[1], (C, C), dtype=jnp.float32) * std, 'bq': jnp.zeros((C,), dtype=jnp.float32), 'Wk': jax.random.normal(ks[2], (C, C), dtype=jnp.float32) * std, 'bk': jnp.zeros((C,), dtype=jnp.float32), 'Wv': jax.random.normal(ks[3], (C, C), dtype=jnp.float32) * std, 'bv': jnp.zeros((C,), dtype=jnp.float32), 'Wo': jax.random.normal(ks[4], (C, C), dtype=jnp.float32) * std, 'bo': jnp.zeros((C,), dtype=jnp.float32)}
    _L0_attn_in = _L0_attn_setup()

    def _L0_ffn_setup():
        import jax, jax.numpy as jnp
        import numpy as np
        import math
        B, S, D = (4, 256, 128)
        H = 16
        E = 8
        K = 2
        F = 512

        def _layernorm(x, g, b, eps=1e-05):
            mu = jnp.mean(x, axis=-1, keepdims=True)
            var = jnp.mean(jnp.square(x - mu), axis=-1, keepdims=True)
            return (x - mu) * jax.lax.rsqrt(var + eps) * g + b

        def _attention(x, Wq, bq, Wk, bk, Wv, bv, Wo, bo):
            b, s, d = x.shape
            dh = d // H
            q = (x @ Wq + bq).reshape(b, s, H, dh)
            k = (x @ Wk + bk).reshape(b, s, H, dh)
            v = (x @ Wv + bv).reshape(b, s, H, dh)
            scores = jnp.einsum('bqhd,bkhd->bhqk', q, k) / math.sqrt(dh)
            attn = jax.nn.softmax(scores, axis=-1)
            out = jnp.einsum('bhqk,bkhd->bqhd', attn, v).reshape(b, s, d)
            return out @ Wo + bo

        def _moe(x, gate_w, gate_b, W1, b1, W2, b2):
            b, s, d = x.shape
            xt = x.reshape(b * s, d)
            probs = jax.nn.softmax(xt @ gate_w + gate_b, axis=-1)
            top_v, top_i = jax.lax.top_k(probs, K)
            combine = jnp.sum(jax.nn.one_hot(top_i, E, dtype=xt.dtype) * top_v[..., None], axis=1)
            out = jnp.zeros_like(xt)
            for e in range(E):
                h = jax.nn.gelu(xt @ W1[e] + b1[e], approximate=False) @ W2[e] + b2[e]
                out = out + combine[:, e:e + 1] * h
            return out.reshape(b, s, d)
        key = jax.random.key(seed)
        ks = jax.random.split(key, 16)
        s_d = 1.0 / math.sqrt(D)
        s_f = 1.0 / math.sqrt(F)
        return {'x': jax.random.normal(ks[0], (B, S, D), jnp.float32), 'Wq': jax.random.normal(ks[1], (D, D), jnp.float32) * s_d, 'Wk': jax.random.normal(ks[2], (D, D), jnp.float32) * s_d, 'Wv': jax.random.normal(ks[3], (D, D), jnp.float32) * s_d, 'Wo': jax.random.normal(ks[4], (D, D), jnp.float32) * s_d, 'bq': jnp.zeros((D,), jnp.float32), 'bk': jnp.zeros((D,), jnp.float32), 'bv': jnp.zeros((D,), jnp.float32), 'bo': jnp.zeros((D,), jnp.float32), 'ln1_g': jnp.ones((D,), jnp.float32), 'ln1_b': jnp.zeros((D,), jnp.float32), 'ln2_g': jnp.ones((D,), jnp.float32), 'ln2_b': jnp.zeros((D,), jnp.float32), 'gate_w': jax.random.normal(ks[5], (D, E), jnp.float32) * s_d, 'gate_b': jnp.zeros((E,), jnp.float32), 'W1': jax.random.normal(ks[6], (E, D, F), jnp.float32) * s_d, 'b1': jnp.zeros((E, F), jnp.float32), 'W2': jax.random.normal(ks[7], (E, F, D), jnp.float32) * s_f, 'b2': jnp.zeros((E, D), jnp.float32)}
    _L0_ffn_in = _L0_ffn_setup()
    _d = {'L0_attn_x': _L0_attn_in['x'], 'L0_attn_Wq': _L0_attn_in['Wq'], 'L0_attn_bq': _L0_attn_in['bq'], 'L0_attn_Wk': _L0_attn_in['Wk'], 'L0_attn_bk': _L0_attn_in['bk'], 'L0_attn_Wv': _L0_attn_in['Wv'], 'L0_attn_bv': _L0_attn_in['bv'], 'L0_attn_Wo': _L0_attn_in['Wo'], 'L0_attn_bo': _L0_attn_in['bo'], 'L0_ffn_Wq': _L0_ffn_in['Wq'], 'L0_ffn_bq': _L0_ffn_in['bq'], 'L0_ffn_Wk': _L0_ffn_in['Wk'], 'L0_ffn_bk': _L0_ffn_in['bk'], 'L0_ffn_Wv': _L0_ffn_in['Wv'], 'L0_ffn_bv': _L0_ffn_in['bv'], 'L0_ffn_Wo': _L0_ffn_in['Wo'], 'L0_ffn_bo': _L0_ffn_in['bo'], 'L0_ffn_ln1_g': _L0_ffn_in['ln1_g'], 'L0_ffn_ln1_b': _L0_ffn_in['ln1_b'], 'L0_ffn_ln2_g': _L0_ffn_in['ln2_g'], 'L0_ffn_ln2_b': _L0_ffn_in['ln2_b'], 'L0_ffn_gate_w': _L0_ffn_in['gate_w'], 'L0_ffn_gate_b': _L0_ffn_in['gate_b'], 'L0_ffn_W1': _L0_ffn_in['W1'], 'L0_ffn_b1': _L0_ffn_in['b1'], 'L0_ffn_W2': _L0_ffn_in['W2'], 'L0_ffn_b2': _L0_ffn_in['b2']}
    _x0 = _d['L0_attn_x']
    _d['L0_attn_x'] = jax.random.normal(jax.random.fold_in(jax.random.key(seed), 1), (4, 1024, 128), dtype=_x0.dtype)
    del _x0
    return _d

def reference(L0_attn_x, L0_attn_Wq, L0_attn_bq, L0_attn_Wk, L0_attn_bk, L0_attn_Wv, L0_attn_bv, L0_attn_Wo, L0_attn_bo, L0_ffn_Wq, L0_ffn_bq, L0_ffn_Wk, L0_ffn_bk, L0_ffn_Wv, L0_ffn_bv, L0_ffn_Wo, L0_ffn_bo, L0_ffn_ln1_g, L0_ffn_ln1_b, L0_ffn_ln2_g, L0_ffn_ln2_b, L0_ffn_gate_w, L0_ffn_gate_b, L0_ffn_W1, L0_ffn_b1, L0_ffn_W2, L0_ffn_b2):

    def _L0_attn_ref(x, Wq, bq, Wk, bk, Wv, bv, Wo, bo):
        import jax, jax.numpy as jnp
        import numpy as np
        import math
        D_MODEL = 128
        N_HEADS = 16
        HEAD_DIM = D_MODEL // N_HEADS

        def alibi_slopes(n_heads: int) -> jnp.ndarray:

            def pow2_slopes(n):
                start = 2 ** (-2 ** (-(math.log2(n) - 3)))
                return [start * start ** i for i in range(n)]
            if math.log2(n_heads).is_integer():
                s = pow2_slopes(n_heads)
            else:
                c = 2 ** math.floor(math.log2(n_heads))
                s = pow2_slopes(c)
                s.extend(pow2_slopes(2 * c)[0::2][:n_heads - c])
            return jnp.array(s, dtype=jnp.float32)
        B, T, C = x.shape
        H, D = (N_HEADS, HEAD_DIM)
        scale = D ** (-0.5)
        q = (x @ Wq + bq).reshape(B, T, H, D).transpose(0, 2, 1, 3)
        k = (x @ Wk + bk).reshape(B, T, H, D).transpose(0, 2, 1, 3)
        v = (x @ Wv + bv).reshape(B, T, H, D).transpose(0, 2, 1, 3)
        scores = jnp.einsum('bhqd,bhkd->bhqk', q, k) * scale
        pos = (jnp.arange(T)[:, None] - jnp.arange(T)[None, :]).astype(jnp.float32)
        bias = alibi_slopes(H)[:, None, None] * pos
        scores = scores + bias[None]
        causal = jnp.tril(jnp.ones((T, T), dtype=bool))
        scores = jnp.where(causal, scores, -jnp.inf)
        attn = jax.nn.softmax(scores, axis=-1)
        out = jnp.einsum('bhqk,bhkd->bhqd', attn, v)
        out = out.transpose(0, 2, 1, 3).reshape(B, T, C)
        return out @ Wo + bo

    def _L0_ffn_ref(x, Wq, bq, Wk, bk, Wv, bv, Wo, bo, ln1_g, ln1_b, ln2_g, ln2_b, gate_w, gate_b, W1, b1, W2, b2):
        import jax, jax.numpy as jnp
        import numpy as np
        import math
        B, S, D = (4, 256, 128)
        H = 16
        E = 8
        K = 2
        F = 512

        def _layernorm(x, g, b, eps=1e-05):
            mu = jnp.mean(x, axis=-1, keepdims=True)
            var = jnp.mean(jnp.square(x - mu), axis=-1, keepdims=True)
            return (x - mu) * jax.lax.rsqrt(var + eps) * g + b

        def _attention(x, Wq, bq, Wk, bk, Wv, bv, Wo, bo):
            b, s, d = x.shape
            dh = d // H
            q = (x @ Wq + bq).reshape(b, s, H, dh)
            k = (x @ Wk + bk).reshape(b, s, H, dh)
            v = (x @ Wv + bv).reshape(b, s, H, dh)
            scores = jnp.einsum('bqhd,bkhd->bhqk', q, k) / math.sqrt(dh)
            attn = jax.nn.softmax(scores, axis=-1)
            out = jnp.einsum('bhqk,bkhd->bqhd', attn, v).reshape(b, s, d)
            return out @ Wo + bo

        def _moe(x, gate_w, gate_b, W1, b1, W2, b2):
            b, s, d = x.shape
            xt = x.reshape(b * s, d)
            probs = jax.nn.softmax(xt @ gate_w + gate_b, axis=-1)
            top_v, top_i = jax.lax.top_k(probs, K)
            combine = jnp.sum(jax.nn.one_hot(top_i, E, dtype=xt.dtype) * top_v[..., None], axis=1)
            out = jnp.zeros_like(xt)
            for e in range(E):
                h = jax.nn.gelu(xt @ W1[e] + b1[e], approximate=False) @ W2[e] + b2[e]
                out = out + combine[:, e:e + 1] * h
            return out.reshape(b, s, d)
        x = x + _layernorm(_attention(x, Wq, bq, Wk, bk, Wv, bv, Wo, bo), ln1_g, ln1_b)
        x = x + _layernorm(_moe(x, gate_w, gate_b, W1, b1, W2, b2), ln2_g, ln2_b)
        return x
    x = L0_attn_x
    x = x + _layernorm(_L0_attn_ref(_layernorm(x, axis=-1), L0_attn_Wq, L0_attn_bq, L0_attn_Wk, L0_attn_bk, L0_attn_Wv, L0_attn_bv, L0_attn_Wo, L0_attn_bo), axis=-1)
    x = x + _layernorm(_L0_ffn_ref(_layernorm(x, axis=-1), L0_ffn_Wq, L0_ffn_bq, L0_ffn_Wk, L0_ffn_bk, L0_ffn_Wv, L0_ffn_bv, L0_ffn_Wo, L0_ffn_bo, L0_ffn_ln1_g, L0_ffn_ln1_b, L0_ffn_ln2_g, L0_ffn_ln2_b, L0_ffn_gate_w, L0_ffn_gate_b, L0_ffn_W1, L0_ffn_b1, L0_ffn_W2, L0_ffn_b2), axis=-1)
    return x

_drawn_inputs = setup_inputs


def setup_inputs(seed=0):
    import zlib

    import numpy as np

    out = dict(_drawn_inputs(seed))
    spreads = {'L0_attn_bq': (0.0, 0.1),
     'L0_attn_bk': (0.0, 0.8),
     'L0_attn_bv': (0.0, 0.1),
     'L0_attn_bo': (0.0, 0.1),
     'L0_ffn_bq': (0.0, 0.343),
     'L0_ffn_bk': (0.0, 0.8),
     'L0_ffn_bv': (0.0, 0.1),
     'L0_ffn_bo': (0.0, 0.1),
     'L0_ffn_ln1_g': (1.0, 0.2),
     'L0_ffn_ln1_b': (0.0, 0.1),
     'L0_ffn_ln2_g': (1.0, 0.2),
     'L0_ffn_ln2_b': (0.0, 0.325),
     'L0_ffn_gate_b': (0.0, 0.1),
     'L0_ffn_b1': (0.0, 0.444),
     'L0_ffn_b2': (0.0, 0.314)}
    factors = {}
    for name, (base, spread) in spreads.items():
        noise = np.random.default_rng([zlib.crc32(name.encode()), seed]).standard_normal(out[name].shape)
        drawn = base * np.exp(spread * noise) if base else spread * noise
        out[name] = jnp.asarray(drawn.astype(out[name].dtype))
    for name, factor in factors.items():
        out[name] = (out[name] * factor).astype(out[name].dtype)
    return out
```

```python
from contextlib import ExitStack

import concourse.bass as bass
from concourse import mybir

F32 = mybir.dt.float32
F32R = mybir.dt.float32r
BF16 = mybir.dt.bfloat16
ALU = mybir.AluOpType
ACT = mybir.ActivationFunctionType
AX = mybir.AxisListType

P = 128
D = 128
B, T = 4, 1024
TB = T // P
NT = B * TB
H, DH = 16, 8
GH = 4
G = H // GH
S = B * G
HW = P // GH
SCALE = DH ** -0.5
EPS = 1e-5
E, FF = 8, 512
FT = FF // P
HALF = 512
HQ = HALF // P
BIG = -1.0e30

ROW_BIAS = 3 * DH
ROW_MAX = 3 * DH + 2


def slopes():
    start = 2.0 ** (-(2.0 ** (3 - 4)))
    return [start * start ** i for i in range(H)]


class Plan:

    def __init__(self, causal):
        self.causal = causal
        self.chunks = []
        for qt in range(TB):
            for kh in range(2):
                n = min(HALF, (qt + 1) * P - kh * HALF) if causal else HALF
                if n <= 0:
                    continue
                per = max(1, HALF // n)
                per = 4 if per >= 4 else per
                for j in range(0, GH, per):
                    self.chunks.append((qt, kh, list(range(j, j + per)), n))
        self.quads = []
        for qh in range(2):
            for kt in range((qh + 1) * HQ if causal else TB):
                self.quads.append((qh, kt))
        self.na = len(self.chunks)
        self.nq = len(self.quads)
        self.nb = GH * self.nq
        self.half_end = [max(i for i, q in enumerate(self.quads) if q[0] == h) for h in range(2)]
        nq = self.nq
        self.lead = 2
        a_steps = nq - 4
        self.a_next = -(-self.na * 4 // nq)
        own = self.na - self.a_next
        self.a_of_step = []
        for i in range(nq):
            if i < a_steps:
                lo, hi = own * i // a_steps, own * (i + 1) // a_steps
                self.a_of_step.append([(1, self.a_next + c) for c in range(lo, hi)])
            else:
                k = i - a_steps
                lo, hi = self.a_next * k // 4, self.a_next * (k + 1) // 4
                self.a_of_step.append([(2, c) for c in range(lo, hi)])
        self.m_step = a_steps - 1
        o0 = self.half_end[0] + 3 - self.lead
        free = [i for i in range(1, nq - 4) if i != o0]
        self.proj_steps = [free[len(free) * i // 4] for i in range(4)]
        self.o_steps = (o0, nq - 1)
        self.mt_steps = (a_steps, a_steps + 1)

    def interleave(self, bs, ass):
        out = []
        nb, na = len(bs), len(ass)
        for i in range(nb):
            out.append(bs[i])
            out += ass[na * i // nb:na * (i + 1) // nb]
        return out if nb else list(ass)

    def body(self, do_proj=True, do_a1=True, do_a2=True):
        out = []
        for i in range(self.nq):
            for n, at in enumerate(self.proj_steps):
                if at == i and do_proj:
                    out.append(("proj", 3, n))
            if i == self.o_steps[0]:
                out.append(("otr", 0, 0))
            q = i + self.lead
            ds, q = (0, q) if q < self.nq else (1, q - self.nq)
            bs = [("b", ds, q * GH + j) for j in range(GH)] if ds == 0 or do_a1 else []
            ass = [("a", d, c) for d, c in self.a_of_step[i] if (do_a1 if d == 1 else do_a2)]
            out += self.interleave(bs, ass)
            if i == self.m_step and do_a1:
                out.append(("m", 1, 0))
            dp, p = (ds, q - 1) if q else (0, self.nq - 1)
            if dp == 0 or do_a1:
                out.append(("pv", dp, p))
                if p in self.half_end:
                    out.append(("oev", dp, self.half_end.index(p)))
            if i in self.mt_steps and do_a1:
                out.append(("mtr", 1, self.mt_steps.index(i)))
            if i == self.o_steps[1]:
                out.append(("otr", 0, 1))
        return out

    def prologue(self):
        out = [("proj", 0, n) for n in range(4)]
        out += self.interleave([("proj", s, n) for s in (1, 2) for n in range(4)],
                               [("a", 0, c) for c in range(self.na)])
        out += [("m", 0, 0), ("mtr", 0, 0), ("mtr", 0, 1)]
        bs = [("b", 0, i) for i in range(GH * self.lead)]
        out += self.interleave(bs[:GH], [("a", 1, c) for c in range(self.a_next)])
        out += bs[GH:] + [("pv", 0, 0)]
        return out


def last_user(n, i, banks):
    return (0, i - banks) if i >= banks else (1, max(k for k in range(n) if k % banks == i))


class Register:

    def __init__(self, eng, value):
        self.eng, self.value, self.kept = eng, value, {}

    def __mul__(self, k):
        if k not in self.kept:
            self.kept[k] = self.eng.snap(self.value * k)
        return self.kept[k]

    def __add__(self, n):
        return self if n == 0 else Shifted(self, n)


class Shifted:

    def __init__(self, register, n):
        self.register, self.n = register, n

    def __mul__(self, k):
        return self.register * k + self.n * k


class Slot:

    def __init__(self, batch, g):
        self.batch, self.g = batch, g

    def __add__(self, n):
        return Slot(self.batch, self.g + n)

    def __sub__(self, n):
        return Slot(self.batch, self.g - n)

    def count(self, per, more=0):
        return self.batch * (G * per) + (self.g * per + more)


def attention(nc, tag, plan, xT, values, heads_out, w3, bias2, slope_row, iota_row, split_sign,
              head_mask, ident, ident16, causal_mask):
    causal = plan.causal
    NA, NB, NQ = plan.na, plan.nb, plan.nq
    with ExitStack() as ctx:
        def sb(name, shape, dt=F32):
            return ctx.enter_context(nc.sbuf_tensor(f"{tag}_{name}", shape, dt))

        def sem(name):
            return ctx.enter_context(nc.semaphore(f"{tag}_{name}"))

        def bank(name):
            return ctx.enter_context(nc.psum_tensor(f"{tag}_{name}", [P, HALF], F32))

        km = [sb(f"km{i}", [P, GH, T], F32R) for i in range(4)]
        fq = [sb(f"fq{i}", [P, T], F32R) for i in range(4)]
        fqm = [sb(f"fqm{i}", [P, T], F32R) for i in range(2)]
        u = [sb(f"u{i}", [P, HALF]) for i in range(2)]
        hi = sb("hi", [P, HALF], F32R)
        part = sb("part", [P, HALF])
        fk = sb("fk", [P, HALF])
        probs = [sb(f"probs{i}", [P, HALF]) for i in range(8)]
        vst = [sb(f"vst{i}", [P, TB, GH, HW]) for i in range(2)]
        mx = sb("mx", [P, 2, TB, GH])
        mfull = sb("mfull", [P, TB, GH])
        mhi = sb("mhi", [P, TB, GH], F32R)
        mpad = sb("mpad", [P, TB, P])
        osb = sb("osb", [P, 2, HALF])
        rec = sb("rec", [P, HQ, GH])
        a_bank = [bank(f"a{i}") for i in range(3)]
        b_bank = [bank(f"b{i}") for i in range(3)]
        pv_bank = bank("pv")
        misc = bank("misc")

        proj_made = sem("proj_made")
        proj_read = sem("proj_read")
        split_done = sem("split_done")
        pool_step = sem("pool_step")
        pool_passed = sem("pool_passed")
        v_staged = sem("v_staged")
        a_made = sem("a_made")
        a_read = sem("a_read")
        m_step = sem("m_step")
        m_padded = sem("m_padded")
        m_turned = sem("m_turned")
        fqm_made = sem("fqm_made")
        b_made = sem("b_made")
        exp_done = sem("exp_done")
        pv_done = sem("pv_done")
        o_read = sem("o_read")
        o_turned = sem("o_turned")
        o_step = sem("o_step")
        o_done = sem("o_done")
        init = sem("init")

        def done(eng, semaphore, per, s, i):
            eng.wait_ge(semaphore, (s + 1).count(per, i + 1))

        block = ctx.enter_context(nc.Block())

        def run(eng, emit):
            emit(plan.prologue(), Slot(0, 0), 0, 0)
            with eng.Fori(0, B - 1) as batch:
                b = Register(eng, batch)
                for g in range(G):
                    emit(plan.body(), Slot(b, g), b, g)
            for g in range(G):
                s = (B - 1) * G + g
                emit(plan.body(s + 3 < S, s + 1 < S, s + 2 < S), Slot(B - 1, g), B - 1, g)

        def where(b, g, ds):
            return (b + (g + ds) // G, (g + ds) % G)

        @block.tensor
        def _(pe):
            pe.wait_ge(init, 4)
            for semaphore, per in ((proj_made, 4), (a_made, NA), (m_turned, 2), (b_made, NB),
                                   (pv_done, NQ), (o_turned, 2)):
                pe.sem_inc(semaphore, per)

            def emit(steps, s0, b0, g0):
                prologue = steps[0][0] == "proj" and steps[0][1] == 0
                before = None if prologue else ("otr", -1, 1)
                for what, ds, n in steps:
                    s = s0 + ds
                    if what in ("proj", "otr", "mtr"):
                        if before is not None:
                            bw, bs, bn = before
                            if bw == "proj":
                                done(pe, proj_read, 4, s0 + bs, bn)
                            elif bw == "mtr":
                                done(pe, fqm_made, 2, s0 + bs, bn)
                            else:
                                done(pe, o_done, 2, s0 + bs, bn)
                                if bs < 0:
                                    done(pe, fqm_made, 2, s0, 1)
                        before = (what, ds, n)
                    if what == "proj":
                        b, g = where(b0, g0, ds)
                        m, h = (1, n) if n < 2 else (0, n - 2)
                        x = xT[:, bass.ds(b * T + h * HALF, HALF)]
                        alibi = causal and m == 1
                        mm = pe.matmul(misc[:, :], w3[:, m, g, :], x, start=True, stop=not alibi)
                        if alibi:
                            mm = pe.matmul(misc[:, :], slope_row[0:1, g, :],
                                           iota_row[0:1, h * HALF:(h + 1) * HALF], start=False, stop=True)
                        mm.then_inc(proj_made, 1)
                    elif what == "a":
                        qt, kh, heads, w = plan.chunks[n]
                        _, g = where(b0, g0, ds)
                        if n == 0:
                            done(pe, split_done, 4, s, 3)
                        back, k = last_user(NA, n, 3)
                        done(pe, a_read, NA, s - back, k)
                        out = a_bank[n % 3]
                        diagonal = causal and kh * HALF + w == (qt + 1) * P
                        for i, j in enumerate(heads):
                            mm = pe.matmul(out[:, i * w:(i + 1) * w], fq[g][:, qt * P:(qt + 1) * P],
                                           km[g][:, j, kh * HALF:kh * HALF + w],
                                           start=True, stop=not diagonal)
                            if diagonal:
                                mm = pe.matmul(out[:, (i + 1) * w - P:(i + 1) * w], ident16[:, :],
                                               causal_mask[:, :], start=False, stop=True)
                        mm.then_inc(a_made, 1)
                    elif what == "mtr":
                        done(pe, m_padded, 1, s, 0)
                        for i in range(HQ):
                            mm = pe.transpose(misc[:, i * P:(i + 1) * P], mpad[:, n * HQ + i, :], ident[:, :])
                        mm.then_inc(m_turned, 1)
                    elif what == "b":
                        _, g = where(b0, g0, ds)
                        t, j = n // GH, n % GH
                        qh, kt = plan.quads[t]
                        if n == 0 or plan.quads[(n - 1) // GH][0] != qh:
                            done(pe, fqm_made, 2, s, qh)
                        back, k = last_user(NB, n, 3)
                        done(pe, exp_done, NB, s - back, k)
                        q0 = max(qh * HALF, kt * P) if causal else qh * HALF
                        w = (qh + 1) * HALF - q0
                        diagonal = causal and kt * P >= qh * HALF
                        out = b_bank[n % 3]
                        mm = pe.matmul(out[:, 0:w], km[g][:, j, kt * P:(kt + 1) * P],
                                       fqm[g % 2][:, q0:q0 + w], start=True, stop=not diagonal)
                        if diagonal:
                            mm = pe.matmul(out[:, 0:P], causal_mask[:, :], ident16[:, :],
                                           start=False, stop=True)
                        mm.then_inc(b_made, 1)
                    elif what == "pv":
                        _, g = where(b0, g0, ds)
                        qh, kt = plan.quads[n]
                        if n == 0:
                            done(pe, v_staged, 1, s, 0)
                        if n == 0 or plan.quads[n - 1][0] != qh:
                            done(pe, o_read, 2, s - (qh == 0), 1 - qh)
                        done(pe, exp_done, NB, s, GH * n + GH - 1)
                        q0 = max(qh * HALF, kt * P) if causal else qh * HALF
                        w = (qh + 1) * HALF - q0
                        for j in range(GH):
                            mm = pe.matmul(pv_bank[HW * j:HW * (j + 1), HALF - w:HALF],
                                           vst[g % 2][:, kt, j, :], probs[(n % 2) * GH + j][:, 0:w],
                                           start=(kt == 0), stop=(n == plan.half_end[qh]))
                        mm.then_inc(pv_done, 1)
                    elif what == "otr":
                        done(pe, o_read, 2, s, n)
                        for i in range(HQ):
                            mm = pe.transpose(misc[:, i * P:(i + 1) * P], osb[:, n, i * P:(i + 1) * P],
                                              ident[:, :])
                        mm.then_inc(o_turned, 1)

            run(pe, emit)

        @block.scalar
        def _(act):
            for semaphore, per in ((proj_read, 4), (exp_done, NB), (o_read, 2)):
                act.sem_inc(semaphore, per)

            def emit(steps, s0, b0, g0):
                for what, ds, n in steps:
                    s = s0 + ds
                    if what == "proj":
                        _, g = where(b0, g0, ds)
                        m = 1 if n < 2 else 0
                        done(act, proj_made, 4, s, n)
                        done(act, split_done, 4, s, n - 2)
                        act.activation(u[n % 2][:, :], misc[:, :], ACT.Identity,
                                       scale=1.0 if m else SCALE,
                                       bias=bias2[:, m, g:g + 1]).then_inc(proj_read, 1)
                    elif what == "b":
                        t, j = n // GH, n % GH
                        qh, kt = plan.quads[t]
                        q0 = max(qh * HALF, kt * P) if causal else qh * HALF
                        w = (qh + 1) * HALF - q0
                        done(act, b_made, NB, s, n)
                        if j == 0:
                            done(act, pv_done, NQ, s, t - 2)
                        act.activation(probs[(t % 2) * GH + j][:, 0:w], b_bank[n % 3][:, 0:w],
                                       ACT.Exp).then_inc(exp_done, 1)
                    elif what == "oev":
                        done(act, pv_done, NQ, s, plan.half_end[n])
                        done(act, o_turned, 2, s - 1, n)
                        act.activation(osb[:, n, :], pv_bank[:, :], ACT.Identity).then_inc(o_read, 1)

            run(act, emit)

        @block.vector
        def _(dve):
            for semaphore, per in ((a_read, NA), (m_padded, 1), (fqm_made, 2), (o_done, 2),
                                   (m_step, 2), (o_step, 2)):
                dve.sem_inc(semaphore, per)
            dve.wait_ge(init, 4)

            def emit(steps, s0, b0, g0):
                for what, ds, n in steps:
                    s = s0 + ds
                    b, g = where(b0, g0, ds)
                    if what == "a":
                        qt, kh, heads, w = plan.chunks[n]
                        done(dve, a_made, NA, s, n)
                        if n == 0:
                            done(dve, m_step, 2, s - 1, 0)
                        k = len(heads)
                        dve.tensor_reduce(mx[:, kh, qt, heads[0]:heads[0] + k],
                                          a_bank[n % 3][:, 0:k * w].rearrange("p (k w) -> p k w", k=k),
                                          AX.X, ALU.max).then_inc(a_read, 1)
                    elif what == "m":
                        done(dve, a_read, NA, s, NA - 1)
                        done(dve, m_step, 2, s - 1, 1)
                        done(dve, m_padded, 1, s - 1, 0)
                        done(dve, m_turned, 2, s - 1, 1)
                        dve.tensor_tensor(mfull[:, :, :], mx[:, 0, :, :], mx[:, 1, :, :],
                                          ALU.max).then_inc(m_step, 1)
                        done(dve, m_step, 2, s, 0)
                        dve.tensor_copy(mhi[:, :, :], mfull[:, :, :]).then_inc(m_step, 1)
                        done(dve, m_step, 2, s, 1)
                        pad = mpad[:, :, :].rearrange("p t (j r) -> p t j r", j=GH)
                        dve.tensor_copy(pad[:, :, :, ROW_MAX], mhi[:, :, :].bitcast(F32))
                        dve.tensor_tensor(pad[:, :, :, ROW_MAX + 1], mfull[:, :, :],
                                          mhi[:, :, :].bitcast(F32), ALU.subtract).then_inc(m_padded, 1)
                    elif what == "mtr":
                        done(dve, m_turned, 2, s, n)
                        h = slice(n * HALF, (n + 1) * HALF)
                        dve.tensor_tensor(fqm[g % 2][:, h], fq[g][:, h].bitcast(F32), misc[:, :],
                                          ALU.add).then_inc(fqm_made, 1)
                    elif what == "otr":
                        turned = misc[:, :].rearrange("p (t j c) -> p t j c", t=HQ, j=GH)
                        done(dve, o_turned, 2, s, n)
                        done(dve, o_done, 2, s, n - 1)
                        dve.reciprocal(rec[:, :, :], turned[:, :, :, DH]).then_inc(o_step, 1)
                        done(dve, o_step, 2, s, n)
                        dve.tensor_tensor(
                            heads_out[:, bass.ds(b * TB + n * HQ, HQ), g * GH * DH:(g + 1) * GH * DH]
                            .rearrange("p t (j c) -> p t j c", j=GH),
                            turned[:, :, :, 0:DH],
                            rec[:, :, :, None].broadcast_to([P, HQ, GH, DH]),
                            ALU.mult).then_inc(o_done, 1)

            run(dve, emit)

        @block.gpsimd
        def _(pool):
            for semaphore, per in ((split_done, 4), (v_staged, 1)):
                pool.sem_inc(semaphore, per)
            pool.memset(mpad[:, :, :], 0.0).then_inc(init, 1)
            pool.memset(mx[:, :, :, :], -3.0e38).then_inc(init, 1)
            for v in vst:
                pool.memset(v[:, :, :, :], 0.0).then_inc(pool_step, 1)
            pool.wait_ge(pool_step, 2)
            for v in vst:
                pool.memset(v[:, :, :, DH:DH + 1], 1.0).then_inc(init, 1)
            pool.wait_ge(init, 4)
            count = 2 * 3 + 2 * 2
            pool.sem_inc(pool_step, count - 2)

            def await_(semaphore, per, s, i):
                done(pool, semaphore, per, s, i)
                pool.sem_inc(pool_passed, 1)

            def stage_values(b, g):
                src = values[:, bass.ds(b * TB, TB), g * GH * DH:(g + 1) * GH * DH]
                pool.tensor_copy(vst[g % 2][:, :, :, 0:DH],
                                 src.rearrange("p t (j c) -> p t j c", j=GH)).then_inc(v_staged, 1)

            def emit(steps, s0, b0, g0):
                if steps[0][1] == 0 and steps[0][0] == "proj":
                    stage_values(0, 0)
                else:
                    if any(k[0] == "pv" and k[1] == 1 for k in steps):
                        b, g = where(b0, g0, 1)
                        await_(pv_done, NQ, s0 - 1, NQ - 1)
                        stage_values(b, g)
                first = True
                for what, ds, n in steps:
                    s = s0 + ds
                    if what != "proj":
                        continue
                    _, g = where(b0, g0, ds)
                    m, h = (1, n) if n < 2 else (0, n - 2)
                    if ds == 3 and first:
                        await_(b_made, NB, s - 4, NB - 1)
                        first = False
                    un = u[n % 2]
                    await_(proj_read, 4, s, n)
                    await_(split_done, 4, s, n - 1)
                    step = 3 * n if m else 6 + 2 * h
                    half = slice(h * HALF, (h + 1) * HALF)
                    pool.tensor_tensor(hi[:, :], un[:, :], split_sign[:, 2:3].broadcast_to([P, HALF]),
                                       ALU.add).then_inc(pool_step, 1)
                    await_(pool_step, count, s, step)
                    pool.tensor_tensor(part[:, :], hi[:, :].bitcast(F32),
                                       split_sign[:, m:m + 1].broadcast_to([P, HALF]),
                                       ALU.mult).then_inc(pool_step, 1)
                    await_(pool_step, count, s, step + 1)
                    if m == 0:
                        pool.tensor_tensor(fq[g][:, half], part[:, :], un[:, :],
                                           ALU.add).then_inc(split_done, 1)
                    else:
                        pool.tensor_tensor(fk[:, :], part[:, :], un[:, :], ALU.add).then_inc(pool_step, 1)
                        await_(pool_step, count, s, step + 2)
                        pool.tensor_tensor(km[g][:, :, half],
                                           fk[:, None, :].broadcast_to([P, GH, HALF]),
                                           head_mask[:, :, None].broadcast_to([P, GH, HALF]),
                                           ALU.mult).then_inc(split_done, 1)

            run(pool, emit)


def layernorm(nc, tag, src, dst, gain=None, shift=None, add=None, final=None):
    with ExitStack() as ctx:
        def sb(name, shape, dt=F32):
            return ctx.enter_context(nc.sbuf_tensor(f"{tag}_{name}", shape, dt))

        def sem(name):
            return ctx.enter_context(nc.semaphore(f"{tag}_{name}"))

        mean = sb("mean", [P, NT])
        total = sb("total", [P, NT])
        rstd = sb("rstd", [P, NT])
        square = sb("square", [P, 2, TB, D])
        centred = sem("centred")
        squared = sem("squared")
        reduced = sem("reduced")
        root = sem("root")
        step = sem("step")
        stored = sem("stored")
        ready = sem("ready")

        def tiles(x, b):
            return x[:, b * TB:(b + 1) * TB, :]

        def wide(x, b):
            return x[:, b * TB:(b + 1) * TB, None].broadcast_to([P, TB, D])

        def row(x):
            return x[:, None, :].broadcast_to([P, TB, D])

        block = ctx.enter_context(nc.Block())

        @block.vector
        def _(dve):
            for b in range(B):
                dve.tensor_reduce(total[:, b * TB:(b + 1) * TB], tiles(src, b), AX.X, ALU.add).then_inc(step, 1)
            dve.wait_ge(step, B)
            dve.tensor_scalar(mean[:, :], total[:, :], 1.0 / D, None, ALU.mult).then_inc(step, 1)
            dve.wait_ge(step, B + 1)
            for b in range(B):
                dve.tensor_tensor(tiles(dst, b), tiles(src, b), wide(mean, b), ALU.subtract).then_inc(centred, 1)
            for b in range(B):
                dve.wait_ge(squared, b + 1)
                dve.tensor_reduce(total[:, b * TB:(b + 1) * TB], square[:, b % 2], AX.X,
                                  ALU.add).then_inc(reduced, 1)
            dve.wait_ge(reduced, B)
            dve.tensor_scalar(mean[:, :], total[:, :], 1.0 / D, EPS, ALU.mult, ALU.add).then_inc(step, 1)
            dve.wait_ge(root, 1)
            dve.reciprocal(rstd[:, :], total[:, :]).then_inc(step, 1)
            n = B + 3
            dve.wait_ge(step, n)
            for b in range(B):
                ops = [(wide(rstd, b), ALU.mult)]
                if gain is not None:
                    ops += [(row(gain), ALU.mult), (row(shift), ALU.add)]
                if add is not None:
                    ops.append((tiles(add, b), ALU.add))
                for operand, op in ops:
                    dve.wait_ge(step, n)
                    last = dve.tensor_tensor(tiles(dst, b), tiles(dst, b), operand, op).then_inc(step, 1)
                    n += 1
                if final is not None:
                    dve.wait_ge(step, n)
                    dve.sem_inc(ready, 1)

        @block.scalar
        def _(act):
            for b in range(B):
                act.wait_ge(centred, b + 1)
                if b >= 2:
                    act.wait_ge(reduced, b - 1)
                act.activation(square[:, b % 2], tiles(dst, b), ACT.Square).then_inc(squared, 1)
            act.wait_ge(step, B + 2)
            act.activation(total[:, :], mean[:, :], ACT.Sqrt).then_inc(root, 1)

        if final is not None:
            @block.sync
            def _(sp):
                for b in range(B):
                    sp.wait_ge(ready, b + 1)
                    sp.dma_start(final[:, b * TB:(b + 1) * TB, :], tiles(dst, b)).then_inc(stored, 16)
                sp.wait_ge(stored, 16 * B)


def turn_and_project(nc, tag, src, turned, weight, bias_row, ones_row, ident, dst, width=D):
    with ExitStack() as ctx:
        def sem(name):
            return ctx.enter_context(nc.semaphore(f"{tag}_{name}"))

        t_bank = [ctx.enter_context(nc.psum_tensor(f"{tag}_t{i}", [P, 4, P], F32)) for i in range(3)]
        y_bank = [ctx.enter_context(nc.psum_tensor(f"{tag}_y{i}", [P, 4, width], F32)) for i in range(3)]
        t_made, t_read, y_made, y_read = sem("t_made"), sem("t_read"), sem("y_made"), sem("y_read")
        block = ctx.enter_context(nc.Block())
        groups = NT // 4

        @block.tensor
        def _(pe):
            def project(n):
                pe.wait_ge(t_read, n + 1)
                if n >= 3:
                    pe.wait_ge(y_read, n - 2)
                for i in range(4):
                    t = 4 * n + i
                    pe.matmul(y_bank[n % 3][:, i, :], turned[:, t * P:(t + 1) * P], weight[:, :],
                              start=True, stop=False)
                    mm = pe.matmul(y_bank[n % 3][:, i, :], ones_row[0:1, :], bias_row[0:1, 0:width],
                                   start=False, stop=True)
                mm.then_inc(y_made, 1)

            for n in range(groups):
                if n >= 3:
                    pe.wait_ge(t_read, n - 2)
                for i in range(4):
                    mm = pe.transpose(t_bank[n % 3][:, i, :], src[:, 4 * n + i, :], ident[:, :])
                mm.then_inc(t_made, 1)
                if n:
                    project(n - 1)
            project(groups - 1)

        @block.scalar
        def _(act):
            for n in range(groups):
                act.wait_ge(t_made, n + 1)
                act.activation(turned[:, n * HALF:(n + 1) * HALF],
                               t_bank[n % 3][:, :, :].rearrange("p a b -> p (a b)"),
                               ACT.Identity).then_inc(t_read, 1)

        @block.vector
        def _(dve):
            for n in range(groups):
                dve.wait_ge(y_made, n + 1)
                dve.tensor_copy(dst[:, 4 * n:4 * n + 4, :], y_bank[n % 3][:, :, :]).then_inc(y_read, 1)


def gate(nc, tag, logits, rank, comb, b2, ident, acc):
    with ExitStack() as ctx:
        def sb(name, shape, dt=F32):
            return ctx.enter_context(nc.sbuf_tensor(f"{tag}_{name}", shape, dt))

        def sem(name):
            return ctx.enter_context(nc.semaphore(f"{tag}_{name}"))

        top = sb("top", [P, NT])
        probs = sb("probs", [P, NT, E])
        rest = sb("rest", [P, NT, E])
        key = sb("key", [P, NT, E])
        chosen = sb("chosen", [P, NT, E])
        comb_t = sb("comb_t", [E, NT * P])
        t_bank = [ctx.enter_context(nc.psum_tensor(f"{tag}_t{i}", [E, 4, P], F32)) for i in range(2)]
        y_bank = [ctx.enter_context(nc.psum_tensor(f"{tag}_y{i}", [P, 4, D], F32)) for i in range(2)]
        step, exped = sem("step"), sem("exped")
        t_made, t_read, y_made, y_read = sem("t_made"), sem("t_read"), sem("y_made"), sem("y_read")
        block = ctx.enter_context(nc.Block())

        def wide(x):
            return x[:, :, None].broadcast_to([P, NT, E])

        ranks = rank[:, None, :].broadcast_to([P, NT, E])
        steps = 0

        @block.vector
        def _(dve):
            n = 0

            def chain(op):
                nonlocal n
                op.then_inc(step, 1)
                n += 1
                dve.wait_ge(step, n)

            chain(dve.tensor_reduce(top[:, :], logits[:, :, :], AX.X, ALU.max))
            chain(dve.tensor_tensor(rest[:, :, :], logits[:, :, :], wide(top), ALU.subtract))
            dve.wait_ge(exped, 1)
            chain(dve.tensor_reduce(top[:, :], key[:, :, :], AX.X, ALU.add))
            chain(dve.reciprocal(chosen[:, :, 0], top[:, :]))
            chain(dve.tensor_tensor(probs[:, :, :], key[:, :, :],
                                    chosen[:, :, 0:1].broadcast_to([P, NT, E]), ALU.mult))
            chain(dve.tensor_copy(rest[:, :, :], probs[:, :, :]))
            for k in range(2):
                chain(dve.tensor_reduce(top[:, :], rest[:, :, :], AX.X, ALU.max))
                chain(dve.tensor_tensor(key[:, :, :], rest[:, :, :], wide(top), ALU.is_equal))
                chain(dve.tensor_tensor(key[:, :, :], key[:, :, :], ranks, ALU.mult))
                chain(dve.tensor_reduce(top[:, :], key[:, :, :], AX.X, ALU.max))
                chain(dve.tensor_tensor(key[:, :, :], key[:, :, :], wide(top), ALU.is_equal))
                if k == 0:
                    chain(dve.tensor_copy(chosen[:, :, :], key[:, :, :]))
                    chain(dve.scalar_tensor_tensor(rest[:, :, :], key[:, :, :], -4.0, rest[:, :, :],
                                                   ALU.mult, ALU.add))
                else:
                    chain(dve.tensor_tensor(chosen[:, :, :], chosen[:, :, :], key[:, :, :], ALU.add))
            chain(dve.tensor_tensor(comb[:, :, :], probs[:, :, :], chosen[:, :, :], ALU.mult))
            dve.sem_inc(exped, 1)
            for i in range(NT // 4):
                dve.wait_ge(y_made, i + 1)
                dve.tensor_copy(acc[:, 4 * i:4 * i + 4, :], y_bank[i % 2][:, :, :]).then_inc(y_read, 1)

        @block.scalar
        def _(act):
            act.wait_ge(step, 2)
            act.activation(key[:, :, :], rest[:, :, :], ACT.Exp).then_inc(exped, 1)
            for i in range(NT // 4):
                act.wait_ge(t_made, i + 1)
                act.activation(comb_t[:, i * HALF:(i + 1) * HALF],
                               t_bank[i % 2][:, :, :].rearrange("p a b -> p (a b)"),
                               ACT.Identity).then_inc(t_read, 1)

        @block.tensor
        def _(pe):
            pe.wait_ge(exped, 2)

            def bias(n):
                pe.wait_ge(t_read, n + 1)
                if n >= 2:
                    pe.wait_ge(y_read, n - 1)
                for i in range(4):
                    t = 4 * n + i
                    mm = pe.matmul(y_bank[n % 2][:, i, :], comb_t[:, t * P:(t + 1) * P], b2[:, :],
                                   start=True, stop=True)
                mm.then_inc(y_made, 1)

            for n in range(NT // 4):
                if n >= 2:
                    pe.wait_ge(t_read, n - 1)
                for i in range(4):
                    mm = pe.transpose(t_bank[n % 2][:, i, :], comb[:, 4 * n + i, :], ident[:, :])
                mm.then_inc(t_made, 1)
                if n:
                    bias(n - 1)
            bias(NT // 4 - 1)


def experts(nc, tag, xT, comb, acc, W1, W2, b1t):
    NBLK = NT // HQ
    with ExitStack() as ctx:
        def sb(name, shape, dt=F32):
            return ctx.enter_context(nc.sbuf_tensor(f"{tag}_{name}", shape, dt))

        def sem(name):
            return ctx.enter_context(nc.semaphore(f"{tag}_{name}"))

        w1 = [sb(f"w1_{i}", [P, FF]) for i in range(2)]
        w2 = [sb(f"w2_{i}", [P, FT, D]) for i in range(2)]
        ht = [sb(f"ht{i}", [P, FT, HALF]) for i in range(2)]
        h_bank = [ctx.enter_context(nc.psum_tensor(f"{tag}_h{i}", [P, HALF], F32)) for i in range(4)]
        y_bank = [ctx.enter_context(nc.psum_tensor(f"{tag}_y{i}", [P, HQ, D], F32)) for i in range(3)]
        w_in = [sem(f"w_in{i}") for i in range(2)]
        h_made = sem("h_made")
        h_done = sem("h_done")
        y_made = sem("y_made")
        y_read = sem("y_read")
        block = ctx.enter_context(nc.Block())
        NH, NY = 2 * NBLK * FT, 2 * NBLK

        def done(eng, semaphore, per, s, i):
            s, back = s if type(s) is tuple else (s, 0)
            eng.wait_ge(semaphore, s * per + (per * (1 - back) + i + 1))

        @block.sync
        def _(sp):
            with sp.Fori(0, E // 2) as register:
                pair = Register(sp, register)
                for k in range(2):
                    done(sp, y_made, NY, (pair, 1), (k + 1) * NBLK - 1)
                    sp.dma_start(w1[k][:, :], W1[bass.ds(pair * 2 + k, 1), :, :]
                                 .rearrange("e p f -> p (e f)")).then_inc(w_in[k], 16)
                    sp.dma_start(w2[k][:, :, :], W2[bass.ds(pair * 2 + k, 1), :, :]
                                 .rearrange("e (t p) d -> p (e t) d", p=P)).then_inc(w_in[k], 16)

        @block.tensor
        def _(pe):
            pe.sem_inc(h_made, NH)
            pe.sem_inc(y_made, NY)

            def hidden(pair, n):
                k, blk = n // NBLK, n % NBLK
                if blk == 0:
                    pe.wait_ge(w_in[k], pair * 32 + 32)
                for f in range(FT):
                    done(pe, h_done, NH, pair, n * FT + f - 4)
                    pe.matmul(h_bank[f][:, :], w1[k][:, f * P:(f + 1) * P],
                              xT[:, blk * HALF:(blk + 1) * HALF], start=True, stop=True).then_inc(h_made, 1)

            def output(pair, n):
                k = n // NBLK
                done(pe, h_done, NH, pair, n * FT + FT - 1)
                back, m = last_user(NY, n, 3)
                done(pe, y_read, NY, (pair, back), m)
                for i in range(HQ):
                    for f in range(FT):
                        mm = pe.matmul(y_bank[n % 3][:, i, :], ht[n % 2][:, f, i * P:(i + 1) * P],
                                       w2[k][:, f, :], start=(f == 0), stop=(f == FT - 1))
                mm.then_inc(y_made, 1)

            with pe.Fori(0, E // 2) as register:
                pair = Register(pe, register)
                for n in range(NY):
                    hidden(pair, n)
                    if n:
                        output(pair, n - 1)
                output(pair, NY - 1)

        @block.scalar
        def _(act):
            act.sem_inc(h_done, NH)
            with act.Fori(0, E // 2) as register:
                pair = Register(act, register)
                for n in range(NY):
                    k = n // NBLK
                    done(act, y_made, NY, pair, n - 2)
                    for f in range(FT):
                        done(act, h_made, NH, pair, n * FT + f)
                        act.activation(ht[n % 2][:, f, :], h_bank[f][:, :], ACT.Gelu,
                                       bias=b1t[:, f, bass.ds(pair * 2 + k, 1)]).then_inc(h_done, 1)

        @block.vector
        def _(dve):
            dve.sem_inc(y_read, NY)
            with dve.Fori(0, E // 2) as register:
                pair = Register(dve, register)
                for n in range(NY):
                    k, blk = n // NBLK, n % NBLK
                    done(dve, y_made, NY, pair, n)
                    done(dve, y_read, NY, pair, n - NBLK)
                    for i in range(HQ):
                        t = blk * HQ + i
                        op = dve.scalar_tensor_tensor(acc[:, t, :], y_bank[n % 3][:, i, :],
                                                      comb[:, t, bass.ds(pair * 2 + k, 1)],
                                                      acc[:, t, :], ALU.mult, ALU.add)
                    op.then_inc(y_read, 1)


def build(nc, x, w, consts, out):
    with ExitStack() as ctx:
        def sb(name, shape, dt=F32):
            return ctx.enter_context(nc.sbuf_tensor(name, shape, dt))

        def sem(name):
            return ctx.enter_context(nc.semaphore(name))

        kept = nc.dram_tensor("kept", [P, NT, D], F32, kind="Internal").ap()
        x_v = x.rearrange("b (t p) d -> p (b t) d", p=P)
        out_v = out.rearrange("b (t p) d -> p (b t) d", p=P)
        resid = sb("resid", [P, NT, D])
        turned = sb("turned", [P, NT * P])
        tokens = sb("tokens", [P, NT, D])
        ident = sb("ident", [P, P])
        split_sign = sb("split_sign", [P, 3])
        head_mask = sb("head_mask", [P, GH])
        rank = sb("rank", [P, E])
        ones_row = sb("ones_row", [1, P])
        slope_row = sb("slope_row", [1, G, P])
        iota_row = sb("iota_row", [1, T])
        ident16 = sb("ident16", [P, P], BF16)
        causal_mask = sb("causal_mask", [P, P], BF16)
        w3 = [sb(f"w3_{i}", [P, 2, G, P]) for i in range(2)]
        bias2 = [sb(f"bias2_{i}", [P, 2, G]) for i in range(2)]
        wv = [sb(f"wv{i}", [P, D]) for i in range(2)]
        wo = [sb(f"wo{i}", [P, D]) for i in range(2)]
        bv = [sb(f"bv{i}", [1, D]) for i in range(2)]
        bo = [sb(f"bo{i}", [1, D]) for i in range(2)]
        ln_rows = {n: sb(n, [P, D]) for n in ("ln1_g", "ln1_b", "ln2_g", "ln2_b")}
        sides = ("L0_attn_", "L0_ffn_")

        with ExitStack() as c2:
            raw = [[c2.enter_context(nc.sbuf_tensor(f"raw{i}{m}", [P, D], F32)) for m in range(2)] for i in range(2)]
            raw_b = c2.enter_context(nc.sbuf_tensor("raw_b", [1, 2, 2, D], F32))
            row3 = c2.enter_context(nc.sbuf_tensor("row3", [1, 2, 2, G, P], F32))
            cols = c2.enter_context(nc.psum_tensor("cols", [P, 2 * 2 * G], F32))
            loaded = c2.enter_context(nc.semaphore("loaded"))
            zeroed = c2.enter_context(nc.semaphore("zeroed"))
            spread = c2.enter_context(nc.semaphore("spread"))
            turned_in = c2.enter_context(nc.semaphore("turned_in"))
            block = c2.enter_context(nc.Block())
            loads = [(raw[i][m][:, :], w[sides[i] + n]) for i in range(2) for m, n in ((0, "Wq"), (1, "Wk"))]
            loads += [(raw_b[0:1, i, m, :], w[sides[i] + n].rearrange("(a d) -> a d", a=1))
                      for i in range(2) for m, n in ((0, "bq"), (1, "bk"))]
            loads += [(wv[i][:, :], w[sides[i] + "Wv"]) for i in range(2)]
            loads += [(wo[i][:, :], w[sides[i] + "Wo"]) for i in range(2)]
            loads += [(bv[i][:, :], w[sides[i] + "bv"].rearrange("(a d) -> a d", a=1)) for i in range(2)]
            loads += [(bo[i][:, :], w[sides[i] + "bo"].rearrange("(a d) -> a d", a=1)) for i in range(2)]
            loads += [(t[:, :], w["L0_ffn_" + n].rearrange("(a d) -> a d", a=1).broadcast_to([P, D]))
                      for n, t in ln_rows.items()]
            loads += [(ident[:, :], consts["ident"]), (split_sign[:, :], consts["split_sign"]),
                      (head_mask[:, :], consts["head_mask"]), (rank[:, :], consts["rank"]),
                      (ones_row[:, :], consts["ones_row"]), (iota_row[:, :], consts["iota_row"]),
                      (slope_row[:, :, :], consts["slope_row"])]
            f32_mask = c2.enter_context(nc.sbuf_tensor("f32_mask", [P, P], F32))
            loads += [(f32_mask[:, :], consts["causal"])]

            @block.sync
            def _(sp):
                for b in range(B):
                    sp.dma_start(resid[:, b * TB:(b + 1) * TB, :], x_v[:, b * TB:(b + 1) * TB, :]).then_inc(loaded, 16)
                for dst, src in loads[0::2]:
                    sp.dma_start(dst, src).then_inc(loaded, 16)

            everything = 16 * (B + len(loads))

            @block.scalar
            def _(act):
                for dst, src in loads[1::2]:
                    act.dma_start(dst, src).then_inc(loaded, 16)
                act.wait_ge(turned_in, 1)
                v = cols[:, :].rearrange("p (i m g) -> p i m g", i=2, m=2)
                for i in range(2):
                    op = act.activation(bias2[i][:, :, :], v[:, i, :, :], ACT.Identity)
                op.then_inc(turned_in, 1)

            @block.gpsimd
            def _(pool):
                for i in range(2):
                    pool.memset(w3[i][:, :, :, :], 0.0)
                pool.memset(row3[:, :, :, :, :], 0.0).then_inc(zeroed, 1)
                pool.wait_ge(zeroed, 1)
                pool.wait_ge(loaded, everything)
                pool.tensor_copy(ident16[:, :], ident[:, :])
                pool.tensor_copy(causal_mask[:, :], f32_mask[:, :])
                for i in range(2):
                    for m in range(2):
                        dst = w3[i][:, m, :, :].rearrange("p g (j r) -> p (g j) r", j=GH)
                        row = row3[0:1, i, m, :, :].rearrange("p g (j r) -> p (g j) r", j=GH)
                        for k in range(3):
                            pool.tensor_copy(dst[:, :, k * DH:(k + 1) * DH],
                                             raw[i][m][:, :].rearrange("p (h d) -> p h d", h=H))
                            src = raw_b[0:1, i, m, :].rearrange("p (h d) -> p h d", h=H)
                            if m == 0:
                                pool.tensor_scalar(row[:, :, k * DH:(k + 1) * DH], src, SCALE, None, ALU.mult)
                            else:
                                pool.tensor_copy(row[:, :, k * DH:(k + 1) * DH], src)
                        one, at = (1.0, ROW_BIAS) if m == 0 else (-1.0, ROW_MAX)
                        op = pool.memset(row[:, :, at:at + 2], one)
                op.then_inc(spread, 1)

            @block.tensor
            def _(pe):
                pe.wait_ge(spread, 1)
                for i in range(2):
                    for m in range(2):
                        for g in range(G):
                            c = (i * 2 + m) * G + g
                            mm = pe.matmul(cols[:, c:c + 1], row3[0:1, i, m, g, :], ones_row[0:1, 0:1],
                                           start=True, stop=True)
                mm.then_inc(turned_in, 1)

        with ExitStack() as c2:
            normed = c2.enter_context(nc.sbuf_tensor("normed", [P, NT, D], F32))
            layernorm(nc, "ln_in", resid, normed)
            turn_and_project(nc, "v1", normed, turned, wv[0], bv[0], ones_row, ident, tokens)
        attention(nc, "at1", Plan(True), turned, tokens, tokens, w3[0], bias2[0], slope_row, iota_row,
                  split_sign, head_mask, ident, ident16, causal_mask)
        with ExitStack() as c2:
            y = c2.enter_context(nc.sbuf_tensor("y1", [P, NT, D], F32))
            y2 = c2.enter_context(nc.sbuf_tensor("y2", [P, NT, D], F32))
            turn_and_project(nc, "o1", tokens, turned, wo[0], bo[0], ones_row, ident, y)
            layernorm(nc, "ln_a1", y, y2, add=resid, final=kept)
            layernorm(nc, "ln_f", y2, resid)
            turn_and_project(nc, "v2", resid, turned, wv[1], bv[1], ones_row, ident, tokens)
        attention(nc, "at2", Plan(False), turned, tokens, tokens, w3[1], bias2[1], slope_row, iota_row,
                  split_sign, head_mask, ident, ident16, causal_mask)
        y = sb("y3", [P, NT, D])
        turn_and_project(nc, "o2", tokens, turned, wo[1], bo[1], ones_row, ident, y)
        layernorm(nc, "ln_a2", y, tokens, ln_rows["ln1_g"], ln_rows["ln1_b"], resid)
        acc = sb("acc", [P, NT, D])
        logits = sb("logits", [P, NT, E])
        comb = sb("comb", [P, NT, E])
        gate_w = sb("gate_w", [P, E])
        gate_b = sb("gate_b", [1, E])
        b2 = sb("b2", [E, D])
        b1t = sb("b1t", [P, FT, E])
        with ExitStack() as c2:
            b1 = c2.enter_context(nc.sbuf_tensor("b1", [E, FF], F32))
            cols = c2.enter_context(nc.psum_tensor("b1cols", [P, FT, E], F32))
            got = c2.enter_context(nc.semaphore("moe_got"))
            tr = c2.enter_context(nc.semaphore("moe_tr"))
            block = c2.enter_context(nc.Block())

            @block.sync
            def _(sp):
                sp.dma_start(gate_w[:, :], w["L0_ffn_gate_w"]).then_inc(got, 16)
                sp.dma_start(gate_b[:, :], w["L0_ffn_gate_b"].rearrange("(a d) -> a d", a=1)).then_inc(got, 16)
                sp.dma_start(b2[:, :], w["L0_ffn_b2"]).then_inc(got, 16)
                sp.dma_start(b1[:, :], w["L0_ffn_b1"]).then_inc(got, 16)
                sp.dma_start(resid[:, :, :], kept).then_inc(got, 16)

            @block.tensor
            def _(pe):
                pe.wait_ge(got, 16 * 5)
                for f in range(FT):
                    mm = pe.transpose(cols[:, f, :], b1[:, f * P:(f + 1) * P], ident[0:E, 0:E])
                mm.then_inc(tr, 1)

            @block.vector
            def _(dve):
                dve.wait_ge(tr, 1)
                dve.tensor_copy(b1t[:, :, :], cols[:, :, :]).then_inc(tr, 1)
        turn_and_project(nc, "gt", tokens, turned, gate_w, gate_b, ones_row, ident, logits, width=E)
        gate(nc, "gate", logits, rank, comb, b2, ident, acc)
        experts(nc, "moe", turned, comb, acc, w["L0_ffn_W1"], w["L0_ffn_W2"], b1t)
        layernorm(nc, "ln_m", acc, y, ln_rows["ln2_g"], ln_rows["ln2_b"], tokens)
        layernorm(nc, "ln_o", y, acc, add=resid, final=out_v)


_INS = ["L0_attn_x", "L0_attn_Wq", "L0_attn_bq", "L0_attn_Wk", "L0_attn_bk", "L0_attn_Wv", "L0_attn_bv",
        "L0_attn_Wo", "L0_attn_bo", "L0_ffn_Wq", "L0_ffn_bq", "L0_ffn_Wk", "L0_ffn_bk", "L0_ffn_Wv",
        "L0_ffn_bv", "L0_ffn_Wo", "L0_ffn_bo", "L0_ffn_ln1_g", "L0_ffn_ln1_b", "L0_ffn_ln2_g",
        "L0_ffn_ln2_b", "L0_ffn_gate_w", "L0_ffn_gate_b", "L0_ffn_W1", "L0_ffn_b1", "L0_ffn_W2",
        "L0_ffn_b2"]


def shape_constants():
    import numpy as np
    lane = np.arange(P)
    row = lane % HW
    query_lo = (row >= 2 * DH) & (row < 3 * DH)
    key_lo = ((row >= DH) & (row < 2 * DH)) | (row == ROW_BIAS + 1)
    slope = np.zeros((1, G, GH, HW), np.float32)
    slope[0, :, :, ROW_BIAS:ROW_BIAS + 2] = -np.array(slopes(), np.float32).reshape(G, GH, 1)
    return {
        "ident": np.eye(P, dtype=np.float32),
        "split_sign": -np.stack([query_lo, key_lo, 0 * lane], 1).astype(np.float32),
        "head_mask": (lane[:, None] // HW == np.arange(GH)).astype(np.float32),
        "rank": np.tile(np.arange(E, 0, -1, dtype=np.float32), (P, 1)),
        "ones_row": np.ones((1, P), np.float32),
        "iota_row": np.arange(T, dtype=np.float32)[None],
        "slope_row": slope.reshape(1, G, P),
        "causal": np.where(lane[None, :] > lane[:, None], np.float32(BIG), np.float32(0)).astype(np.float32),
    }


def kernel(**inputs):
    import numpy as np
    import concourse.bacc as bacc
    from concourse.bass_utils import run_bass_kernel_spmd

    nc = bacc.Bacc("TRN2", target_bir_lowering=False, num_devices=1)
    nc.disable_value_cache = True
    arrays, aps = {}, {}
    for name in _INS:
        arrays[name] = np.ascontiguousarray(inputs[name])
    for name, a in shape_constants().items():
        arrays["const_" + name] = a
    for name, a in arrays.items():
        aps[name] = nc.dram_tensor(name, a.shape, mybir.dt.from_np(a.dtype), kind="ExternalInput").ap()
    out = nc.dram_tensor("out_0", (B, T, D), F32, kind="ExternalOutput").ap()
    consts = {k[6:]: v for k, v in aps.items() if k.startswith("const_")}
    build(nc, aps["L0_attn_x"], aps, consts, out)
    r = run_bass_kernel_spmd(nc, [arrays], core_ids=[0])
    return r.results[0]["out_0"]
```

```python
from contextlib import ExitStack

import concourse.bass as bass
from concourse import mybir

F32 = mybir.dt.float32
F32R = mybir.dt.float32r
BF16 = mybir.dt.bfloat16
ALU = mybir.AluOpType
ACT = mybir.ActivationFunctionType
AX = mybir.AxisListType

P = 128
D = 128
B, T = 4, 1024
TB = T // P
NT = B * TB
H, DH = 16, 8
GH = 4
G = H // GH
S = B * G
HW = P // GH
SCALE = DH ** -0.5
EPS = 1e-5
E, FF = 8, 512
FT = FF // P
HALF = 512
HQ = HALF // P
BIG = -1.0e30

ROW_BIAS = 3 * DH
ROW_MAX = 3 * DH + 2


def slopes():
    start = 2.0 ** (-(2.0 ** (3 - 4)))
    return [start * start ** i for i in range(H)]


class Plan:

    def __init__(self, causal):
        self.causal = causal
        self.chunks = []
        for qt in range(TB):
            for kh in range(2):
                n = min(HALF, (qt + 1) * P - kh * HALF) if causal else HALF
                if n <= 0:
                    continue
                per = max(1, HALF // n)
                per = 4 if per >= 4 else per
                for j in range(0, GH, per):
                    self.chunks.append((qt, kh, list(range(j, j + per)), n))
        self.quads = []
        for qh in range(2):
            for kt in range((qh + 1) * HQ if causal else TB):
                self.quads.append((qh, kt))
        self.na = len(self.chunks)
        self.nq = len(self.quads)
        self.nb = GH * self.nq
        self.half_end = [max(i for i, q in enumerate(self.quads) if q[0] == h) for h in range(2)]
        nq = self.nq
        self.lead = 2
        a_steps = nq - 4
        self.a_next = -(-self.na * 4 // nq)
        own = self.na - self.a_next
        self.a_of_step = []
        for i in range(nq):
            if i < a_steps:
                lo, hi = own * i // a_steps, own * (i + 1) // a_steps
                self.a_of_step.append([(1, self.a_next + c) for c in range(lo, hi)])
            else:
                k = i - a_steps
                lo, hi = self.a_next * k // 4, self.a_next * (k + 1) // 4
                self.a_of_step.append([(2, c) for c in range(lo, hi)])
        self.m_step = a_steps - 1
        o0 = self.half_end[0] + 3 - self.lead
        free = [i for i in range(1, nq - 4) if i != o0]
        self.proj_steps = [free[len(free) * i // 4] for i in range(4)]
        self.o_steps = (o0, nq - 1)
        self.mt_steps = (a_steps, a_steps + 1)

    def interleave(self, bs, ass):
        out = []
        nb, na = len(bs), len(ass)
        for i in range(nb):
            out.append(bs[i])
            out += ass[na * i // nb:na * (i + 1) // nb]
        return out if nb else list(ass)

    def body(self, do_proj=True, do_a1=True, do_a2=True):
        out = []
        for i in range(self.nq):
            for n, at in enumerate(self.proj_steps):
                if at == i and do_proj:
                    out.append(("proj", 3, n))
            if i == self.o_steps[0]:
                out.append(("otr", 0, 0))
            q = i + self.lead
            ds, q = (0, q) if q < self.nq else (1, q - self.nq)
            bs = [("b", ds, q * GH + j) for j in range(GH)] if ds == 0 or do_a1 else []
            ass = [("a", d, c) for d, c in self.a_of_step[i] if (do_a1 if d == 1 else do_a2)]
            out += self.interleave(bs, ass)
            if i == self.m_step and do_a1:
                out.append(("m", 1, 0))
            dp, p = (ds, q - 1) if q else (0, self.nq - 1)
            if dp == 0 or do_a1:
                out.append(("pv", dp, p))
                if p in self.half_end:
                    out.append(("oev", dp, self.half_end.index(p)))
            if i in self.mt_steps and do_a1:
                out.append(("mtr", 1, self.mt_steps.index(i)))
            if i == self.o_steps[1]:
                out.append(("otr", 0, 1))
        return out

    def prologue(self):
        out = [("proj", 0, n) for n in range(4)]
        out += self.interleave([("proj", s, n) for s in (1, 2) for n in range(4)],
                               [("a", 0, c) for c in range(self.na)])
        out += [("m", 0, 0), ("mtr", 0, 0), ("mtr", 0, 1)]
        bs = [("b", 0, i) for i in range(GH * self.lead)]
        out += self.interleave(bs[:GH], [("a", 1, c) for c in range(self.a_next)])
        out += bs[GH:] + [("pv", 0, 0)]
        return out


def last_user(n, i, banks):
    return (0, i - banks) if i >= banks else (1, max(k for k in range(n) if k % banks == i))


class Register:

    def __init__(self, eng, value):
        self.eng, self.value, self.kept = eng, value, {}

    def __mul__(self, k):
        if k not in self.kept:
            self.kept[k] = self.eng.snap(self.value * k)
        return self.kept[k]

    def __add__(self, n):
        return self if n == 0 else Shifted(self, n)


class Shifted:

    def __init__(self, register, n):
        self.register, self.n = register, n

    def __mul__(self, k):
        return self.register * k + self.n * k


class Slot:

    def __init__(self, batch, g):
        self.batch, self.g = batch, g

    def __add__(self, n):
        return Slot(self.batch, self.g + n)

    def __sub__(self, n):
        return Slot(self.batch, self.g - n)

    def count(self, per, more=0):
        return self.batch * (G * per) + (self.g * per + more)


def attention(nc, tag, plan, xT, values, heads_out, w3, bias2, slope_row, iota_row, split_sign,
              head_mask, ident, ident16, causal_mask):
    causal = plan.causal
    NA, NB, NQ = plan.na, plan.nb, plan.nq
    with ExitStack() as ctx:
        def sb(name, shape, dt=F32):
            return ctx.enter_context(nc.sbuf_tensor(f"{tag}_{name}", shape, dt))

        def sem(name):
            return ctx.enter_context(nc.semaphore(f"{tag}_{name}"))

        def bank(name):
            return ctx.enter_context(nc.psum_tensor(f"{tag}_{name}", [P, HALF], F32))

        km = [sb(f"km{i}", [P, GH, T], F32R) for i in range(4)]
        fq = [sb(f"fq{i}", [P, T], F32R) for i in range(4)]
        fqm = [sb(f"fqm{i}", [P, T], F32R) for i in range(2)]
        u = [sb(f"u{i}", [P, HALF]) for i in range(2)]
        hi = sb("hi", [P, HALF], F32R)
        part = sb("part", [P, HALF])
        fk = sb("fk", [P, HALF])
        probs = [sb(f"probs{i}", [P, HALF]) for i in range(8)]
        vst = [sb(f"vst{i}", [P, TB, GH, HW]) for i in range(2)]
        mx = sb("mx", [P, 2, TB, GH])
        mfull = sb("mfull", [P, TB, GH])
        mhi = sb("mhi", [P, TB, GH], F32R)
        mpad = sb("mpad", [P, TB, P])
        osb = sb("osb", [P, 2, HALF])
        rec = sb("rec", [P, HQ, GH])
        a_bank = [bank(f"a{i}") for i in range(3)]
        b_bank = [bank(f"b{i}") for i in range(3)]
        pv_bank = bank("pv")
        misc = bank("misc")

        proj_made = sem("proj_made")
        proj_read = sem("proj_read")
        split_done = sem("split_done")
        pool_step = sem("pool_step")
        pool_passed = sem("pool_passed")
        v_staged = sem("v_staged")
        a_made = sem("a_made")
        a_read = sem("a_read")
        m_step = sem("m_step")
        m_padded = sem("m_padded")
        m_turned = sem("m_turned")
        fqm_made = sem("fqm_made")
        b_made = sem("b_made")
        exp_done = sem("exp_done")
        pv_done = sem("pv_done")
        o_read = sem("o_read")
        o_turned = sem("o_turned")
        o_step = sem("o_step")
        o_done = sem("o_done")
        init = sem("init")

        def done(eng, semaphore, per, s, i):
            eng.wait_ge(semaphore, (s + 1).count(per, i + 1))

        block = ctx.enter_context(nc.Block())

        def run(eng, emit):
            emit(plan.prologue(), Slot(0, 0), 0, 0)
            with eng.Fori(0, B - 1) as batch:
                b = Register(eng, batch)
                for g in range(G):
                    emit(plan.body(), Slot(b, g), b, g)
            for g in range(G):
                s = (B - 1) * G + g
                emit(plan.body(s + 3 < S, s + 1 < S, s + 2 < S), Slot(B - 1, g), B - 1, g)

        def where(b, g, ds):
            return (b + (g + ds) // G, (g + ds) % G)

        @block.tensor
        def _(pe):
            pe.wait_ge(init, 4)
            for semaphore, per in ((proj_made, 4), (a_made, NA), (m_turned, 2), (b_made, NB),
                                   (pv_done, NQ), (o_turned, 2)):
                pe.sem_inc(semaphore, per)

            def emit(steps, s0, b0, g0):
                prologue = steps[0][0] == "proj" and steps[0][1] == 0
                before = None if prologue else ("otr", -1, 1)
                for what, ds, n in steps:
                    s = s0 + ds
                    if what in ("proj", "otr", "mtr"):
                        if before is not None:
                            bw, bs, bn = before
                            if bw == "proj":
                                done(pe, proj_read, 4, s0 + bs, bn)
                            elif bw == "mtr":
                                done(pe, fqm_made, 2, s0 + bs, bn)
                            else:
                                done(pe, o_done, 2, s0 + bs, bn)
                                if bs < 0:
                                    done(pe, fqm_made, 2, s0, 1)
                        before = (what, ds, n)
                    if what == "proj":
                        b, g = where(b0, g0, ds)
                        m, h = (1, n) if n < 2 else (0, n - 2)
                        x = xT[:, bass.ds(b * T + h * HALF, HALF)]
                        alibi = causal and m == 1
                        mm = pe.matmul(misc[:, :], w3[:, m, g, :], x, start=True, stop=not alibi)
                        if alibi:
                            mm = pe.matmul(misc[:, :], slope_row[0:1, g, :],
                                           iota_row[0:1, h * HALF:(h + 1) * HALF], start=False, stop=True)
                        mm.then_inc(proj_made, 1)
                    elif what == "a":
                        qt, kh, heads, w = plan.chunks[n]
                        _, g = where(b0, g0, ds)
                        if n == 0:
                            done(pe, split_done, 4, s, 3)
                        back, k = last_user(NA, n, 3)
                        done(pe, a_read, NA, s - back, k)
                        out = a_bank[n % 3]
                        diagonal = causal and kh * HALF + w == (qt + 1) * P
                        for i, j in enumerate(heads):
                            mm = pe.matmul(out[:, i * w:(i + 1) * w], fq[g][:, qt * P:(qt + 1) * P],
                                           km[g][:, j, kh * HALF:kh * HALF + w],
                                           start=True, stop=not diagonal)
                            if diagonal:
                                mm = pe.matmul(out[:, (i + 1) * w - P:(i + 1) * w], ident16[:, :],
                                               causal_mask[:, :], start=False, stop=True)
                        mm.then_inc(a_made, 1)
                    elif what == "mtr":
                        done(pe, m_padded, 1, s, 0)
                        for i in range(HQ):
                            mm = pe.transpose(misc[:, i * P:(i + 1) * P], mpad[:, n * HQ + i, :], ident[:, :])
                        mm.then_inc(m_turned, 1)
                    elif what == "b":
                        _, g = where(b0, g0, ds)
                        t, j = n // GH, n % GH
                        qh, kt = plan.quads[t]
                        if n == 0 or plan.quads[(n - 1) // GH][0] != qh:
                            done(pe, fqm_made, 2, s, qh)
                        back, k = last_user(NB, n, 3)
                        done(pe, exp_done, NB, s - back, k)
                        q0 = max(qh * HALF, kt * P) if causal else qh * HALF
                        w = (qh + 1) * HALF - q0
                        diagonal = causal and kt * P >= qh * HALF
                        out = b_bank[n % 3]
                        mm = pe.matmul(out[:, 0:w], km[g][:, j, kt * P:(kt + 1) * P],
                                       fqm[g % 2][:, q0:q0 + w], start=True, stop=not diagonal)
                        if diagonal:
                            mm = pe.matmul(out[:, 0:P], causal_mask[:, :], ident16[:, :],
                                           start=False, stop=True)
                        mm.then_inc(b_made, 1)
                    elif what == "pv":
                        _, g = where(b0, g0, ds)
                        qh, kt = plan.quads[n]
                        if n == 0:
                            done(pe, v_staged, 1, s, 0)
                        if n == 0 or plan.quads[n - 1][0] != qh:
                            done(pe, o_read, 2, s - (qh == 0), 1 - qh)
                        done(pe, exp_done, NB, s, GH * n + GH - 1)
                        q0 = max(qh * HALF, kt * P) if causal else qh * HALF
                        w = (qh + 1) * HALF - q0
                        for j in range(GH):
                            mm = pe.matmul(pv_bank[HW * j:HW * (j + 1), HALF - w:HALF],
                                           vst[g % 2][:, kt, j, :], probs[(n % 2) * GH + j][:, 0:w],
                                           start=(kt == 0), stop=(n == plan.half_end[qh]))
                        mm.then_inc(pv_done, 1)
                    elif what == "otr":
                        done(pe, o_read, 2, s, n)
                        for i in range(HQ):
                            mm = pe.transpose(misc[:, i * P:(i + 1) * P], osb[:, n, i * P:(i + 1) * P],
                                              ident[:, :])
                        mm.then_inc(o_turned, 1)

            run(pe, emit)

        @block.scalar
        def _(act):
            for semaphore, per in ((proj_read, 4), (exp_done, NB), (o_read, 2)):
                act.sem_inc(semaphore, per)

            def emit(steps, s0, b0, g0):
                for what, ds, n in steps:
                    s = s0 + ds
                    if what == "proj":
                        _, g = where(b0, g0, ds)
                        m = 1 if n < 2 else 0
                        done(act, proj_made, 4, s, n)
                        done(act, split_done, 4, s, n - 2)
                        act.activation(u[n % 2][:, :], misc[:, :], ACT.Identity,
                                       scale=1.0 if m else SCALE,
                                       bias=bias2[:, m, g:g + 1]).then_inc(proj_read, 1)
                    elif what == "b":
                        t, j = n // GH, n % GH
                        qh, kt = plan.quads[t]
                        q0 = max(qh * HALF, kt * P) if causal else qh * HALF
                        w = (qh + 1) * HALF - q0
                        done(act, b_made, NB, s, n)
                        if j == 0:
                            done(act, pv_done, NQ, s, t - 2)
                        act.activation(probs[(t % 2) * GH + j][:, 0:w], b_bank[n % 3][:, 0:w],
                                       ACT.Exp).then_inc(exp_done, 1)
                    elif what == "oev":
                        done(act, pv_done, NQ, s, plan.half_end[n])
                        done(act, o_turned, 2, s - 1, n)
                        act.activation(osb[:, n, :], pv_bank[:, :], ACT.Identity).then_inc(o_read, 1)

            run(act, emit)

        @block.vector
        def _(dve):
            for semaphore, per in ((a_read, NA), (m_padded, 1), (fqm_made, 2), (o_done, 2),
                                   (m_step, 2), (o_step, 2)):
                dve.sem_inc(semaphore, per)
            dve.wait_ge(init, 4)

            def emit(steps, s0, b0, g0):
                for what, ds, n in steps:
                    s = s0 + ds
                    b, g = where(b0, g0, ds)
                    if what == "a":
                        qt, kh, heads, w = plan.chunks[n]
                        done(dve, a_made, NA, s, n)
                        if n == 0:
                            done(dve, m_step, 2, s - 1, 0)
                        k = len(heads)
                        dve.tensor_reduce(mx[:, kh, qt, heads[0]:heads[0] + k],
                                          a_bank[n % 3][:, 0:k * w].rearrange("p (k w) -> p k w", k=k),
                                          AX.X, ALU.max).then_inc(a_read, 1)
                    elif what == "m":
                        done(dve, a_read, NA, s, NA - 1)
                        done(dve, m_step, 2, s - 1, 1)
                        done(dve, m_padded, 1, s - 1, 0)
                        done(dve, m_turned, 2, s - 1, 1)
                        dve.tensor_tensor(mfull[:, :, :], mx[:, 0, :, :], mx[:, 1, :, :],
                                          ALU.max).then_inc(m_step, 1)
                        done(dve, m_step, 2, s, 0)
                        dve.tensor_copy(mhi[:, :, :], mfull[:, :, :]).then_inc(m_step, 1)
                        done(dve, m_step, 2, s, 1)
                        pad = mpad[:, :, :].rearrange("p t (j r) -> p t j r", j=GH)
                        dve.tensor_copy(pad[:, :, :, ROW_MAX], mhi[:, :, :].bitcast(F32))
                        dve.tensor_tensor(pad[:, :, :, ROW_MAX + 1], mfull[:, :, :],
                                          mhi[:, :, :].bitcast(F32), ALU.subtract).then_inc(m_padded, 1)
                    elif what == "mtr":
                        done(dve, m_turned, 2, s, n)
                        h = slice(n * HALF, (n + 1) * HALF)
                        dve.tensor_tensor(fqm[g % 2][:, h], fq[g][:, h].bitcast(F32), misc[:, :],
                                          ALU.add).then_inc(fqm_made, 1)
                    elif what == "otr":
                        turned = misc[:, :].rearrange("p (t j c) -> p t j c", t=HQ, j=GH)
                        done(dve, o_turned, 2, s, n)
                        done(dve, o_done, 2, s, n - 1)
                        dve.reciprocal(rec[:, :, :], turned[:, :, :, DH]).then_inc(o_step, 1)
                        done(dve, o_step, 2, s, n)
                        dve.tensor_tensor(
                            heads_out[:, bass.ds(b * TB + n * HQ, HQ), g * GH * DH:(g + 1) * GH * DH]
                            .rearrange("p t (j c) -> p t j c", j=GH),
                            turned[:, :, :, 0:DH],
                            rec[:, :, :, None].broadcast_to([P, HQ, GH, DH]),
                            ALU.mult).then_inc(o_done, 1)

            run(dve, emit)

        @block.gpsimd
        def _(pool):
            for semaphore, per in ((split_done, 4), (v_staged, 1)):
                pool.sem_inc(semaphore, per)
            pool.memset(mpad[:, :, :], 0.0).then_inc(init, 1)
            pool.memset(mx[:, :, :, :], -3.0e38).then_inc(init, 1)
            for v in vst:
                pool.memset(v[:, :, :, :], 0.0).then_inc(pool_step, 1)
            pool.wait_ge(pool_step, 2)
            for v in vst:
                pool.memset(v[:, :, :, DH:DH + 1], 1.0).then_inc(init, 1)
            pool.wait_ge(init, 4)
            count = 2 * 3 + 2 * 2
            pool.sem_inc(pool_step, count - 2)

            def await_(semaphore, per, s, i):
                done(pool, semaphore, per, s, i)
                pool.sem_inc(pool_passed, 1)

            def stage_values(b, g):
                src = values[:, bass.ds(b * TB, TB), g * GH * DH:(g + 1) * GH * DH]
                pool.tensor_copy(vst[g % 2][:, :, :, 0:DH],
                                 src.rearrange("p t (j c) -> p t j c", j=GH)).then_inc(v_staged, 1)

            def emit(steps, s0, b0, g0):
                if steps[0][1] == 0 and steps[0][0] == "proj":
                    stage_values(0, 0)
                else:
                    if any(k[0] == "pv" and k[1] == 1 for k in steps):
                        b, g = where(b0, g0, 1)
                        await_(pv_done, NQ, s0 - 1, NQ - 1)
                        stage_values(b, g)
                first = True
                for what, ds, n in steps:
                    s = s0 + ds
                    if what != "proj":
                        continue
                    _, g = where(b0, g0, ds)
                    m, h = (1, n) if n < 2 else (0, n - 2)
                    if ds == 3 and first:
                        await_(b_made, NB, s - 4, NB - 1)
                        first = False
                    un = u[n % 2]
                    await_(proj_read, 4, s, n)
                    await_(split_done, 4, s, n - 1)
                    step = 3 * n if m else 6 + 2 * h
                    half = slice(h * HALF, (h + 1) * HALF)
                    pool.tensor_tensor(hi[:, :], un[:, :], split_sign[:, 2:3].broadcast_to([P, HALF]),
                                       ALU.add).then_inc(pool_step, 1)
                    await_(pool_step, count, s, step)
                    pool.tensor_tensor(part[:, :], hi[:, :].bitcast(F32),
                                       split_sign[:, m:m + 1].broadcast_to([P, HALF]),
                                       ALU.mult).then_inc(pool_step, 1)
                    await_(pool_step, count, s, step + 1)
                    if m == 0:
                        pool.tensor_tensor(fq[g][:, half], part[:, :], un[:, :],
                                           ALU.add).then_inc(split_done, 1)
                    else:
                        pool.tensor_tensor(fk[:, :], part[:, :], un[:, :], ALU.add).then_inc(pool_step, 1)
                        await_(pool_step, count, s, step + 2)
                        pool.tensor_tensor(km[g][:, :, half],
                                           fk[:, None, :].broadcast_to([P, GH, HALF]),
                                           head_mask[:, :, None].broadcast_to([P, GH, HALF]),
                                           ALU.mult).then_inc(split_done, 1)

            run(pool, emit)


def layernorm(nc, tag, src, dst, gain=None, shift=None, add=None, final=None):
    with ExitStack() as ctx:
        def sb(name, shape, dt=F32):
            return ctx.enter_context(nc.sbuf_tensor(f"{tag}_{name}", shape, dt))

        def sem(name):
            return ctx.enter_context(nc.semaphore(f"{tag}_{name}"))

        mean = sb("mean", [P, NT])
        total = sb("total", [P, NT])
        rstd = sb("rstd", [P, NT])
        square = sb("square", [P, 2, TB, D])
        centred = sem("centred")
        squared = sem("squared")
        reduced = sem("reduced")
        root = sem("root")
        step = sem("step")
        stored = sem("stored")
        ready = sem("ready")

        def tiles(x, b):
            return x[:, b * TB:(b + 1) * TB, :]

        def wide(x, b):
            return x[:, b * TB:(b + 1) * TB, None].broadcast_to([P, TB, D])

        def row(x):
            return x[:, None, :].broadcast_to([P, TB, D])

        block = ctx.enter_context(nc.Block())

        @block.vector
        def _(dve):
            for b in range(B):
                dve.tensor_reduce(total[:, b * TB:(b + 1) * TB], tiles(src, b), AX.X, ALU.add).then_inc(step, 1)
            dve.wait_ge(step, B)
            dve.tensor_scalar(mean[:, :], total[:, :], 1.0 / D, None, ALU.mult).then_inc(step, 1)
            dve.wait_ge(step, B + 1)
            for b in range(B):
                dve.tensor_tensor(tiles(dst, b), tiles(src, b), wide(mean, b), ALU.subtract).then_inc(centred, 1)
            for b in range(B):
                dve.wait_ge(squared, b + 1)
                dve.tensor_reduce(total[:, b * TB:(b + 1) * TB], square[:, b % 2], AX.X,
                                  ALU.add).then_inc(reduced, 1)
            dve.wait_ge(reduced, B)
            dve.tensor_scalar(mean[:, :], total[:, :], 1.0 / D, EPS, ALU.mult, ALU.add).then_inc(step, 1)
            dve.wait_ge(root, 1)
            dve.reciprocal(rstd[:, :], total[:, :]).then_inc(step, 1)
            n = B + 3
            dve.wait_ge(step, n)
            for b in range(B):
                ops = [(wide(rstd, b), ALU.mult)]
                if gain is not None:
                    ops += [(row(gain), ALU.mult), (row(shift), ALU.add)]
                if add is not None:
                    ops.append((tiles(add, b), ALU.add))
                for operand, op in ops:
                    dve.wait_ge(step, n)
                    last = dve.tensor_tensor(tiles(dst, b), tiles(dst, b), operand, op).then_inc(step, 1)
                    n += 1
                if final is not None:
                    dve.wait_ge(step, n)
                    dve.sem_inc(ready, 1)

        @block.scalar
        def _(act):
            for b in range(B):
                act.wait_ge(centred, b + 1)
                if b >= 2:
                    act.wait_ge(reduced, b - 1)
                act.activation(square[:, b % 2], tiles(dst, b), ACT.Square).then_inc(squared, 1)
            act.wait_ge(step, B + 2)
            act.activation(total[:, :], mean[:, :], ACT.Sqrt).then_inc(root, 1)

        if final is not None:
            @block.sync
            def _(sp):
                for b in range(B):
                    sp.wait_ge(ready, b + 1)
                    sp.dma_start(final[:, b * TB:(b + 1) * TB, :], tiles(dst, b)).then_inc(stored, 16)
                sp.wait_ge(stored, 16 * B)


def turn_and_project(nc, tag, src, turned, weight, bias_row, ones_row, ident, dst, width=D):
    with ExitStack() as ctx:
        def sem(name):
            return ctx.enter_context(nc.semaphore(f"{tag}_{name}"))

        t_bank = [ctx.enter_context(nc.psum_tensor(f"{tag}_t{i}", [P, 4, P], F32)) for i in range(3)]
        y_bank = [ctx.enter_context(nc.psum_tensor(f"{tag}_y{i}", [P, 4, width], F32)) for i in range(3)]
        t_made, t_read, y_made, y_read = sem("t_made"), sem("t_read"), sem("y_made"), sem("y_read")
        block = ctx.enter_context(nc.Block())
        groups = NT // 4

        @block.tensor
        def _(pe):
            def project(n):
                pe.wait_ge(t_read, n + 1)
                if n >= 3:
                    pe.wait_ge(y_read, n - 2)
                for i in range(4):
                    t = 4 * n + i
                    pe.matmul(y_bank[n % 3][:, i, :], turned[:, t * P:(t + 1) * P], weight[:, :],
                              start=True, stop=False)
                    mm = pe.matmul(y_bank[n % 3][:, i, :], ones_row[0:1, :], bias_row[0:1, 0:width],
                                   start=False, stop=True)
                mm.then_inc(y_made, 1)

            for n in range(groups):
                if n >= 3:
                    pe.wait_ge(t_read, n - 2)
                for i in range(4):
                    mm = pe.transpose(t_bank[n % 3][:, i, :], src[:, 4 * n + i, :], ident[:, :])
                mm.then_inc(t_made, 1)
                if n:
                    project(n - 1)
            project(groups - 1)

        @block.scalar
        def _(act):
            for n in range(groups):
                act.wait_ge(t_made, n + 1)
                act.activation(turned[:, n * HALF:(n + 1) * HALF],
                               t_bank[n % 3][:, :, :].rearrange("p a b -> p (a b)"),
                               ACT.Identity).then_inc(t_read, 1)

        @block.vector
        def _(dve):
            for n in range(groups):
                dve.wait_ge(y_made, n + 1)
                dve.tensor_copy(dst[:, 4 * n:4 * n + 4, :], y_bank[n % 3][:, :, :]).then_inc(y_read, 1)


class Turn:

    def __init__(self, pair, c):
        self.pair, self.c = pair, c
        self.side = c % 2

    def __add__(self, n):
        return Turn(self.pair, self.c + n)

    def __sub__(self, n):
        return Turn(self.pair, self.c - n)

    def count(self, per, more=0):
        return self.pair * (2 * per) + (self.c * per + more)

    def landed(self):
        return self.pair * 16 + (self.c // 2 + 1) * 16


NBLK = NT // HQ

ENTER = {
    "pe": {"turn_heads": -7.98, "project": -7.5, "turn_w": -4.7, "logits": -4.0, "turn_comb": -1.5, "bias2": -1.02},
    "act": {"heads_t": -7.8, "w_hi": -4.55, "comb_hi": -1.38},
    "dve": {"y": -7.1, "stats": -7.1, "mean": -7.1, "centre": -6.4, "w_lo": -4.35,
            "logits": -3.7, "top": -3.7, "less_top": -3.7,
            "sum": -2.25, "recip": -2.25, "probs": -2.25, "rest": -2.25,
            "top0": -2.2, "eq0": -2.2, "key0": -2.2, "best0": -2.2, "pick0": -2.2, "chosen0": -2.2,
            "drop0": -2.2,
            "top1": -2.05, "eq1": -2.05, "key1": -2.05, "best1": -2.05, "pick1": -2.05, "chosen1": -2.05, "comb": -2.05,
            "comb_lo": -1.2, "acc": -0.7},
    "pool": {"var": -6.8, "rstd": -6.8, "gain": -6.2, "shift": -5.8, "w": -5.05, "exp": -3.3},
}
LEAVE = {
    "pe": {"turn_acc": 9.25},
    "dve": {"stats1": 9.4, "mean1": 9.4, "centre1": 9.9, "stats2": 11.3, "mean2": 11.3, "centre2": 11.8},
    "pool": {"var1": 9.65, "rstd1": 9.65, "gain": 10.15, "shift": 10.6, "z": 10.9, "var2": 11.6, "rstd2": 11.6,
             "out": 12.1},
}
POOL_ROUNDS = {e: e != 5 for e in range(E)}


def rounder(f, e):
    return "pool" if f < 2 and POOL_ROUNDS[e] else "act"


HIDDEN = {
    "pe": {f"{k}{e}": e + t for e in range(E)
           for k, t in (("weight", 0), ("h0_", .08), ("h1_", .19), ("h2_", .3), ("h3_", .41))},
    "act": {f"{k}{e}": e + t for e in range(E)
            for k, t in (("weight", .08), ("gelu0_", .25), ("gelu1_", .37), ("gelu2_", .49), ("gelu3_", .61),
                         ("hi0_", .71), ("hi1_", .73), ("hi2_", .75), ("hi3_", .85))
            if k[:2] != "hi" or rounder(int(k[2]), e) == "act"},
    "dve": {f"{k}{e}": e + t for e in range(E)
            for k, t in (("lo0_", .65), ("lo1_", .85), ("lo2_", .95), ("lo3_", 1.05))},
    "pool": {f"hi{f}_{e}": e + .4 + .2 * f for e in range(E) for f in range(2) if rounder(f, e) == "pool"},
}
OUTPUT = {
    "pe": {f"y{e}": e + 1.53 for e in range(E)},
    "dve": {f"{k}{e}": e + 2.03 for e in range(E) for k in ("weighed", "acc")},
}
SPLIT = {k: {f"split{e}": (e - 1.5 if e >= 2 else -7.6 + e / 2) for e in range(E)} for k in ("act", "dve")}


def tail(nc, heads, kept_u, kept, out_v, wo, rows, gate_w, ident, rank, pows, b1t, b2, W1, W2):
    with ExitStack() as ctx:
        def sb(name, shape, dt=F32):
            return ctx.enter_context(nc.sbuf_tensor(f"t_{name}", shape, dt))

        def sem(name):
            return ctx.enter_context(nc.semaphore(f"t_{name}"))

        def bank(name):
            return ctx.enter_context(nc.psum_tensor(f"t_bank_{name}", [P, HALF], F32))

        raw = [[sb(f"raw{m}{i}", [P, FF]) for i in range(2)] for m in range(2)]
        w1 = [sb(f"w1{k}", [P, E, FF], F32R) for k in ("hi", "lo")]
        w2 = [sb(f"w2{k}", [P, E, FT, D], F32R) for k in ("hi", "lo")]
        gw = [sb(f"gw{k}", [P, E], F32R) for k in ("hi", "lo")]
        bb = [sb(f"b2{k}", [E, D], F32R) for k in ("hi", "lo")]
        select = sb("select", [E, E, P], F32R)
        heads_in = [sb(f"heads_in{i}", [P, HQ, D]) for i in range(2)]
        u_in = [sb(f"u_in{i}", [P, HQ, D]) for i in range(2)]
        x_in = [sb(f"x_in{i}", [P, HQ, D]) for i in range(2)]
        z_out = [sb(f"z_out{i}", [P, HQ, D]) for i in range(2)]
        heads_t = sb("heads_t", [P, HALF])
        y = sb("y", [P, HQ, D])
        stats = sb("stats", [P, HQ, 6])
        mean_var = sb("mean_var", [P, HQ, 2])
        var = sb("var", [P, HQ])
        rstd = sb("rstd", [P, HQ])
        w_tok = [sb(f"w_tok{i}", [P, HQ, D]) for i in range(2)]
        w_t = [[sb(f"w_t{i}{k}", [P, HALF], F32R) for k in ("hi", "lo")] for i in range(2)]
        logits = sb("logits", [P, HQ, E])
        top = sb("top", [P, HQ])
        exped = sb("exped", [P, HQ, E])
        probs = sb("probs", [P, HQ, E])
        rest = sb("rest", [P, HQ, E])
        key = sb("key", [P, HQ, E])
        chosen = sb("chosen", [P, HQ, E])
        comb = sb("comb", [P, HQ, E])
        comb_t = [[sb(f"comb_t{i}{k}", [E, HALF], F32R) for k in ("hi", "lo")] for i in range(2)]
        weight = [sb(f"weight{i}", [P, HALF]) for i in range(2)]
        hid = sb("hid", [P, FT, HALF])
        hid_hi = [sb(f"hid_hi{i}", [P, FT, HALF], F32R) for i in range(2)]
        hid_lo = [sb(f"hid_lo{i}", [P, FT, HALF], F32R) for i in range(2)]
        weighed = sb("weighed", [P, HALF])
        acc = [sb(f"acc{i}", [P, HALF]) for i in range(2)]
        l_stats = sb("l_stats", [P, HQ, 6])
        l_mv = sb("l_mv", [P, HQ, 2])
        l_var = sb("l_var", [P, HQ])
        l_rstd = sb("l_rstd", [P, HQ])
        z = sb("z", [P, HQ, D])
        h_bank = [bank(f"h{i}") for i in range(FT)]
        y_bank, w_bank, e_bank, l_bank = bank("y"), bank("w"), bank("e"), bank("l")

        enter = {k: sem(f"enter_{k}") for k in ENTER}
        leave = {k: sem(f"leave_{k}") for k in LEAVE}
        hidden = {k: sem(f"hidden_{k}") for k in HIDDEN}
        output = {k: sem(f"output_{k}") for k in OUTPUT}
        steps = {id(enter): ENTER, id(leave): LEAVE, id(hidden): HIDDEN, id(output): OUTPUT}
        in_sems = [[sem(f"{n}_landed{i}") for i in range(2)] for n in ("heads", "u", "x")]
        stored = [sem(f"stored{i}") for i in range(2)]
        raw_in = [sem(f"raw_landed{i}") for i in range(2)]
        w_hi_made = sem("w_hi_made")
        w_lo_made = sem("w_lo_made")
        small_hi = sem("small_hi")
        small_lo = sem("small_lo")
        pool_passed = sem("pool_passed")
        dve_passed = sem("dve_passed")

        def after(eng, stage, who, step, turn):
            names = list(steps[id(stage)][who])
            eng.wait_ge(stage[who], (turn + 2).count(len(names), names.index(step) + 1))

        def advance(eng, who):
            for stage in (enter, leave, hidden, output):
                if who in stage:
                    eng.sem_inc(stage[who], 2 * len(steps[id(stage)][who]))

        def order(who, windows):
            out = []
            for name, stage in (("enter", ENTER), ("leave", LEAVE), ("hidden", HIDDEN), ("output", OUTPUT)):
                for place, (step, at) in enumerate(stage.get(who, {}).items()):
                    window = int(at // E)
                    if window in windows:
                        out.append((at - E * window, name, place, step, -window))
            if windows == (-1,) or windows == (-1, 0):
                window = -1 if windows == (-1,) else 0
                for step, at in SPLIT.get(who, {}).items():
                    if int(at // E) == window:
                        out.append((at - E * window, "split", 0, step, -window))
            return [(name, step, d) for at, name, place, step, d in sorted(out)]

        def run(eng, who, emit):
            def part(windows, now):
                for name, step, d in order(who, windows):
                    emit(name, step, now + d)
            part((-1,), Turn(0, -1))
            part((-1, 0), Turn(0, 0))
            with eng.Fori(0, (NBLK - 2) // 2) as register:
                pair = Register(eng, register)
                for c in (1, 2):
                    part((-1, 0, 1), Turn(pair, c))
            part((0, 1), Turn(0, NBLK - 1))
            part((1,), Turn(0, NBLK))

        def tiles(x):
            return x[:, :].rearrange("p (t c) -> p t c", t=HQ)

        def wide(x, n=E):
            return x[:, :, None].broadcast_to([P, HQ, n])

        def row(x):
            return x[:, None, :].broadcast_to([P, HQ, D])

        block = ctx.enter_context(nc.Block())

        @block.sync
        def _(sp):
            def load(turn, register, c):
                at = bass.ds(register * (2 * HQ) + c * HQ, HQ)
                i = turn.side
                after(sp, enter, "pe", "turn_heads", turn - 2)
                sp.dma_start(heads_in[i][:, :, :], heads[:, at, :]).then_inc(in_sems[0][i], 16)
                after(sp, enter, "pool", "w", turn - 2)
                sp.dma_start(u_in[i][:, :, :], kept_u[:, at, :]).then_inc(in_sems[1][i], 16)

            def load_x(turn, register, c):
                after(sp, leave, "pool", "out", turn - 2)
                sp.dma_start(x_in[turn.side][:, :, :],
                             kept[:, bass.ds(register * (2 * HQ) + c * HQ, HQ), :]).then_inc(in_sems[2][turn.side], 16)

            def store(turn, register, c):
                after(sp, leave, "pool", "out", turn)
                sp.dma_start(out_v[:, bass.ds(register * (2 * HQ) + c * HQ, HQ), :],
                             z_out[turn.side][:, :, :]).then_inc(stored[turn.side], 16)

            load(Turn(0, 0), 0, 0)
            load(Turn(0, 1), 0, 1)
            load_x(Turn(0, 0), 0, 0)
            for e in range(E):
                if e >= 2:
                    sp.wait_ge(w_lo_made, 2 * (e - 1))
                sp.dma_start(raw[0][e % 2][:, :], W1[e]).then_inc(raw_in[e % 2], 16)
                sp.dma_start(raw[1][e % 2][:, :].rearrange("p (t d) -> p t d", t=FT),
                             W2[e].rearrange("(t p) d -> p t d", p=P)).then_inc(raw_in[e % 2], 16)
            with sp.Fori(0, (NBLK - 2) // 2) as register:
                pair = Register(sp, register)
                for c in (1, 2):
                    load(Turn(pair, c + 1), register, c + 1)
                    load_x(Turn(pair, c), register, c)
                    store(Turn(pair, c - 1), register, c - 1)
            load_x(Turn(0, NBLK - 1), 0, NBLK - 1)
            store(Turn(0, NBLK - 2), 0, NBLK - 2)
            store(Turn(0, NBLK - 1), 0, NBLK - 1)
            for s in stored:
                sp.wait_ge(s, 16 * NBLK // 2)

        def three(pe, out, a, b, start=True, stop=True):
            pe.matmul(out, a[0], b[0], start=start, stop=False)
            pe.matmul(out, a[0], b[1], start=False, stop=False)
            return pe.matmul(out, a[1], b[0], start=False, stop=stop)

        @block.tensor
        def _(pe):
            advance(pe, "pe")

            def emit(stage, step, turn):
                i = turn.side
                if (stage, step) == ("enter", "turn_heads"):
                    pe.wait_ge(in_sems[0][i], turn.landed())
                    after(pe, enter, "dve", "acc", turn - 1)
                    for t in range(HQ):
                        mm = pe.transpose(e_bank[:, t * P:(t + 1) * P], heads_in[i][:, t, :], ident[:, :])
                    mm.then_inc(enter["pe"], 1)
                elif (stage, step) == ("enter", "project"):
                    after(pe, enter, "act", "heads_t", turn)
                    for t in range(HQ):
                        mm = pe.matmul(e_bank[:, t * P:(t + 1) * P], heads_t[:, t * P:(t + 1) * P],
                                       wo[:, :], start=True, stop=True)
                    mm.then_inc(enter["pe"], 1)
                elif (stage, step) == ("enter", "turn_w"):
                    after(pe, enter, "pool", "w", turn)
                    after(pe, enter, "dve", "y", turn)
                    for t in range(HQ):
                        mm = pe.transpose(e_bank[:, t * P:(t + 1) * P], w_tok[i][:, t, :], ident[:, :])
                    mm.then_inc(enter["pe"], 1)
                elif (stage, step) == ("enter", "logits"):
                    after(pe, enter, "dve", "w_lo", turn)
                    pe.wait_ge(small_lo, 2)
                    for t in range(HQ):
                        at = slice(t * P, (t + 1) * P)
                        mm = three(pe, e_bank[:, t * E:(t + 1) * E], [m[:, at] for m in w_t[i]],
                                   [m[:, :] for m in gw])
                    mm.then_inc(enter["pe"], 1)
                elif (stage, step) == ("enter", "turn_comb"):
                    after(pe, enter, "dve", "comb", turn)
                    for t in range(HQ):
                        mm = pe.transpose(e_bank[0:E, t * P:(t + 1) * P], comb[:, t, :], ident[:, :])
                    mm.then_inc(enter["pe"], 1)
                elif (stage, step) == ("enter", "bias2"):
                    after(pe, enter, "dve", "comb_lo", turn)
                    mm = three(pe, e_bank[:, :], [m[:, :] for m in bb], [m[:, :] for m in comb_t[i]])
                    mm.then_inc(enter["pe"], 1)
                elif stage == "leave":
                    after(pe, output, "dve", f"acc{E - 1}", turn)
                    after(pe, leave, "dve", "centre1", turn - 1)
                    for t in range(HQ):
                        mm = pe.transpose(l_bank[:, t * P:(t + 1) * P], acc[i][:, t * P:(t + 1) * P],
                                          ident[:, :])
                    mm.then_inc(leave["pe"], 1)
                elif stage == "hidden" and step.startswith("weight"):
                    e = int(step[6:])
                    before, p = (turn, e - 1) if e else (turn - 1, E - 1)
                    if e == 0:
                        after(pe, enter, "dve", "comb_lo", turn)
                    if type(turn.pair) is int and turn.c == 0:
                        pe.wait_ge(w_lo_made, 2 * (e + 1))
                    after(pe, hidden, "act", f"weight{p}", before)
                    for n in range(2):
                        mm = pe.matmul(w_bank[:, :], select[:, e, :], comb_t[i][n][:, :],
                                       start=(n == 0), stop=(n == 1))
                    mm.then_inc(hidden["pe"], 1)
                elif stage == "hidden":
                    f, e = int(step[1]), int(step[3:])
                    before, p = (turn, e - 1) if e else (turn - 1, E - 1)
                    after(pe, hidden, "act", f"gelu{f}_{p}", before)
                    at = slice(f * P, (f + 1) * P)
                    three(pe, h_bank[f][:, :], [m[:, e, at] for m in w1],
                          [m[:, :] for m in w_t[i]]).then_inc(hidden["pe"], 1)
                elif stage == "output":
                    e = int(step[1:])
                    before, p = (turn, e - 1) if e else (turn - 1, E - 1)
                    after(pe, output, "dve", f"weighed{p}", before)
                    for f in range(FT):
                        after(pe, hidden, "dve", f"lo{f}_{e}", turn)
                        mm = three(pe, y_bank[:, :], [m[:, e, f, :] for m in w2],
                                   [m[e % 2][:, f, :] for m in (hid_hi, hid_lo)],
                                   start=(f == 0), stop=(f == FT - 1))
                    mm.then_inc(output["pe"], 1)

            run(pe, "pe", emit)

        @block.scalar
        def _(act):
            advance(act, "act")

            def emit(stage, step, turn):
                i = turn.side
                if stage == "split":
                    e = int(step[5:])
                    act.wait_ge(raw_in[e % 2], 32 * (e // 2 + 1))
                    act.activation(w1[0][:, e, :], raw[0][e % 2][:, :], ACT.Identity).then_inc(w_hi_made, 1)
                    act.activation(w2[0][:, e, :, :], raw[1][e % 2][:, :].rearrange("p (t d) -> p t d", t=FT),
                                   ACT.Identity).then_inc(w_hi_made, 1)
                elif (stage, step) == ("enter", "heads_t"):
                    after(act, enter, "pe", "turn_heads", turn)
                    after(act, enter, "pe", "project", turn - 1)
                    act.activation(heads_t[:, :], e_bank[:, :], ACT.Identity).then_inc(enter["act"], 1)
                elif (stage, step) == ("enter", "w_hi"):
                    after(act, enter, "pe", "turn_w", turn)
                    after(act, hidden, "pe", f"h3_{E - 1}", turn - 2)
                    act.activation(w_t[i][0][:, :], e_bank[:, :], ACT.Identity).then_inc(enter["act"], 1)
                elif (stage, step) == ("enter", "comb_hi"):
                    after(act, enter, "pe", "turn_comb", turn)
                    after(act, hidden, "pe", f"weight{E - 1}", turn - 2)
                    act.activation(comb_t[i][0][:, :], e_bank[0:E, :], ACT.Identity).then_inc(enter["act"], 1)
                elif step.startswith("weight"):
                    e = int(step[6:])
                    before, p = (turn, e - 2) if e >= 2 else (turn - 1, E + e - 2)
                    after(act, hidden, "pe", f"weight{e}", turn)
                    after(act, output, "dve", f"weighed{p}", before)
                    act.activation(weight[e % 2][:, :], w_bank[:, :], ACT.Identity).then_inc(hidden["act"], 1)
                elif step.startswith("gelu"):
                    f, e = int(step[4]), int(step[6:])
                    before, p = (turn, e - 1) if e else (turn - 1, E - 1)
                    after(act, hidden, "pe", f"h{f}_{e}", turn)
                    after(act, hidden, "dve", f"lo{f}_{p}", before)
                    act.activation(hid[:, f, :], h_bank[f][:, :], ACT.Gelu,
                                   bias=b1t[:, f, e:e + 1]).then_inc(hidden["act"], 1)
                else:
                    f, e = int(step[2]), int(step[4:])
                    before, p = (turn, e - 2) if e >= 2 else (turn - 1, E + e - 2)
                    after(act, hidden, "act", f"gelu{f}_{e}", turn)
                    after(act, output, "pe", f"y{p}", before)
                    act.activation(hid_hi[e % 2][:, f, :], hid[:, f, :],
                                   ACT.Identity).then_inc(hidden["act"], 1)

            run(act, "act", emit)

        @block.vector
        def _(dve):
            advance(dve, "dve")
            dve.wait_ge(small_hi, 2)
            dve.tensor_tensor(gw[1][:, :], gate_w[:, :], gw[0][:, :].bitcast(F32), ALU.subtract).then_inc(small_lo, 1)
            dve.tensor_tensor(bb[1][:, :], b2[:, :], bb[0][:, :].bitcast(F32), ALU.subtract).then_inc(small_lo, 1)

            def split(e):
                dve.wait_ge(w_hi_made, 2 * e + 2)
                dve.tensor_tensor(w1[1][:, e, :], raw[0][e % 2][:, :], w1[0][:, e, :].bitcast(F32),
                                  ALU.subtract).then_inc(w_lo_made, 1)
                dve.tensor_tensor(w2[1][:, e, :, :], raw[1][e % 2][:, :].rearrange("p (t d) -> p t d", t=FT),
                                  w2[0][:, e, :, :].bitcast(F32), ALU.subtract).then_inc(w_lo_made, 1)

            def layer_stats(stage, turn, name, source, st, mv, last_reader):
                after(dve, stage, *last_reader)
                for t in range(HQ):
                    op = dve.bn_stats(st[:, t, :], source(t))
                op.then_inc(stage["dve"], 1)
                after(dve, stage, "dve", name[0], turn)
                dve.sem_inc(dve_passed, 1)
                for t in range(HQ):
                    op = dve.bn_aggr(mv[:, t, :], st[:, t, :])
                op.then_inc(stage["dve"], 1)

            def centre(stage, turn, source, mv, rs, dst):
                for t in range(HQ):
                    op = dve.tensor_scalar(dst(t), source(t), mv[:, t, 0:1], rs[:, t:t + 1],
                                           ALU.subtract, ALU.mult)
                op.then_inc(stage["dve"], 1)

            def emit(stage, step, turn):
                i = turn.side

                def then(name, op):
                    op.then_inc(enter["dve"], 1)
                    after(dve, enter, "dve", name, turn)

                def pick(n):
                    ranks = rank[:, None, :].broadcast_to([P, HQ, E])
                    then(f"top{n}", dve.tensor_reduce(top[:, :], rest[:, :, :], AX.X, ALU.max))
                    then(f"eq{n}", dve.tensor_tensor(key[:, :, :], rest[:, :, :], wide(top), ALU.is_equal))
                    then(f"key{n}", dve.tensor_tensor(key[:, :, :], key[:, :, :], ranks, ALU.mult))
                    then(f"best{n}", dve.tensor_reduce(top[:, :], key[:, :, :], AX.X, ALU.max))
                    then(f"pick{n}", dve.tensor_tensor(key[:, :, :], key[:, :, :], wide(top), ALU.is_equal))

                if stage == "split":
                    split(int(step[5:]))
                elif (stage, step) == ("enter", "y"):
                    after(dve, enter, "pe", "project", turn)
                    after(dve, enter, "pool", "w", turn - 1)
                    then("y", dve.tensor_tensor(y[:, :, :], tiles(e_bank), row(rows["bo"]), ALU.add))
                    layer_stats(enter, turn, ("stats",), lambda t: y[:, t, :], stats, mean_var,
                                ("dve", "centre", turn - 1))
                elif (stage, step) == ("enter", "centre"):
                    after(dve, enter, "pool", "rstd", turn)
                    centre(enter, turn, lambda t: y[:, t, :], mean_var, rstd, lambda t: y[:, t, :])
                elif (stage, step) == ("enter", "w_lo"):
                    after(dve, enter, "act", "w_hi", turn)
                    after(dve, hidden, "pe", f"h3_{E - 1}", turn - 2)
                    dve.tensor_tensor(w_t[i][1][:, :], e_bank[:, :], w_t[i][0][:, :].bitcast(F32),
                                      ALU.subtract).then_inc(enter["dve"], 1)
                elif (stage, step) == ("enter", "logits"):
                    after(dve, enter, "pe", "logits", turn)
                    then("logits", dve.tensor_tensor(
                        logits[:, :, :], e_bank[:, 0:HQ * E].rearrange("p (t e) -> p t e", t=HQ),
                        rows["gate_b"][:, None, :].broadcast_to([P, HQ, E]), ALU.add))
                    then("top", dve.tensor_reduce(top[:, :], logits[:, :, :], AX.X, ALU.max))
                    dve.tensor_tensor(rest[:, :, :], logits[:, :, :], wide(top),
                                      ALU.subtract).then_inc(enter["dve"], 1)
                elif (stage, step) == ("enter", "sum"):
                    after(dve, enter, "pool", "exp", turn)
                    then("sum", dve.tensor_reduce(top[:, :], exped[:, :, :], AX.X, ALU.add))
                    then("recip", dve.reciprocal(chosen[:, :, 0], top[:, :]))
                    then("probs", dve.tensor_tensor(probs[:, :, :], exped[:, :, :],
                                                    chosen[:, :, 0:1].broadcast_to([P, HQ, E]), ALU.mult))
                    then("rest", dve.tensor_copy(rest[:, :, :], probs[:, :, :]))
                elif (stage, step) == ("enter", "top0"):
                    pick(0)
                    then("chosen0", dve.tensor_copy(chosen[:, :, :], key[:, :, :]))
                    dve.scalar_tensor_tensor(rest[:, :, :], key[:, :, :], -4.0, rest[:, :, :],
                                             ALU.mult, ALU.add).then_inc(enter["dve"], 1)
                elif (stage, step) == ("enter", "top1"):
                    after(dve, enter, "dve", "drop0", turn)
                    pick(1)
                    then("chosen1", dve.tensor_tensor(chosen[:, :, :], chosen[:, :, :], key[:, :, :], ALU.add))
                    after(dve, enter, "pe", "turn_comb", turn - 1)
                    dve.tensor_tensor(comb[:, :, :], probs[:, :, :], chosen[:, :, :],
                                      ALU.mult).then_inc(enter["dve"], 1)
                elif (stage, step) == ("enter", "comb_lo"):
                    after(dve, enter, "act", "comb_hi", turn)
                    after(dve, hidden, "pe", f"weight{E - 1}", turn - 2)
                    dve.tensor_tensor(comb_t[i][1][:, :], e_bank[0:E, :], comb_t[i][0][:, :].bitcast(F32),
                                      ALU.subtract).then_inc(enter["dve"], 1)
                elif (stage, step) == ("enter", "acc"):
                    after(dve, enter, "pe", "bias2", turn)
                    after(dve, leave, "pe", "turn_acc", turn - 2)
                    dve.tensor_copy(acc[i][:, :], e_bank[:, :]).then_inc(enter["dve"], 1)
                elif (stage, step) == ("leave", "stats1"):
                    after(dve, leave, "pe", "turn_acc", turn)
                    layer_stats(leave, turn, ("stats1",), lambda t: l_bank[:, t * P:(t + 1) * P], l_stats,
                                l_mv, ("dve", "centre2", turn - 1))
                elif (stage, step) == ("leave", "centre1"):
                    after(dve, leave, "pool", "rstd1", turn)
                    after(dve, leave, "pool", "out", turn - 1)
                    centre(leave, turn, lambda t: l_bank[:, t * P:(t + 1) * P], l_mv, l_rstd,
                           lambda t: z[:, t, :])
                elif (stage, step) == ("leave", "stats2"):
                    after(dve, leave, "pool", "z", turn)
                    layer_stats(leave, turn, ("stats2",), lambda t: z[:, t, :], l_stats,
                                l_mv, ("dve", "centre1", turn))
                elif (stage, step) == ("leave", "centre2"):
                    after(dve, leave, "pool", "rstd2", turn)
                    centre(leave, turn, lambda t: z[:, t, :], l_mv, l_rstd, lambda t: z[:, t, :])
                elif stage == "hidden":
                    f, e = int(step[2]), int(step[4:])
                    before, p = (turn, e - 2) if e >= 2 else (turn - 1, E + e - 2)
                    after(dve, output, "pe", f"y{p}", before)
                    after(dve, hidden, rounder(f, e), f"hi{f}_{e}", turn)
                    dve.tensor_tensor(hid_lo[e % 2][:, f, :], hid[:, f, :],
                                      hid_hi[e % 2][:, f, :].bitcast(F32),
                                      ALU.subtract).then_inc(hidden["dve"], 1)
                elif stage == "output" and step.startswith("weighed"):
                    e = int(step[7:])
                    before, p = (turn, e - 1) if e else (turn - 1, E - 1)
                    after(dve, output, "pe", f"y{e}", turn)
                    after(dve, hidden, "act", f"weight{e}", turn)
                    after(dve, output, "dve", f"acc{p}", before)
                    dve.tensor_tensor(weighed[:, :], y_bank[:, :], weight[e % 2][:, :],
                                      ALU.mult).then_inc(output["dve"], 1)
                elif stage == "output":
                    e = int(step[3:])
                    if e == 0:
                        after(dve, enter, "dve", "acc", turn)
                    after(dve, output, "dve", f"weighed{e}", turn)
                    dve.tensor_tensor(acc[i][:, :], acc[i][:, :], weighed[:, :],
                                      ALU.add).then_inc(output["dve"], 1)

            run(dve, "dve", emit)

        @block.gpsimd
        def _(pool):
            advance(pool, "pool")
            pool.tensor_copy(select[:, :, :], rows["select"])
            pool.tensor_copy(gw[0][:, :], gate_w[:, :]).then_inc(small_hi, 1)
            pool.tensor_copy(bb[0][:, :], b2[:, :]).then_inc(small_hi, 1)

            def passed(*what):
                after(pool, *what)
                pool.sem_inc(pool_passed, 1)

            def binary(out, a, b, op, stage):
                pool.tensor_tensor(out, a, b, op).then_inc(stage["pool"], 1)

            def inverse_root(stage, mv, var, rs, names, turn):
                binary(var[:, :], mv[:, :, 1], pows["eps"][:, 0:1].broadcast_to([P, HQ]), ALU.add, stage)
                passed(stage, "pool", names, turn)
                binary(rs[:, :], var[:, :], pows["half"][:, 0:1].broadcast_to([P, HQ]), ALU.pow, stage)

            def emit(stage, step, turn):
                i = turn.side
                if (stage, step) == ("enter", "var"):
                    passed(enter, "dve", "mean", turn)
                    passed(enter, "dve", "centre", turn - 1)
                    inverse_root(enter, mean_var, var, rstd, "var", turn)
                elif (stage, step) == ("enter", "gain"):
                    passed(enter, "dve", "centre", turn)
                    binary(y[:, :, :], y[:, :, :], row(rows["ln1_g"]), ALU.mult, enter)
                elif (stage, step) == ("enter", "shift"):
                    passed(enter, "pool", "gain", turn)
                    binary(y[:, :, :], y[:, :, :], row(rows["ln1_b"]), ALU.add, enter)
                elif (stage, step) == ("enter", "w"):
                    passed(enter, "pool", "shift", turn)
                    passed(leave, "pool", "z", turn - 2)
                    passed(enter, "pe", "turn_w", turn - 2)
                    pool.wait_ge(in_sems[1][i], turn.landed())
                    pool.sem_inc(pool_passed, 1)
                    binary(w_tok[i][:, :, :], y[:, :, :], u_in[i][:, :, :], ALU.add, enter)
                elif (stage, step) == ("enter", "exp"):
                    passed(enter, "dve", "less_top", turn)
                    passed(enter, "dve", "probs", turn - 1)
                    binary(exped[:, :, :], pows["e"][:, 0:1, None].broadcast_to([P, HQ, E]), rest[:, :, :],
                           ALU.pow, enter)
                elif (stage, step) == ("leave", "var1"):
                    passed(leave, "dve", "mean1", turn)
                    passed(leave, "dve", "centre2", turn - 1)
                    inverse_root(leave, l_mv, l_var, l_rstd, "var1", turn)
                elif (stage, step) == ("leave", "gain"):
                    passed(leave, "dve", "centre1", turn)
                    binary(z[:, :, :], z[:, :, :], row(rows["ln2_g"]), ALU.mult, leave)
                elif (stage, step) == ("leave", "shift"):
                    passed(leave, "pool", "gain", turn)
                    binary(z[:, :, :], z[:, :, :], row(rows["ln2_b"]), ALU.add, leave)
                elif (stage, step) == ("leave", "z"):
                    passed(leave, "pool", "shift", turn)
                    binary(z[:, :, :], z[:, :, :], w_tok[i][:, :, :], ALU.add, leave)
                elif (stage, step) == ("leave", "var2"):
                    passed(leave, "dve", "mean2", turn)
                    inverse_root(leave, l_mv, l_var, l_rstd, "var2", turn)
                elif (stage, step) == ("leave", "out"):
                    passed(leave, "dve", "centre2", turn)
                    pool.wait_ge(in_sems[2][i], turn.landed())
                    pool.sem_inc(pool_passed, 1)
                    if not (type(turn.pair) is int and turn.c < 2):
                        pool.wait_ge(stored[i], (turn - 2).landed())
                        pool.sem_inc(pool_passed, 1)
                    binary(z_out[i][:, :, :], z[:, :, :], x_in[i][:, :, :], ALU.add, leave)
                elif stage == "hidden":
                    f, e = int(step[2]), int(step[4:])
                    before, p = (turn, e - 2) if e >= 2 else (turn - 1, E + e - 2)
                    passed(output, "pe", f"y{p}", before)
                    passed(hidden, "act", f"gelu{f}_{e}", turn)
                    binary(hid_hi[e % 2][:, f, :], hid[:, f, :],
                           pows["zero"][:, 0:1].broadcast_to([P, HALF]), ALU.add, hidden)

            run(pool, "pool", emit)


def build(nc, x, w, consts, out):
    with ExitStack() as ctx:
        def sb(name, shape, dt=F32):
            return ctx.enter_context(nc.sbuf_tensor(name, shape, dt))

        def sem(name):
            return ctx.enter_context(nc.semaphore(name))

        kept = nc.dram_tensor("kept", [P, NT, D], F32, kind="Internal").ap()
        kept_u = nc.dram_tensor("kept_u", [P, NT, D], F32, kind="Internal").ap()
        x_v = x.rearrange("b (t p) d -> p (b t) d", p=P)
        out_v = out.rearrange("b (t p) d -> p (b t) d", p=P)
        tokens = sb("tokens", [P, NT, D])
        ident = sb("ident", [P, P])
        rank = sb("rank", [P, E])
        ln_rows = {n: sb(n, [P, D]) for n in ("ln1_g", "ln1_b", "ln2_g", "ln2_b")}
        wo1 = sb("wo1", [P, D])
        early = ExitStack()

        def sb_early(name, shape, dt=F32):
            return early.enter_context(nc.sbuf_tensor(name, shape, dt))

        resid = sb_early("resid", [P, NT, D])
        turned = sb_early("turned", [P, NT * P])
        split_sign = sb_early("split_sign", [P, 3])
        head_mask = sb_early("head_mask", [P, GH])
        ones_row = sb_early("ones_row", [1, P])
        slope_row = sb_early("slope_row", [1, G, P])
        iota_row = sb_early("iota_row", [1, T])
        ident16 = sb_early("ident16", [P, P], BF16)
        causal_mask = sb_early("causal_mask", [P, P], BF16)
        w3 = [sb_early(f"w3_{i}", [P, 2, G, P]) for i in range(2)]
        bias2 = [sb_early(f"bias2_{i}", [P, 2, G]) for i in range(2)]
        wv = [sb_early(f"wv{i}", [P, D]) for i in range(2)]
        wo = [sb_early("wo0", [P, D]), wo1]
        bv = [sb_early(f"bv{i}", [1, D]) for i in range(2)]
        bo = [sb_early(f"bo{i}", [1, D]) for i in range(2)]
        sides = ("L0_attn_", "L0_ffn_")

        with ExitStack() as c2:
            raw = [[c2.enter_context(nc.sbuf_tensor(f"raw{i}{m}", [P, D], F32)) for m in range(2)] for i in range(2)]
            raw_b = c2.enter_context(nc.sbuf_tensor("raw_b", [1, 2, 2, D], F32))
            row3 = c2.enter_context(nc.sbuf_tensor("row3", [1, 2, 2, G, P], F32))
            cols = c2.enter_context(nc.psum_tensor("cols", [P, 2 * 2 * G], F32))
            loaded = c2.enter_context(nc.semaphore("loaded"))
            zeroed = c2.enter_context(nc.semaphore("zeroed"))
            spread = c2.enter_context(nc.semaphore("spread"))
            turned_in = c2.enter_context(nc.semaphore("turned_in"))
            block = c2.enter_context(nc.Block())
            loads = [(raw[i][m][:, :], w[sides[i] + n]) for i in range(2) for m, n in ((0, "Wq"), (1, "Wk"))]
            loads += [(raw_b[0:1, i, m, :], w[sides[i] + n].rearrange("(a d) -> a d", a=1))
                      for i in range(2) for m, n in ((0, "bq"), (1, "bk"))]
            loads += [(wv[i][:, :], w[sides[i] + "Wv"]) for i in range(2)]
            loads += [(wo[i][:, :], w[sides[i] + "Wo"]) for i in range(2)]
            loads += [(bv[i][:, :], w[sides[i] + "bv"].rearrange("(a d) -> a d", a=1)) for i in range(2)]
            loads += [(bo[i][:, :], w[sides[i] + "bo"].rearrange("(a d) -> a d", a=1)) for i in range(2)]
            loads += [(t[:, :], w["L0_ffn_" + n].rearrange("(a d) -> a d", a=1).broadcast_to([P, D]))
                      for n, t in ln_rows.items()]
            loads += [(ident[:, :], consts["ident"]), (split_sign[:, :], consts["split_sign"]),
                      (head_mask[:, :], consts["head_mask"]), (rank[:, :], consts["rank"]),
                      (ones_row[:, :], consts["ones_row"]), (iota_row[:, :], consts["iota_row"]),
                      (slope_row[:, :, :], consts["slope_row"])]
            f32_mask = c2.enter_context(nc.sbuf_tensor("f32_mask", [P, P], F32))
            loads += [(f32_mask[:, :], consts["causal"])]

            @block.sync
            def _(sp):
                for b in range(B):
                    sp.dma_start(resid[:, b * TB:(b + 1) * TB, :], x_v[:, b * TB:(b + 1) * TB, :]).then_inc(loaded, 16)
                for dst, src in loads[0::2]:
                    sp.dma_start(dst, src).then_inc(loaded, 16)

            everything = 16 * (B + len(loads))

            @block.scalar
            def _(act):
                for dst, src in loads[1::2]:
                    act.dma_start(dst, src).then_inc(loaded, 16)
                act.wait_ge(turned_in, 1)
                v = cols[:, :].rearrange("p (i m g) -> p i m g", i=2, m=2)
                for i in range(2):
                    op = act.activation(bias2[i][:, :, :], v[:, i, :, :], ACT.Identity)
                op.then_inc(turned_in, 1)

            @block.gpsimd
            def _(pool):
                for i in range(2):
                    pool.memset(w3[i][:, :, :, :], 0.0)
                pool.memset(row3[:, :, :, :, :], 0.0).then_inc(zeroed, 1)
                pool.wait_ge(zeroed, 1)
                pool.wait_ge(loaded, everything)
                pool.tensor_copy(ident16[:, :], ident[:, :])
                pool.tensor_copy(causal_mask[:, :], f32_mask[:, :])
                for i in range(2):
                    for m in range(2):
                        dst = w3[i][:, m, :, :].rearrange("p g (j r) -> p (g j) r", j=GH)
                        row = row3[0:1, i, m, :, :].rearrange("p g (j r) -> p (g j) r", j=GH)
                        for k in range(3):
                            pool.tensor_copy(dst[:, :, k * DH:(k + 1) * DH],
                                             raw[i][m][:, :].rearrange("p (h d) -> p h d", h=H))
                            src = raw_b[0:1, i, m, :].rearrange("p (h d) -> p h d", h=H)
                            if m == 0:
                                pool.tensor_scalar(row[:, :, k * DH:(k + 1) * DH], src, SCALE, None, ALU.mult)
                            else:
                                pool.tensor_copy(row[:, :, k * DH:(k + 1) * DH], src)
                        one, at = (1.0, ROW_BIAS) if m == 0 else (-1.0, ROW_MAX)
                        op = pool.memset(row[:, :, at:at + 2], one)
                op.then_inc(spread, 1)

            @block.tensor
            def _(pe):
                pe.wait_ge(spread, 1)
                for i in range(2):
                    for m in range(2):
                        for g in range(G):
                            c = (i * 2 + m) * G + g
                            mm = pe.matmul(cols[:, c:c + 1], row3[0:1, i, m, g, :], ones_row[0:1, 0:1],
                                           start=True, stop=True)
                mm.then_inc(turned_in, 1)

        with ExitStack() as c2:
            normed = c2.enter_context(nc.sbuf_tensor("normed", [P, NT, D], F32))
            layernorm(nc, "ln_in", resid, normed)
            turn_and_project(nc, "v1", normed, turned, wv[0], bv[0], ones_row, ident, tokens)
        attention(nc, "at1", Plan(True), turned, tokens, tokens, w3[0], bias2[0], slope_row, iota_row,
                  split_sign, head_mask, ident, ident16, causal_mask)
        with ExitStack() as c2:
            y = c2.enter_context(nc.sbuf_tensor("y1", [P, NT, D], F32))
            y2 = c2.enter_context(nc.sbuf_tensor("y2", [P, NT, D], F32))
            turn_and_project(nc, "o1", tokens, turned, wo[0], bo[0], ones_row, ident, y)
            layernorm(nc, "ln_a1", y, y2, add=resid, final=kept)
            layernorm(nc, "ln_f", y2, resid, final=kept_u)
            turn_and_project(nc, "v2", resid, turned, wv[1], bv[1], ones_row, ident, tokens)
        attention(nc, "at2", Plan(False), turned, tokens, tokens, w3[1], bias2[1], slope_row, iota_row,
                  split_sign, head_mask, ident, ident16, causal_mask)
        early.close()
        gate_w = sb("gate_w", [P, E])
        b2 = sb("b2", [E, D])
        b1t = sb("b1t", [P, FT, E])
        bo_row, gate_row = sb("bo_row", [P, D]), sb("gate_row", [P, E])
        pow_cols = sb("pow_cols", [P, 4])
        select = sb("select", [E, E, P])
        with ExitStack() as c2:
            b1 = c2.enter_context(nc.sbuf_tensor("b1", [E, FF], F32))
            cols = c2.enter_context(nc.psum_tensor("b1cols", [P, FT, E], F32))
            got = c2.enter_context(nc.semaphore("moe_got"))
            tr = c2.enter_context(nc.semaphore("moe_tr"))
            block = c2.enter_context(nc.Block())
            wanted = [(gate_w[:, :], w["L0_ffn_gate_w"]), (b2[:, :], w["L0_ffn_b2"]), (b1[:, :], w["L0_ffn_b1"]),
                      (bo_row[:, :], w["L0_ffn_bo"].rearrange("(a d) -> a d", a=1).broadcast_to([P, D])),
                      (gate_row[:, :], w["L0_ffn_gate_b"].rearrange("(a d) -> a d", a=1).broadcast_to([P, E])),
                      (pow_cols[:, :], consts["pow_cols"]), (select[:, :, :], consts["select"])]

            @block.sync
            def _(sp):
                for dst, src in wanted:
                    sp.dma_start(dst, src).then_inc(got, 16)

            @block.tensor
            def _(pe):
                pe.wait_ge(got, 16 * len(wanted))
                for f in range(FT):
                    mm = pe.transpose(cols[:, f, :], b1[:, f * P:(f + 1) * P], ident[0:E, 0:E])
                mm.then_inc(tr, 1)

            @block.vector
            def _(dve):
                dve.wait_ge(tr, 1)
                dve.tensor_copy(b1t[:, :, :], cols[:, :, :]).then_inc(tr, 1)
        rows = dict(ln_rows, bo=bo_row, gate_b=gate_row, select=select[:, :, :])
        pows = {k: pow_cols[:, i:i + 1] for i, k in enumerate(("eps", "half", "e", "zero"))}
        tail(nc, tokens, kept_u, kept, out_v, wo[1], rows, gate_w, ident, rank, pows, b1t, b2,
             w["L0_ffn_W1"], w["L0_ffn_W2"])


_INS = ["L0_attn_x", "L0_attn_Wq", "L0_attn_bq", "L0_attn_Wk", "L0_attn_bk", "L0_attn_Wv", "L0_attn_bv",
        "L0_attn_Wo", "L0_attn_bo", "L0_ffn_Wq", "L0_ffn_bq", "L0_ffn_Wk", "L0_ffn_bk", "L0_ffn_Wv",
        "L0_ffn_bv", "L0_ffn_Wo", "L0_ffn_bo", "L0_ffn_ln1_g", "L0_ffn_ln1_b", "L0_ffn_ln2_g",
        "L0_ffn_ln2_b", "L0_ffn_gate_w", "L0_ffn_gate_b", "L0_ffn_W1", "L0_ffn_b1", "L0_ffn_W2",
        "L0_ffn_b2"]


def shape_constants():
    import numpy as np
    lane = np.arange(P)
    row = lane % HW
    query_lo = (row >= 2 * DH) & (row < 3 * DH)
    key_lo = ((row >= DH) & (row < 2 * DH)) | (row == ROW_BIAS + 1)
    slope = np.zeros((1, G, GH, HW), np.float32)
    slope[0, :, :, ROW_BIAS:ROW_BIAS + 2] = -np.array(slopes(), np.float32).reshape(G, GH, 1)
    return {
        "ident": np.eye(P, dtype=np.float32),
        "split_sign": -np.stack([query_lo, key_lo, 0 * lane], 1).astype(np.float32),
        "head_mask": (lane[:, None] // HW == np.arange(GH)).astype(np.float32),
        "rank": np.tile(np.arange(E, 0, -1, dtype=np.float32), (P, 1)),
        "ones_row": np.ones((1, P), np.float32),
        "pow_cols": np.tile(np.array([EPS, -0.5, np.e, 0.0], np.float32), (P, 1)),
        "select": np.repeat(np.eye(E, dtype=np.float32)[:, :, None], P, 2),
        "iota_row": np.arange(T, dtype=np.float32)[None],
        "slope_row": slope.reshape(1, G, P),
        "causal": np.where(lane[None, :] > lane[:, None], np.float32(BIG), np.float32(0)).astype(np.float32),
    }


def kernel(**inputs):
    import numpy as np
    import concourse.bacc as bacc
    from concourse.bass_utils import run_bass_kernel_spmd

    nc = bacc.Bacc("TRN2", target_bir_lowering=False, num_devices=1)
    nc.disable_value_cache = True
    arrays, aps = {}, {}
    for name in _INS:
        arrays[name] = np.ascontiguousarray(inputs[name])
    for name, a in shape_constants().items():
        arrays["const_" + name] = a
    for name, a in arrays.items():
        aps[name] = nc.dram_tensor(name, a.shape, mybir.dt.from_np(a.dtype), kind="ExternalInput").ap()
    out = nc.dram_tensor("out_0", (B, T, D), F32, kind="ExternalOutput").ap()
    consts = {k[6:]: v for k, v in aps.items() if k.startswith("const_")}
    build(nc, aps["L0_attn_x"], aps, consts, out)
    r = run_bass_kernel_spmd(nc, [arrays], core_ids=[0])
    return r.results[0]["out_0"]
```

```python
from contextlib import ExitStack

import concourse.bass as bass
from concourse import mybir

F32 = mybir.dt.float32
F32R = mybir.dt.float32r
BF16 = mybir.dt.bfloat16
ALU = mybir.AluOpType
ACT = mybir.ActivationFunctionType
AX = mybir.AxisListType

P = 128
D = 128
B, T = 4, 1024
TB = T // P
NT = B * TB
H, DH = 16, 8
GH = 4
G = H // GH
S = B * G
HW = P // GH
SCALE = DH ** -0.5
EPS = 1e-5
E, FF = 8, 512
FT = FF // P
HALF = 512
HQ = HALF // P
BIG = -1.0e30

ROW_BIAS = 3 * DH
ROW_MAX = 3 * DH + 2


def slopes():
    start = 2.0 ** (-(2.0 ** (3 - 4)))
    return [start * start ** i for i in range(H)]


class Plan:

    def __init__(self, causal):
        self.causal = causal
        self.chunks = []
        for qt in range(TB):
            for kh in range(2):
                n = min(HALF, (qt + 1) * P - kh * HALF) if causal else HALF
                if n <= 0:
                    continue
                per = max(1, HALF // n)
                per = 4 if per >= 4 else per
                for j in range(0, GH, per):
                    self.chunks.append((qt, kh, list(range(j, j + per)), n))
        self.quads = []
        for qh in range(2):
            for kt in range((qh + 1) * HQ if causal else TB):
                self.quads.append((qh, kt))
        self.na = len(self.chunks)
        self.nq = len(self.quads)
        self.nb = GH * self.nq
        self.half_end = [max(i for i, q in enumerate(self.quads) if q[0] == h) for h in range(2)]
        nq = self.nq
        self.lead = 2
        a_steps = nq - 4
        self.a_next = -(-self.na * 4 // nq)
        o0 = self.half_end[0] + 3 - self.lead
        free = [i for i in range(1, nq - 4) if i != o0]
        self.proj_steps = [free[len(free) * i // 4] for i in range(4)]
        self.o_steps = (o0, nq - 1)
        self.mt_steps = (a_steps, a_steps + 1)
        self.m_step = a_steps - 1
        weights = [4 + .6 * (i in self.proj_steps) - (i in self.o_steps) - 1.5 * (i in self.mt_steps) - .5 * (i == self.m_step)
                   for i in range(nq)]
        self.a_of_step = []
        for i in range(nq):
            first, last = (0, a_steps) if i < a_steps else (a_steps, nq)
            n, slot, base = ((self.na - self.a_next, 1, self.a_next) if i < a_steps else (self.a_next, 2, 0))
            total = sum(weights[first:last])
            lo = int(n * sum(weights[first:i]) / total + .5)
            hi = int(n * sum(weights[first:i + 1]) / total + .5)
            self.a_of_step.append([(slot, base + c) for c in range(lo, hi)])

    def interleave(self, bs, ass):
        out = []
        nb, na = len(bs), len(ass)
        for i in range(nb):
            out += ass[na * i // nb:na * (i + 1) // nb]
            out.append(bs[i])
        return out if nb else list(ass)

    def body(self, do_proj=True, do_a1=True, do_a2=True):
        out = []
        for i in range(self.nq):
            q = i + self.lead
            ds, q = (0, q) if q < self.nq else (1, q - self.nq)
            bs = [("b", ds, q * GH + j) for j in range(GH)] if ds == 0 or do_a1 else []
            ass = [("a", d, c) for d, c in self.a_of_step[i] if (do_a1 if d == 1 else do_a2)]
            out += self.interleave(bs, ass)
            if i == self.m_step and do_a1:
                out.append(("m", 1, 0))
            for n, at in enumerate(self.proj_steps):
                if at == i and do_proj:
                    out.append(("proj", 3, n))
            if i in self.o_steps:
                out.append(("otr", 0, self.o_steps.index(i)))
            if i in self.mt_steps and do_a1:
                out.append(("mtr", 1, self.mt_steps.index(i)))
            dp, p = (ds, q - 1) if q else (0, self.nq - 1)
            if dp == 0 or do_a1:
                out.append(("pv", dp, p))
                if p in self.half_end:
                    out.append(("oev", dp, self.half_end.index(p)))
        return out

    def prologue(self):
        out = [("proj", 0, n) for n in range(4)]
        ahead = [("proj", s, n) for s in (1, 2) for n in range(4)]
        early = 5 if self.causal else 8
        out += self.interleave(ahead[:early], [("a", 0, c) for c in range(self.na)])
        out += [("m", 0, 0), ("mtr", 0, 0), ("mtr", 0, 1)]
        bs = [("b", 0, i) for i in range(GH * self.lead)]
        out += self.interleave(bs[:GH] + ahead[early:], [("a", 1, c) for c in range(self.a_next)])
        out += bs[GH:] + [("pv", 0, 0)]
        return out


def last_user(n, i, banks):
    return (0, i - banks) if i >= banks else (1, max(k for k in range(n) if k % banks == i))


class Register:

    def __init__(self, eng, value):
        self.eng, self.value, self.kept = eng, value, {}

    def __mul__(self, k):
        if k not in self.kept:
            self.kept[k] = self.eng.snap(self.value * k)
        return self.kept[k]

    def __add__(self, n):
        return self if n == 0 else Shifted(self, n)


class Shifted:

    def __init__(self, register, n):
        self.register, self.n = register, n

    def __mul__(self, k):
        return self.register * k + self.n * k


class Slot:

    def __init__(self, batch, g):
        self.batch, self.g = batch, g

    def __add__(self, n):
        return Slot(self.batch, self.g + n)

    def __sub__(self, n):
        return Slot(self.batch, self.g - n)

    def count(self, per, more=0):
        return self.batch * (G * per) + (self.g * per + more)


def three(pe, out, a, b, start=True, stop=True):
    pe.matmul(out, a[0], b[0], start=start, stop=False)
    pe.matmul(out, a[0], b[1], start=False, stop=False)
    return pe.matmul(out, a[1], b[0], start=False, stop=stop)


def attention(nc, tag, plan, xT, values, heads_out, w3, bias2, slope_rows, iota_rows, split_sign,
              head_mask, ident, ident16, causal_mask):
    causal = plan.causal
    NA, NB, NQ = plan.na, plan.nb, plan.nq
    with ExitStack() as ctx:
        def sb(name, shape, dt=F32):
            return ctx.enter_context(nc.sbuf_tensor(f"{tag}_{name}", shape, dt))

        def sem(name):
            return ctx.enter_context(nc.semaphore(f"{tag}_{name}"))

        def bank(name):
            return ctx.enter_context(nc.psum_tensor(f"{tag}_{name}", [P, HALF], F32))

        km = [sb(f"km{i}", [P, GH, T], F32R) for i in range(4)]
        fq = [sb(f"fq{i}", [P, T], F32R) for i in range(4)]
        fqm = [sb(f"fqm{i}", [P, T], F32R) for i in range(2)]
        u = [sb(f"u{i}", [P, HALF]) for i in range(2)]
        hi = sb("hi", [P, HALF], F32R)
        part = sb("part", [P, HALF])
        fk = sb("fk", [P, HALF])
        probs = [sb(f"probs{i}", [P, HALF]) for i in range(8)]
        vst = [sb(f"vst{i}", [P, TB, GH, HW]) for i in range(2)]
        mx = sb("mx", [P, 2, TB, GH])
        mfull = sb("mfull", [P, TB, GH])
        mhi = sb("mhi", [P, TB, GH], F32R)
        mpad = sb("mpad", [P, TB, P])
        osb = sb("osb", [P, 2, HALF])
        rec = sb("rec", [P, HQ, GH])
        a_bank = [bank(f"a{i}") for i in range(3)]
        b_bank = [bank(f"b{i}") for i in range(3)]
        pv_bank = bank("pv")
        misc = bank("misc")

        proj_made = sem("proj_made")
        proj_read = sem("proj_read")
        split_done = sem("split_done")
        pool_step = sem("pool_step")
        pool_passed = sem("pool_passed")
        dve_step = sem("dve_step")
        v_staged = sem("v_staged")
        a_made = sem("a_made")
        a_read = sem("a_read")
        m_step = sem("m_step")
        m_padded = sem("m_padded")
        m_turned = sem("m_turned")
        fqm_made = sem("fqm_made")
        b_made = sem("b_made")
        exp_done = sem("exp_done")
        pv_done = sem("pv_done")
        o_read = sem("o_read")
        o_turned = sem("o_turned")
        o_step = sem("o_step")
        o_done = sem("o_done")
        init = sem("init")

        def done(eng, semaphore, per, s, i):
            eng.wait_ge(semaphore, (s + 1).count(per, i + 1))

        block = ctx.enter_context(nc.Block())

        def run(eng, emit):
            emit(plan.prologue(), Slot(0, 0), 0, 0)
            with eng.Fori(0, B - 1) as batch:
                b = Register(eng, batch)
                for g in range(G):
                    emit(plan.body(), Slot(b, g), b, g)
            for g in range(G):
                s = (B - 1) * G + g
                emit(plan.body(s + 3 < S, s + 1 < S, s + 2 < S), Slot(B - 1, g), B - 1, g)

        def where(b, g, ds):
            return (b + (g + ds) // G, (g + ds) % G)

        @block.tensor
        def _(pe):
            for semaphore, per in ((proj_made, 4), (a_made, NA), (m_turned, 2), (b_made, NB),
                                   (pv_done, NQ), (o_turned, 2)):
                pe.sem_inc(semaphore, per)

            def emit(steps, s0, b0, g0):
                prologue = steps[0][0] == "proj" and steps[0][1] == 0
                before = None if prologue else ("otr", -1, 1)
                for what, ds, n in steps:
                    s = s0 + ds
                    if what in ("proj", "otr", "mtr"):
                        if before is not None:
                            bw, bs, bn = before
                            if bw == "proj":
                                done(pe, proj_read, 4, s0 + bs, bn)
                            elif bw == "mtr":
                                done(pe, fqm_made, 2, s0 + bs, bn)
                            else:
                                done(pe, o_done, 2, s0 + bs, bn)
                                if bs < 0:
                                    done(pe, fqm_made, 2, s0, 1)
                        before = (what, ds, n)
                    if what == "proj":
                        b, g = where(b0, g0, ds)
                        m, h = 1 - n % 2, n // 2
                        x = [part[:, bass.ds(b * T + h * HALF, HALF)] for part in xT]
                        alibi = causal and m == 1
                        mm = three(pe, misc[:, :], [part[:, m, g, :] for part in w3], x, stop=not alibi)
                        if alibi:
                            mm = pe.matmul(misc[:, :], slope_rows[:, g, :],
                                           iota_rows[:, h * HALF:(h + 1) * HALF], start=False, stop=True)
                        mm.then_inc(proj_made, 1)
                    elif what == "a":
                        qt, kh, heads, w = plan.chunks[n]
                        _, g = where(b0, g0, ds)
                        needs = [max(2 * kh, 2 * (qt // HQ) + 1) for qt, kh, _, _ in plan.chunks[:n + 1]]
                        if n == 0 or needs[-1] > max(needs[:-1]):
                            done(pe, split_done, 4, s, needs[-1])
                        back, k = last_user(NA, n, 3)
                        done(pe, a_read, NA, s - back, k)
                        out = a_bank[n % 3]
                        diagonal = causal and kh * HALF + w == (qt + 1) * P
                        k = len(heads)
                        scores = out[:, 0:k * w].rearrange("p (k w) -> p k w", k=k)
                        mm = pe.matmul(scores, fq[g][:, qt * P:(qt + 1) * P],
                                       km[g][:, heads[0]:heads[0] + k, kh * HALF:kh * HALF + w],
                                       start=True, stop=not diagonal)
                        if diagonal:
                            mm = pe.matmul(scores[:, :, w - P:w], ident16[:, :],
                                           causal_mask[:, None, :].broadcast_to([P, k, P]),
                                           start=False, stop=True)
                        mm.then_inc(a_made, 1)
                    elif what == "mtr":
                        if prologue and ds == 0 and n == 0:
                            pe.wait_ge(init, 4)
                        done(pe, m_padded, 1, s, 0)
                        for i in range(HQ):
                            mm = pe.transpose(misc[:, i * P:(i + 1) * P], mpad[:, n * HQ + i, :], ident[:, :])
                        mm.then_inc(m_turned, 1)
                    elif what == "b":
                        _, g = where(b0, g0, ds)
                        t, j = n // GH, n % GH
                        qh, kt = plan.quads[t]
                        if n == 0 or plan.quads[(n - 1) // GH][0] != qh:
                            done(pe, fqm_made, 2, s, qh)
                        back, k = last_user(NB, n, 3)
                        done(pe, exp_done, NB, s - back, k)
                        q0 = max(qh * HALF, kt * P) if causal else qh * HALF
                        w = (qh + 1) * HALF - q0
                        diagonal = causal and kt * P >= qh * HALF
                        out = b_bank[n % 3]
                        mm = pe.matmul(out[:, 0:w], km[g][:, j, kt * P:(kt + 1) * P],
                                       fqm[g % 2][:, q0:q0 + w], start=True, stop=not diagonal)
                        if diagonal:
                            mm = pe.matmul(out[:, 0:P], causal_mask[:, :], ident16[:, :],
                                           start=False, stop=True)
                        mm.then_inc(b_made, 1)
                    elif what == "pv":
                        _, g = where(b0, g0, ds)
                        qh, kt = plan.quads[n]
                        if n == 0:
                            done(pe, v_staged, 1, s, 0)
                        if n == 0 or plan.quads[n - 1][0] != qh:
                            done(pe, o_read, 2, s - (qh == 0), 1 - qh)
                        done(pe, exp_done, NB, s, GH * n + GH - 1)
                        q0 = max(qh * HALF, kt * P) if causal else qh * HALF
                        w = (qh + 1) * HALF - q0
                        for j in range(GH):
                            mm = pe.matmul(pv_bank[HW * j:HW * (j + 1), HALF - w:HALF],
                                           vst[g % 2][:, kt, j, :], probs[(n % 2) * GH + j][:, 0:w],
                                           start=(kt == 0), stop=(n == plan.half_end[qh]))
                        mm.then_inc(pv_done, 1)
                    elif what == "otr":
                        done(pe, o_read, 2, s, n)
                        for i in range(HQ):
                            mm = pe.transpose(misc[:, i * P:(i + 1) * P], osb[:, n, i * P:(i + 1) * P],
                                              ident[:, :])
                        mm.then_inc(o_turned, 1)

            run(pe, emit)

        @block.scalar
        def _(act):
            for semaphore, per in ((proj_read, 4), (exp_done, NB), (o_read, 2)):
                act.sem_inc(semaphore, per)

            def emit(steps, s0, b0, g0):
                for what, ds, n in steps:
                    s = s0 + ds
                    if what == "proj":
                        _, g = where(b0, g0, ds)
                        m = 1 - n % 2
                        done(act, proj_made, 4, s, n)
                        done(act, split_done, 4, s, n - 2)
                        act.activation(u[n % 2][:, :], misc[:, :], ACT.Identity,
                                       scale=1.0 if m else SCALE,
                                       bias=bias2[:, m, g:g + 1]).then_inc(proj_read, 1)
                    elif what == "b":
                        t, j = n // GH, n % GH
                        qh, kt = plan.quads[t]
                        q0 = max(qh * HALF, kt * P) if causal else qh * HALF
                        w = (qh + 1) * HALF - q0
                        done(act, b_made, NB, s, n)
                        if j == 0:
                            done(act, pv_done, NQ, s, t - 2)
                        act.activation(probs[(t % 2) * GH + j][:, 0:w], b_bank[n % 3][:, 0:w],
                                       ACT.Exp).then_inc(exp_done, 1)
                    elif what == "oev":
                        done(act, pv_done, NQ, s, plan.half_end[n])
                        done(act, o_turned, 2, s - 1, n)
                        act.activation(osb[:, n, :], pv_bank[:, :], ACT.Identity).then_inc(o_read, 1)

            run(act, emit)

        @block.vector
        def _(dve):
            for semaphore, per in ((a_read, NA), (m_padded, 1), (fqm_made, 2), (o_done, 2),
                                   (m_step, 2), (o_step, 2)):
                dve.sem_inc(semaphore, per)

            def emit(steps, s0, b0, g0):
                for what, ds, n in steps:
                    s = s0 + ds
                    b, g = where(b0, g0, ds)
                    if what == "proj" and ds == 0:
                        m, h = 1 - n % 2, n // 2
                        half = slice(h * HALF, (h + 1) * HALF)
                        un = u[n % 2]
                        own = 5 * h if m else 5 * h + 3
                        done(dve, proj_read, 4, s, n)
                        done(dve, split_done, 4, s, n - 1)
                        dve.tensor_copy(hi[:, :], un[:, :]).then_inc(dve_step, 1)
                        dve.wait_ge(dve_step, own + 1)
                        dve.tensor_tensor(part[:, :], hi[:, :].bitcast(F32),
                                          split_sign[:, m:m + 1].broadcast_to([P, HALF]),
                                          ALU.mult).then_inc(dve_step, 1)
                        dve.wait_ge(dve_step, own + 2)
                        if m == 0:
                            dve.tensor_tensor(fq[g][:, half], part[:, :], un[:, :],
                                              ALU.add).then_inc(split_done, 1)
                        else:
                            dve.tensor_tensor(fk[:, :], part[:, :], un[:, :], ALU.add).then_inc(dve_step, 1)
                            dve.wait_ge(dve_step, own + 3)
                            dve.tensor_tensor(km[g][:, :, half],
                                              fk[:, None, :].broadcast_to([P, GH, HALF]),
                                              head_mask[:, :, None].broadcast_to([P, GH, HALF]),
                                              ALU.mult).then_inc(split_done, 1)
                    elif what == "a":
                        qt, kh, heads, w = plan.chunks[n]
                        done(dve, a_made, NA, s, n)
                        if n == 0:
                            if steps[0] == ("proj", 0, 0) and type(b0) is int and ds == 0:
                                dve.wait_ge(init, 4)
                            done(dve, m_step, 2, s - 1, 0)
                        k = len(heads)
                        dve.tensor_reduce(mx[:, kh, qt, heads[0]:heads[0] + k],
                                          a_bank[n % 3][:, 0:k * w].rearrange("p (k w) -> p k w", k=k),
                                          AX.X, ALU.max).then_inc(a_read, 1)
                    elif what == "m":
                        done(dve, a_read, NA, s, NA - 1)
                        done(dve, m_step, 2, s - 1, 1)
                        done(dve, m_padded, 1, s - 1, 0)
                        done(dve, m_turned, 2, s - 1, 1)
                        dve.tensor_tensor(mfull[:, :, :], mx[:, 0, :, :], mx[:, 1, :, :],
                                          ALU.max).then_inc(m_step, 1)
                        done(dve, m_step, 2, s, 0)
                        dve.tensor_copy(mhi[:, :, :], mfull[:, :, :]).then_inc(m_step, 1)
                        done(dve, m_step, 2, s, 1)
                        pad = mpad[:, :, :].rearrange("p t (j r) -> p t j r", j=GH)
                        dve.tensor_copy(pad[:, :, :, ROW_MAX], mhi[:, :, :].bitcast(F32))
                        dve.tensor_tensor(pad[:, :, :, ROW_MAX + 1], mfull[:, :, :],
                                          mhi[:, :, :].bitcast(F32), ALU.subtract).then_inc(m_padded, 1)
                    elif what == "mtr":
                        done(dve, m_turned, 2, s, n)
                        h = slice(n * HALF, (n + 1) * HALF)
                        dve.tensor_tensor(fqm[g % 2][:, h], fq[g][:, h].bitcast(F32), misc[:, :],
                                          ALU.add).then_inc(fqm_made, 1)
                    elif what == "otr":
                        turned = misc[:, :].rearrange("p (t j c) -> p t j c", t=HQ, j=GH)
                        done(dve, o_turned, 2, s, n)
                        done(dve, o_done, 2, s, n - 1)
                        dve.reciprocal(rec[:, :, :], turned[:, :, :, DH]).then_inc(o_step, 1)
                        done(dve, o_step, 2, s, n)
                        dve.tensor_tensor(
                            heads_out[:, bass.ds(b * TB + n * HQ, HQ), g * GH * DH:(g + 1) * GH * DH]
                            .rearrange("p t (j c) -> p t j c", j=GH),
                            turned[:, :, :, 0:DH],
                            rec[:, :, :, None].broadcast_to([P, HQ, GH, DH]),
                            ALU.mult).then_inc(o_done, 1)

            run(dve, emit)

        @block.gpsimd
        def _(pool):
            for semaphore, per in ((split_done, 4), (v_staged, 1)):
                pool.sem_inc(semaphore, per)
            pool.memset(mpad[:, :, :], 0.0).then_inc(init, 1)
            pool.memset(mx[:, :, :, :], -3.0e38).then_inc(init, 1)
            for v in vst:
                pool.memset(v[:, :, :, :], 0.0).then_inc(pool_step, 1)
            pool.wait_ge(pool_step, 2)
            for v in vst:
                pool.memset(v[:, :, :, DH:DH + 1], 1.0).then_inc(init, 1)
            pool.wait_ge(init, 4)
            count = 2 * 3 + 2 * 2
            pool.sem_inc(pool_step, count - 2 + count)

            def await_(semaphore, per, s, i):
                done(pool, semaphore, per, s, i)
                pool.sem_inc(pool_passed, 1)

            def stage_values(b, g):
                src = values[:, bass.ds(b * TB, TB), g * GH * DH:(g + 1) * GH * DH]
                pool.tensor_copy(vst[g % 2][:, :, :, 0:DH],
                                 src.rearrange("p t (j c) -> p t j c", j=GH)).then_inc(v_staged, 1)

            def emit(steps, s0, b0, g0):
                if steps[0][1] == 0 and steps[0][0] == "proj":
                    stage_values(0, 0)
                else:
                    if any(k[0] == "pv" and k[1] == 1 for k in steps):
                        b, g = where(b0, g0, 1)
                        await_(pv_done, NQ, s0 - 1, NQ - 1)
                        stage_values(b, g)
                first = True
                for what, ds, n in steps:
                    s = s0 + ds
                    if what != "proj":
                        continue
                    _, g = where(b0, g0, ds)
                    m, h = 1 - n % 2, n // 2
                    if ds == 3 and first:
                        await_(b_made, NB, s - 4, NB - 1)
                        first = False
                    if type(b0) is int and steps[0] == ("proj", 0, 0) and ds == 0:
                        continue
                    un = u[n % 2]
                    await_(proj_read, 4, s, n)
                    await_(split_done, 4, s, n - 1)
                    step = 5 * h if m else 5 * h + 3
                    half = slice(h * HALF, (h + 1) * HALF)
                    pool.tensor_tensor(hi[:, :], un[:, :], split_sign[:, 2:3].broadcast_to([P, HALF]),
                                       ALU.add).then_inc(pool_step, 1)
                    await_(pool_step, count, s, step)
                    pool.tensor_tensor(part[:, :], hi[:, :].bitcast(F32),
                                       split_sign[:, m:m + 1].broadcast_to([P, HALF]),
                                       ALU.mult).then_inc(pool_step, 1)
                    await_(pool_step, count, s, step + 1)
                    if m == 0:
                        pool.tensor_tensor(fq[g][:, half], part[:, :], un[:, :],
                                           ALU.add).then_inc(split_done, 1)
                    else:
                        pool.tensor_tensor(fk[:, :], part[:, :], un[:, :], ALU.add).then_inc(pool_step, 1)
                        await_(pool_step, count, s, step + 2)
                        pool.tensor_tensor(km[g][:, :, half],
                                           fk[:, None, :].broadcast_to([P, GH, HALF]),
                                           head_mask[:, :, None].broadcast_to([P, GH, HALF]),
                                           ALU.mult).then_inc(split_done, 1)

            run(pool, emit)


GROUPS = NT // HQ

JOIN = {
    "pe": {"turn_heads": 0, "project": .4},
    "act": {"heads_t": .24, "root1": 1.2, "norm1": 1.5},
    "dve": {"y": .7, "stats1": .85, "scale1": 1.25},
    "pool": {"x1": 1.87},
}
ONLY_SPLIT = {
    "pe": {"turn": 1.6, "values": 2.85},
    "act": {"root2": .5, "norm2": .9, "turned": 2.6, "high": 3.55},
    "dve": {"stats2": 0, "scale2": .6, "values": 3.55, "low": 3.8},
    "pool": {},
}
SPLIT_OFF = {
    "pe": {"turn": 3.22, "values": 3.5},
    "act": {"root2": 2.47, "norm2": 2.85, "turned": 3.35},
    "dve": {"stats2": 2.15, "scale2": 2.52, "values": 3.8, "low": 3.95},
    "pool": {"high": 3.55},
}


def rows_pass(nc, tag, heads, x, turned, values, wo, bo, wv, bv, eps, zero, ident, kept=None, kept_u=None, extra=None):
    extra = extra or {}
    with ExitStack() as ctx:
        def sb(name, shape, dt=F32):
            return ctx.enter_context(nc.sbuf_tensor(f"{tag}_{name}", shape, dt))

        def sem(name):
            return ctx.enter_context(nc.semaphore(f"{tag}_{name}"))

        def banks(name):
            return [ctx.enter_context(nc.psum_tensor(f"{tag}_bank_{name}{i}", [P, HQ, P], F32)) for i in range(2)]

        join = heads is not None
        if join:
            h_bank, y_bank = banks("h"), banks("y")
            heads_t = [sb(f"heads_t{i}", [P, HALF]) for i in range(2)]
            y = [sb(f"y{i}", [P, HQ, D]) for i in range(2)]
            z = [sb(f"z{i}", [P, HQ, D]) for i in range(2)]
            x_in = [sb(f"x_in{i}", [P, HQ, D]) for i in range(2)]
            joined = [sb(f"joined{i}", [P, HQ, D]) for i in range(4)]
            x_landed = [sem(f"x_landed{i}") for i in range(2)]
            kept_landed = [sem(f"kept_landed{i}") for i in range(4)]
            kept_u_landed = [sem(f"kept_u_landed{i}") for i in range(4)]
        n_bank, v_bank = banks("n"), banks("v")
        turned32 = [sb(f"turned32_{i}", [P, HALF]) for i in range(2)]
        normed = [sb(f"normed{i}", [P, HQ, D]) for i in range(4)]
        stats = [[sb(f"stats{k}{i}", [P, HQ, 6]) for i in range(2)] for k in (1, 2)]
        mean_var = [[sb(f"mean_var{k}{i}", [P, HQ, 2]) for i in range(2)] for k in (1, 2)]
        root = [[sb(f"root{k}{i}", [P, HQ]) for i in range(2)] for k in (1, 2)]
        scale = [[sb(f"scale{k}{i}", [P, HQ]) for i in range(2)] for k in (1, 2)]
        shift = [[sb(f"shift{k}{i}", [P, HQ]) for i in range(2)] for k in (1, 2)]
        made = {(who, step): sem(f"{who}_{step}") for stage in ((JOIN, SPLIT_OFF) if join else (ONLY_SPLIT,)) for who in stage
                for step in stage[who]}
        inner = [sem(f"inner{k}") for k in (1, 2)]
        scaled = [sem(f"scaled{k}") for k in (1, 2)]

        def order(who):
            steps = dict(SPLIT_OFF[who], **JOIN[who]) if join else ONLY_SPLIT[who]
            return [(step, n) for _, step, n in sorted((n + at, step, n) for step, at in steps.items()
                                                       for n in range(GROUPS))]

        def after(eng, who, step, n):
            if n >= 0:
                eng.wait_ge(made[who, step], n + 1)

        def group(t, n):
            return t[:, n * HQ:(n + 1) * HQ, :]

        def source(n):
            return joined[n % 4][:, :, :] if join else group(x, n)

        block = ctx.enter_context(nc.Block())

        @block.sync
        def _(sp):
            extra.get("sync", lambda _: None)(sp)
            if join:
                for n in range(2):
                    sp.dma_start(x_in[n][:, :, :], group(x, n)).then_inc(x_landed[n], 16)
                for n in range(GROUPS):
                    after(sp, "pool", "x1", n)
                    sp.dma_start(group(kept, n), joined[n % 4][:, :, :]).then_inc(kept_landed[n % 4], 16)
                    if n + 2 < GROUPS:
                        sp.dma_start(x_in[n % 2][:, :, :], group(x, n + 2)).then_inc(x_landed[n % 2], 16)
                    after(sp, "act", "norm2", n)
                    sp.dma_start(group(kept_u, n), normed[n % 4][:, :, :]).then_inc(kept_u_landed[n % 4], 16)
                for s in kept_landed + kept_u_landed:
                    sp.wait_ge(s, 16 * GROUPS // 4)

        @block.tensor
        def _(pe):
            extra.get("tensor", lambda _: None)(pe)
            for step, n in order("pe"):
                i = n % 2
                if step == "turn_heads":
                    after(pe, "act", "heads_t", n - 2)
                    for t in range(HQ):
                        mm = pe.transpose(h_bank[i][:, t, :], heads[:, n * HQ + t, :], ident[:, :])
                elif step == "project":
                    after(pe, "act", "heads_t", n)
                    after(pe, "dve", "y", n - 2)
                    for t in range(HQ):
                        mm = pe.matmul(y_bank[i][:, t, :], heads_t[i][:, t * P:(t + 1) * P], wo[:, :],
                                       start=True, stop=True)
                elif step == "turn":
                    after(pe, "act", "norm2", n)
                    after(pe, "act", "turned", n - 2)
                    for t in range(HQ):
                        mm = pe.transpose(n_bank[i][:, t, :], normed[n % 4][:, t, :], ident[:, :])
                elif step == "values":
                    after(pe, "act", "turned", n)
                    after(pe, "dve", "values", n - 2)
                    for t in range(HQ):
                        mm = pe.matmul(v_bank[i][:, t, :], turned32[i][:, t * P:(t + 1) * P], wv[:, :],
                                       start=True, stop=True)
                mm.then_inc(made["pe", step], 1)
                if step == "values":
                    extra.get("tensor_between", lambda *_: None)(pe, n)

        @block.scalar
        def _(act):
            extra.get("scalar", lambda _: None)(act)
            for step, n in order("act"):
                i = n % 2
                k = 0 if step.endswith("1") else 1
                if step == "heads_t":
                    after(act, "pe", "turn_heads", n)
                    after(act, "pe", "project", n - 2)
                    op = act.activation(heads_t[i][:, :], h_bank[i][:, :, :].rearrange("p a b -> p (a b)"),
                                        ACT.Identity)
                elif step.startswith("root"):
                    after(act, "dve", f"stats{k + 1}", n)
                    after(act, "dve", f"scale{k + 1}", n - 2)
                    op = act.activation(root[k][i][:, :], mean_var[k][i][:, :, 1], ACT.Sqrt, bias=eps)
                elif step.startswith("norm"):
                    after(act, "dve", f"scale{k + 1}", n)
                    if k == 0:
                        after(act, "pool", "x1", n - 2)
                    else:
                        after(act, "pe", "turn", n - 4)
                        if join and n >= 4:
                            act.wait_ge(kept_u_landed[n % 4], 16 * (n // 4))
                    for t in range(HQ):
                        src = y[i][:, t, :] if k == 0 else source(n)[:, t, :]
                        dst = z[i][:, t, :] if k == 0 else normed[n % 4][:, t, :]
                        op = act.activation(dst, src, ACT.Identity, bias=shift[k][i][:, t:t + 1],
                                            scale=scale[k][i][:, t:t + 1])
                elif step == "turned":
                    after(act, "pe", "turn", n)
                    after(act, "pe", "values", n - 2)
                    after(act, "dve", "low", n - 2)
                    op = act.activation(turned32[i][:, :],
                                        n_bank[i][:, :, :].rearrange("p a b -> p (a b)"), ACT.Identity)
                elif step == "high":
                    after(act, "act", "turned", n)
                    op = act.activation(turned[0][:, n * HALF:(n + 1) * HALF], turned32[i][:, :], ACT.Identity)
                op.then_inc(made["act", step], 1)
            extra.get("scalar_end", lambda _: None)(act)

        @block.vector
        def _(dve):
            extra.get("vector", lambda _: None)(dve)
            for step, n in order("dve"):
                i = n % 2
                k = 0 if step.endswith("1") else 1
                if step == "y":
                    after(dve, "pe", "project", n)
                    after(dve, "act", "norm1", n - 2)
                    op = dve.tensor_tensor(y[i][:, :, :], y_bank[i][:, :, :],
                                           bo[:, None, :].broadcast_to([P, HQ, D]), ALU.add)
                elif step.startswith("stats"):
                    if k == 0:
                        after(dve, "dve", "y", n)
                    elif join:
                        after(dve, "pool", "x1", n)
                    else:
                        dve.wait_ge(extra["x_landed"][n * HQ // TB], 16)
                    after(dve, "act", f"root{k + 1}", n - 2)
                    after(dve, "dve", f"scale{k + 1}", n - 2)
                    for t in range(HQ):
                        src = y[i][:, t, :] if k == 0 else source(n)[:, t, :]
                        op = dve.bn_stats(stats[k][i][:, t, :], src)
                    op.then_inc(inner[k], 1)
                    dve.wait_ge(inner[k], n + 1)
                    for t in range(HQ):
                        op = dve.bn_aggr(mean_var[k][i][:, t, :], stats[k][i][:, t, :])
                elif step.startswith("scale"):
                    after(dve, "act", f"root{k + 1}", n)
                    after(dve, "act", f"norm{k + 1}", n - 2)
                    dve.reciprocal(scale[k][i][:, :], root[k][i][:, :]).then_inc(scaled[k], 1)
                    dve.wait_ge(scaled[k], n + 1)
                    op = dve.scalar_tensor_tensor(shift[k][i][:, :], mean_var[k][i][:, :, 0], -1.0,
                                                  scale[k][i][:, :], ALU.mult, ALU.mult)
                elif step == "low":
                    after(dve, "pool" if join else "act", "high", n)
                    at = slice(n * HALF, (n + 1) * HALF)
                    op = dve.tensor_tensor(turned[1][:, at], turned32[i][:, :],
                                           turned[0][:, at].bitcast(F32), ALU.subtract)
                elif step == "values":
                    after(dve, "pe", "values", n)
                    op = dve.tensor_tensor(group(values, n), v_bank[i][:, :, :],
                                           bv[:, None, :].broadcast_to([P, HQ, D]), ALU.add)
                op.then_inc(made["dve", step], 1)
            extra.get("vector_end", lambda _: None)(dve)

        @block.gpsimd
        def _(pool):
            extra.get("gpsimd", lambda _: None)(pool)
            for step, n in order("pool"):
                if step == "x1":
                    after(pool, "act", "norm1", n)
                    after(pool, "act", "norm2", n - 4)
                    after(pool, "dve", "stats2", n - 4)
                    pool.wait_ge(x_landed[n % 2], 16 * (n // 2 + 1))
                    if n >= 4:
                        pool.wait_ge(kept_landed[n % 4], 16 * (n // 4))
                    pool.tensor_tensor(joined[n % 4][:, :, :], x_in[n % 2][:, :, :], z[n % 2][:, :, :],
                                       ALU.add).then_inc(made["pool", step], 1)
                else:
                    after(pool, "act", "turned", n)
                    pool.tensor_tensor(turned[0][:, n * HALF:(n + 1) * HALF], turned32[n % 2][:, :],
                                       zero.broadcast_to([P, HALF]), ALU.add).then_inc(made["pool", step], 1)


class Turn:

    def __init__(self, pair, c):
        self.pair, self.c = pair, c
        self.side = c % 2

    def __add__(self, n):
        return Turn(self.pair, self.c + n)

    def __sub__(self, n):
        return Turn(self.pair, self.c - n)

    def count(self, per, more=0):
        return self.pair * (2 * per) + (self.c * per + more)

    def landed(self):
        return self.pair * 16 + (self.c // 2 + 1) * 16


NBLK = NT // HQ

ENTER = {
    "pe": {"turn_heads": -7.855, "project": -7.64, "turn_w": -4.189, "logits": -3.444, "turn_comb": -1.138,
            "bias2": -0.01},
    "act": {"heads_t": -7.8, "w_hi": -3.963, "comb_hi": -0.874},
    "dve": {"y": -7.1, "stats": -7.1, "mean": -7.1, "centre": -6.498, "w_lo": -4.02, "logits": -3.437,
            "top": -3.437, "less_top": -3.437, "sum": -2.281, "recip": -2.281, "probs": -2.281,
            "rest": -2.281, "top0": -2.1, "eq0": -2.1, "key0": -2.1, "best0": -2.1, "pick0": -2.1,
            "chosen0": -2.1, "drop0": -2.1, "top1": -1.467, "eq1": -1.467, "key1": -1.467, "best1": -1.467,
            "pick1": -1.467, "chosen1": -1.467, "comb": -1.467, "comb_lo": -0.4, "acc": -0.295},
    "pool": {"var": -7.133, "rstd": -7.133, "gain": -6.2, "shift": -5.8, "w": -5.05, "exp": -3.416},
}
LEAVE = {
    "pe": {"turn_acc": 9.559},
    "dve": {"stats1": 9.58, "mean1": 9.58, "centre1": 10.031, "stats2": 11.301, "mean2": 11.301,
            "centre2": 12.273},
    "pool": {"var1": 9.8, "rstd1": 9.8, "gain": 10.25, "shift": 10.932, "z": 10.944, "var2": 11.987,
            "rstd2": 11.987, "out": 12.577},
}
POOL_ROUNDS = {e: e != 5 for e in range(E)}


def rounder(f, e):
    return "pool" if f < 2 and POOL_ROUNDS[e] else "act"


HIDDEN = {
    "pe": {f"{k}{e}": e + t for e in range(E)
           for k, t in (("h0_", 0), ("h1_", 0.189), ("weight", 0.256), ("h2_", 0.284), ("h3_", 0.394))},
    "act": {f"{k}{e}": e + t for e in range(E)
            for k, t in (("gelu0_", 0.066), ("gelu1_", 0.237), ("gelu2_", 0.521), ("gelu3_", 0.54),
                         ("hi0_", 0.557), ("hi1_", 0.63), ("hi2_", 0.67), ("hi3_", 0.683),
                         ("weight", 0.904))
            if k[:2] != "hi" or rounder(int(k[2]), e) == "act"},
    "dve": {f"{k}{e}": e + t for e in range(E)
            for k, t in (("lo0_", 0.553), ("lo1_", 0.597), ("lo2_", 0.957), ("lo3_", 1.122))},
    "pool": {f"hi{f}_{e}": e + t for e in range(E) for f, t in ((0, 0.417), (1, 0.537))
             if rounder(f, e) == "pool"},
}
OUTPUT = {
    "pe": {f"y{e}": e + 1.575 for e in range(E)},
    "dve": {f"{k}{e}": e + 2.036 for e in range(E) for k in ("weighed", "acc")},
}
SPLIT = {k: {f"split{e}": (e - 1.5 if e >= 2 else -7.6 + e / 2) for e in range(E)} for k in ("act", "dve")}


def tail(nc, heads, kept_u, kept, out_v, wo, rows, gate_w, ident, rank, pows, b1t, b2, W1, W2):
    with ExitStack() as ctx:
        def sb(name, shape, dt=F32):
            return ctx.enter_context(nc.sbuf_tensor(f"t_{name}", shape, dt))

        def sem(name):
            return ctx.enter_context(nc.semaphore(f"t_{name}"))

        def bank(name):
            return ctx.enter_context(nc.psum_tensor(f"t_bank_{name}", [P, HALF], F32))

        raw = [[sb(f"raw{m}{i}", [P, FF]) for i in range(2)] for m in range(2)]
        w1 = [sb(f"w1{k}", [P, E, FF], F32R) for k in ("hi", "lo")]
        w2 = [sb(f"w2{k}", [P, E, FT, D], F32R) for k in ("hi", "lo")]
        gw = [sb(f"gw{k}", [P, E], F32R) for k in ("hi", "lo")]
        bb = [sb(f"b2{k}", [E, D], F32R) for k in ("hi", "lo")]
        select = sb("select", [E, E, P], F32R)
        heads_in = [sb(f"heads_in{i}", [P, HQ, D]) for i in range(2)]
        u_in = [sb(f"u_in{i}", [P, HQ, D]) for i in range(2)]
        x_in = [sb(f"x_in{i}", [P, HQ, D]) for i in range(2)]
        z_out = [sb(f"z_out{i}", [P, HQ, D]) for i in range(2)]
        heads_t = sb("heads_t", [P, HALF])
        y = sb("y", [P, HQ, D])
        stats = sb("stats", [P, HQ, 6])
        mean_var = sb("mean_var", [P, HQ, 2])
        var = sb("var", [P, HQ])
        rstd = sb("rstd", [P, HQ])
        w_tok = [sb(f"w_tok{i}", [P, HQ, D]) for i in range(2)]
        w_t = [[sb(f"w_t{i}{k}", [P, HALF], F32R) for k in ("hi", "lo")] for i in range(2)]
        logits = sb("logits", [P, HQ, E])
        top = sb("top", [P, HQ])
        exped = sb("exped", [P, HQ, E])
        probs = sb("probs", [P, HQ, E])
        rest = sb("rest", [P, HQ, E])
        key = sb("key", [P, HQ, E])
        chosen = sb("chosen", [P, HQ, E])
        comb = sb("comb", [P, HQ, E])
        comb_t = [[sb(f"comb_t{i}{k}", [E, HALF], F32R) for k in ("hi", "lo")] for i in range(2)]
        weight = [sb(f"weight{i}", [P, HALF]) for i in range(2)]
        hid = sb("hid", [P, FT, HALF])
        hid_hi = [sb(f"hid_hi{i}", [P, FT, HALF], F32R) for i in range(2)]
        hid_lo = [sb(f"hid_lo{i}", [P, FT, HALF], F32R) for i in range(2)]
        weighed = sb("weighed", [P, HALF])
        acc = [sb(f"acc{i}", [P, HALF]) for i in range(2)]
        l_stats = sb("l_stats", [P, HQ, 6])
        l_mv = sb("l_mv", [P, HQ, 2])
        l_var = sb("l_var", [P, HQ])
        l_rstd = sb("l_rstd", [P, HQ])
        z = sb("z", [P, HQ, D])
        h_bank = [bank(f"h{i}") for i in range(FT)]
        y_bank, w_bank, e_bank, l_bank = bank("y"), bank("w"), bank("e"), bank("l")

        enter = {k: sem(f"enter_{k}") for k in ENTER}
        leave = {k: sem(f"leave_{k}") for k in LEAVE}
        hidden = {k: sem(f"hidden_{k}") for k in HIDDEN}
        output = {k: sem(f"output_{k}") for k in OUTPUT}
        steps = {id(enter): ENTER, id(leave): LEAVE, id(hidden): HIDDEN, id(output): OUTPUT}
        in_sems = [[sem(f"{n}_landed{i}") for i in range(2)] for n in ("heads", "u", "x")]
        stored = [sem(f"stored{i}") for i in range(2)]
        raw_in = [sem(f"raw_landed{i}") for i in range(2)]
        w_hi_made = sem("w_hi_made")
        w_lo_made = sem("w_lo_made")
        small_hi = sem("small_hi")
        small_lo = sem("small_lo")
        pool_passed = sem("pool_passed")
        dve_passed = sem("dve_passed")

        def after(eng, stage, who, step, turn):
            names = list(steps[id(stage)][who])
            eng.wait_ge(stage[who], (turn + 2).count(len(names), names.index(step) + 1))

        def advance(eng, who):
            for stage in (enter, leave, hidden, output):
                if who in stage:
                    eng.sem_inc(stage[who], 2 * len(steps[id(stage)][who]))

        def order(who, windows):
            out = []
            for name, stage in (("enter", ENTER), ("leave", LEAVE), ("hidden", HIDDEN), ("output", OUTPUT)):
                for place, (step, at) in enumerate(stage.get(who, {}).items()):
                    window = int(at // E)
                    if window in windows:
                        out.append((at - E * window, name, place, step, -window))
            if windows == (-1,) or windows == (-1, 0):
                window = -1 if windows == (-1,) else 0
                for step, at in SPLIT.get(who, {}).items():
                    if int(at // E) == window:
                        out.append((at - E * window, "split", 0, step, -window))
            return [(name, step, d) for at, name, place, step, d in sorted(out)]

        def run(eng, who, emit):
            def part(windows, now):
                for name, step, d in order(who, windows):
                    emit(name, step, now + d)
            part((-1,), Turn(0, -1))
            part((-1, 0), Turn(0, 0))
            with eng.Fori(0, (NBLK - 2) // 2) as register:
                pair = Register(eng, register)
                for c in (1, 2):
                    part((-1, 0, 1), Turn(pair, c))
            part((0, 1), Turn(0, NBLK - 1))
            part((1,), Turn(0, NBLK))

        def tiles(x):
            return x[:, :].rearrange("p (t c) -> p t c", t=HQ)

        def wide(x, n=E):
            return x[:, :, None].broadcast_to([P, HQ, n])

        def row(x):
            return x[:, None, :].broadcast_to([P, HQ, D])

        block = ctx.enter_context(nc.Block())

        @block.sync
        def _(sp):
            def load(turn, register, c):
                at = bass.ds(register * (2 * HQ) + c * HQ, HQ)
                i = turn.side
                after(sp, enter, "pe", "turn_heads", turn - 2)
                sp.dma_start(heads_in[i][:, :, :], heads[:, at, :]).then_inc(in_sems[0][i], 16)
                after(sp, enter, "pool", "w", turn - 2)
                sp.dma_start(u_in[i][:, :, :], kept_u[:, at, :]).then_inc(in_sems[1][i], 16)

            def load_x(turn, register, c):
                after(sp, leave, "pool", "out", turn - 2)
                sp.dma_start(x_in[turn.side][:, :, :],
                             kept[:, bass.ds(register * (2 * HQ) + c * HQ, HQ), :]).then_inc(in_sems[2][turn.side], 16)

            def store(turn, register, c):
                after(sp, leave, "pool", "out", turn)
                sp.dma_start(out_v[:, bass.ds(register * (2 * HQ) + c * HQ, HQ), :],
                             z_out[turn.side][:, :, :]).then_inc(stored[turn.side], 16)

            load(Turn(0, 0), 0, 0)
            load(Turn(0, 1), 0, 1)
            load_x(Turn(0, 0), 0, 0)
            for e in range(E):
                if e >= 2:
                    sp.wait_ge(w_lo_made, 2 * (e - 1))
                sp.dma_start(raw[0][e % 2][:, :], W1[e]).then_inc(raw_in[e % 2], 16)
                sp.dma_start(raw[1][e % 2][:, :].rearrange("p (t d) -> p t d", t=FT),
                             W2[e].rearrange("(t p) d -> p t d", p=P)).then_inc(raw_in[e % 2], 16)
            with sp.Fori(0, (NBLK - 2) // 2) as register:
                pair = Register(sp, register)
                for c in (1, 2):
                    load(Turn(pair, c + 1), register, c + 1)
                    load_x(Turn(pair, c), register, c)
                    store(Turn(pair, c - 1), register, c - 1)
            load_x(Turn(0, NBLK - 1), 0, NBLK - 1)
            store(Turn(0, NBLK - 2), 0, NBLK - 2)
            store(Turn(0, NBLK - 1), 0, NBLK - 1)
            for s in stored:
                sp.wait_ge(s, 16 * NBLK // 2)

        @block.tensor
        def _(pe):
            advance(pe, "pe")

            def emit(stage, step, turn):
                i = turn.side
                if (stage, step) == ("enter", "turn_heads"):
                    pe.wait_ge(in_sems[0][i], turn.landed())
                    after(pe, enter, "dve", "acc", turn - 1)
                    for t in range(HQ):
                        mm = pe.transpose(e_bank[:, t * P:(t + 1) * P], heads_in[i][:, t, :], ident[:, :])
                    mm.then_inc(enter["pe"], 1)
                elif (stage, step) == ("enter", "project"):
                    after(pe, enter, "act", "heads_t", turn)
                    for t in range(HQ):
                        mm = pe.matmul(e_bank[:, t * P:(t + 1) * P], heads_t[:, t * P:(t + 1) * P],
                                       wo[:, :], start=True, stop=True)
                    mm.then_inc(enter["pe"], 1)
                elif (stage, step) == ("enter", "turn_w"):
                    after(pe, enter, "pool", "w", turn)
                    after(pe, enter, "dve", "y", turn)
                    for t in range(HQ):
                        mm = pe.transpose(e_bank[:, t * P:(t + 1) * P], w_tok[i][:, t, :], ident[:, :])
                    mm.then_inc(enter["pe"], 1)
                elif (stage, step) == ("enter", "logits"):
                    after(pe, enter, "dve", "w_lo", turn)
                    pe.wait_ge(small_lo, 2)
                    for t in range(HQ):
                        at = slice(t * P, (t + 1) * P)
                        mm = three(pe, e_bank[:, t * E:(t + 1) * E], [m[:, at] for m in w_t[i]],
                                   [m[:, :] for m in gw])
                    mm.then_inc(enter["pe"], 1)
                elif (stage, step) == ("enter", "turn_comb"):
                    after(pe, enter, "dve", "comb", turn)
                    for t in range(HQ):
                        mm = pe.transpose(e_bank[0:E, t * P:(t + 1) * P], comb[:, t, :], ident[:, :])
                    mm.then_inc(enter["pe"], 1)
                elif (stage, step) == ("enter", "bias2"):
                    after(pe, enter, "dve", "comb_lo", turn)
                    mm = three(pe, e_bank[:, :], [m[:, :] for m in bb], [m[:, :] for m in comb_t[i]])
                    mm.then_inc(enter["pe"], 1)
                elif stage == "leave":
                    after(pe, output, "dve", f"acc{E - 1}", turn)
                    after(pe, leave, "dve", "centre1", turn - 1)
                    for t in range(HQ):
                        mm = pe.transpose(l_bank[:, t * P:(t + 1) * P], acc[i][:, t * P:(t + 1) * P],
                                          ident[:, :])
                    mm.then_inc(leave["pe"], 1)
                elif stage == "hidden" and step.startswith("weight"):
                    e = int(step[6:])
                    before, p = (turn, e - 1) if e else (turn - 1, E - 1)
                    if e == 0:
                        after(pe, enter, "dve", "comb_lo", turn)
                    after(pe, hidden, "act", f"weight{p}", before)
                    for n in range(2):
                        mm = pe.matmul(w_bank[:, :], select[:, e, :], comb_t[i][n][:, :],
                                       start=(n == 0), stop=(n == 1))
                    mm.then_inc(hidden["pe"], 1)
                elif stage == "hidden":
                    f, e = int(step[1]), int(step[3:])
                    before, p = (turn, e - 1) if e else (turn - 1, E - 1)
                    if type(turn.pair) is int and turn.c == 0 and f == 0:
                        pe.wait_ge(w_lo_made, 2 * (e + 1))
                    if f == 0 and e == 0:
                        after(pe, enter, "dve", "w_lo", turn)
                    after(pe, hidden, "act", f"gelu{f}_{p}", before)
                    at = slice(f * P, (f + 1) * P)
                    three(pe, h_bank[f][:, :], [m[:, e, at] for m in w1],
                          [m[:, :] for m in w_t[i]]).then_inc(hidden["pe"], 1)
                elif stage == "output":
                    e = int(step[1:])
                    before, p = (turn, e - 1) if e else (turn - 1, E - 1)
                    after(pe, output, "dve", f"weighed{p}", before)
                    for f in range(FT):
                        after(pe, hidden, "dve", f"lo{f}_{e}", turn)
                        mm = three(pe, y_bank[:, :], [m[:, e, f, :] for m in w2],
                                   [m[e % 2][:, f, :] for m in (hid_hi, hid_lo)],
                                   start=(f == 0), stop=(f == FT - 1))
                    mm.then_inc(output["pe"], 1)

            run(pe, "pe", emit)

        @block.scalar
        def _(act):
            advance(act, "act")

            def emit(stage, step, turn):
                i = turn.side
                if stage == "split":
                    e = int(step[5:])
                    act.wait_ge(raw_in[e % 2], 32 * (e // 2 + 1))
                    act.activation(w1[0][:, e, :], raw[0][e % 2][:, :], ACT.Identity).then_inc(w_hi_made, 1)
                    act.activation(w2[0][:, e, :, :], raw[1][e % 2][:, :].rearrange("p (t d) -> p t d", t=FT),
                                   ACT.Identity).then_inc(w_hi_made, 1)
                elif (stage, step) == ("enter", "heads_t"):
                    after(act, enter, "pe", "turn_heads", turn)
                    after(act, enter, "pe", "project", turn - 1)
                    act.activation(heads_t[:, :], e_bank[:, :], ACT.Identity).then_inc(enter["act"], 1)
                elif (stage, step) == ("enter", "w_hi"):
                    after(act, enter, "pe", "turn_w", turn)
                    after(act, hidden, "pe", f"h3_{E - 1}", turn - 2)
                    act.activation(w_t[i][0][:, :], e_bank[:, :], ACT.Identity).then_inc(enter["act"], 1)
                elif (stage, step) == ("enter", "comb_hi"):
                    after(act, enter, "pe", "turn_comb", turn)
                    after(act, hidden, "pe", f"weight{E - 1}", turn - 2)
                    act.activation(comb_t[i][0][:, :], e_bank[0:E, :], ACT.Identity).then_inc(enter["act"], 1)
                elif step.startswith("weight"):
                    e = int(step[6:])
                    before, p = (turn, e - 2) if e >= 2 else (turn - 1, E + e - 2)
                    after(act, hidden, "pe", f"weight{e}", turn)
                    after(act, output, "dve", f"weighed{p}", before)
                    act.activation(weight[e % 2][:, :], w_bank[:, :], ACT.Identity).then_inc(hidden["act"], 1)
                elif step.startswith("gelu"):
                    f, e = int(step[4]), int(step[6:])
                    before, p = (turn, e - 1) if e else (turn - 1, E - 1)
                    after(act, hidden, "pe", f"h{f}_{e}", turn)
                    after(act, hidden, "dve", f"lo{f}_{p}", before)
                    act.activation(hid[:, f, :], h_bank[f][:, :], ACT.Gelu,
                                   bias=b1t[:, f, e:e + 1]).then_inc(hidden["act"], 1)
                else:
                    f, e = int(step[2]), int(step[4:])
                    before, p = (turn, e - 2) if e >= 2 else (turn - 1, E + e - 2)
                    after(act, hidden, "act", f"gelu{f}_{e}", turn)
                    after(act, output, "pe", f"y{p}", before)
                    act.activation(hid_hi[e % 2][:, f, :], hid[:, f, :],
                                   ACT.Identity).then_inc(hidden["act"], 1)

            run(act, "act", emit)

        @block.vector
        def _(dve):
            advance(dve, "dve")
            dve.wait_ge(small_hi, 2)
            dve.tensor_tensor(gw[1][:, :], gate_w[:, :], gw[0][:, :].bitcast(F32), ALU.subtract).then_inc(small_lo, 1)
            dve.tensor_tensor(bb[1][:, :], b2[:, :], bb[0][:, :].bitcast(F32), ALU.subtract).then_inc(small_lo, 1)

            def split(e):
                dve.wait_ge(w_hi_made, 2 * e + 2)
                dve.tensor_tensor(w1[1][:, e, :], raw[0][e % 2][:, :], w1[0][:, e, :].bitcast(F32),
                                  ALU.subtract).then_inc(w_lo_made, 1)
                dve.tensor_tensor(w2[1][:, e, :, :], raw[1][e % 2][:, :].rearrange("p (t d) -> p t d", t=FT),
                                  w2[0][:, e, :, :].bitcast(F32), ALU.subtract).then_inc(w_lo_made, 1)

            def layer_stats(stage, turn, name, source, st, mv, last_reader):
                after(dve, stage, *last_reader)
                for t in range(HQ):
                    op = dve.bn_stats(st[:, t, :], source(t))
                op.then_inc(stage["dve"], 1)
                after(dve, stage, "dve", name[0], turn)
                dve.sem_inc(dve_passed, 1)
                for t in range(HQ):
                    op = dve.bn_aggr(mv[:, t, :], st[:, t, :])
                op.then_inc(stage["dve"], 1)

            def centre(stage, turn, source, mv, rs, dst):
                for t in range(HQ):
                    op = dve.tensor_scalar(dst(t), source(t), mv[:, t, 0:1], rs[:, t:t + 1],
                                           ALU.subtract, ALU.mult)
                op.then_inc(stage["dve"], 1)

            def emit(stage, step, turn):
                i = turn.side

                def then(name, op):
                    op.then_inc(enter["dve"], 1)
                    after(dve, enter, "dve", name, turn)

                def pick(n):
                    ranks = rank[:, None, :].broadcast_to([P, HQ, E])
                    then(f"top{n}", dve.tensor_reduce(top[:, :], rest[:, :, :], AX.X, ALU.max))
                    then(f"eq{n}", dve.tensor_tensor(key[:, :, :], rest[:, :, :], wide(top), ALU.is_equal))
                    then(f"key{n}", dve.tensor_tensor(key[:, :, :], key[:, :, :], ranks, ALU.mult))
                    then(f"best{n}", dve.tensor_reduce(top[:, :], key[:, :, :], AX.X, ALU.max))
                    then(f"pick{n}", dve.tensor_tensor(key[:, :, :], key[:, :, :], wide(top), ALU.is_equal))

                if stage == "split":
                    split(int(step[5:]))
                elif (stage, step) == ("enter", "y"):
                    after(dve, enter, "pe", "project", turn)
                    after(dve, enter, "pool", "w", turn - 1)
                    then("y", dve.tensor_tensor(y[:, :, :], tiles(e_bank), row(rows["bo"]), ALU.add))
                    layer_stats(enter, turn, ("stats",), lambda t: y[:, t, :], stats, mean_var,
                                ("dve", "centre", turn - 1))
                elif (stage, step) == ("enter", "centre"):
                    after(dve, enter, "pool", "rstd", turn)
                    centre(enter, turn, lambda t: y[:, t, :], mean_var, rstd, lambda t: y[:, t, :])
                elif (stage, step) == ("enter", "w_lo"):
                    after(dve, enter, "act", "w_hi", turn)
                    after(dve, hidden, "pe", f"h3_{E - 1}", turn - 2)
                    dve.tensor_tensor(w_t[i][1][:, :], e_bank[:, :], w_t[i][0][:, :].bitcast(F32),
                                      ALU.subtract).then_inc(enter["dve"], 1)
                elif (stage, step) == ("enter", "logits"):
                    after(dve, enter, "pe", "logits", turn)
                    then("logits", dve.tensor_tensor(
                        logits[:, :, :], e_bank[:, 0:HQ * E].rearrange("p (t e) -> p t e", t=HQ),
                        rows["gate_b"][:, None, :].broadcast_to([P, HQ, E]), ALU.add))
                    then("top", dve.tensor_reduce(top[:, :], logits[:, :, :], AX.X, ALU.max))
                    dve.tensor_tensor(rest[:, :, :], logits[:, :, :], wide(top),
                                      ALU.subtract).then_inc(enter["dve"], 1)
                elif (stage, step) == ("enter", "sum"):
                    after(dve, enter, "pool", "exp", turn)
                    then("sum", dve.tensor_reduce(top[:, :], exped[:, :, :], AX.X, ALU.add))
                    then("recip", dve.reciprocal(chosen[:, :, 0], top[:, :]))
                    then("probs", dve.tensor_tensor(probs[:, :, :], exped[:, :, :],
                                                    chosen[:, :, 0:1].broadcast_to([P, HQ, E]), ALU.mult))
                    then("rest", dve.tensor_copy(rest[:, :, :], probs[:, :, :]))
                elif (stage, step) == ("enter", "top0"):
                    pick(0)
                    then("chosen0", dve.tensor_copy(chosen[:, :, :], key[:, :, :]))
                    dve.scalar_tensor_tensor(rest[:, :, :], key[:, :, :], -4.0, rest[:, :, :],
                                             ALU.mult, ALU.add).then_inc(enter["dve"], 1)
                elif (stage, step) == ("enter", "top1"):
                    after(dve, enter, "dve", "drop0", turn)
                    pick(1)
                    then("chosen1", dve.tensor_tensor(chosen[:, :, :], chosen[:, :, :], key[:, :, :], ALU.add))
                    after(dve, enter, "pe", "turn_comb", turn - 1)
                    dve.tensor_tensor(comb[:, :, :], probs[:, :, :], chosen[:, :, :],
                                      ALU.mult).then_inc(enter["dve"], 1)
                elif (stage, step) == ("enter", "comb_lo"):
                    after(dve, enter, "act", "comb_hi", turn)
                    after(dve, hidden, "pe", f"weight{E - 1}", turn - 2)
                    dve.tensor_tensor(comb_t[i][1][:, :], e_bank[0:E, :], comb_t[i][0][:, :].bitcast(F32),
                                      ALU.subtract).then_inc(enter["dve"], 1)
                elif (stage, step) == ("enter", "acc"):
                    after(dve, enter, "pe", "bias2", turn)
                    after(dve, leave, "pe", "turn_acc", turn - 2)
                    dve.tensor_copy(acc[i][:, :], e_bank[:, :]).then_inc(enter["dve"], 1)
                elif (stage, step) == ("leave", "stats1"):
                    after(dve, leave, "pe", "turn_acc", turn)
                    layer_stats(leave, turn, ("stats1",), lambda t: l_bank[:, t * P:(t + 1) * P], l_stats,
                                l_mv, ("dve", "centre2", turn - 1))
                elif (stage, step) == ("leave", "centre1"):
                    after(dve, leave, "pool", "rstd1", turn)
                    after(dve, leave, "pool", "out", turn - 1)
                    centre(leave, turn, lambda t: l_bank[:, t * P:(t + 1) * P], l_mv, l_rstd,
                           lambda t: z[:, t, :])
                elif (stage, step) == ("leave", "stats2"):
                    after(dve, leave, "pool", "z", turn)
                    layer_stats(leave, turn, ("stats2",), lambda t: z[:, t, :], l_stats,
                                l_mv, ("dve", "centre1", turn))
                elif (stage, step) == ("leave", "centre2"):
                    after(dve, leave, "pool", "rstd2", turn)
                    centre(leave, turn, lambda t: z[:, t, :], l_mv, l_rstd, lambda t: z[:, t, :])
                elif stage == "hidden":
                    f, e = int(step[2]), int(step[4:])
                    before, p = (turn, e - 2) if e >= 2 else (turn - 1, E + e - 2)
                    after(dve, output, "pe", f"y{p}", before)
                    after(dve, hidden, rounder(f, e), f"hi{f}_{e}", turn)
                    dve.tensor_tensor(hid_lo[e % 2][:, f, :], hid[:, f, :],
                                      hid_hi[e % 2][:, f, :].bitcast(F32),
                                      ALU.subtract).then_inc(hidden["dve"], 1)
                elif stage == "output" and step.startswith("weighed"):
                    e = int(step[7:])
                    before, p = (turn, e - 1) if e else (turn - 1, E - 1)
                    after(dve, output, "pe", f"y{e}", turn)
                    after(dve, hidden, "act", f"weight{e}", turn)
                    after(dve, output, "dve", f"acc{p}", before)
                    dve.tensor_tensor(weighed[:, :], y_bank[:, :], weight[e % 2][:, :],
                                      ALU.mult).then_inc(output["dve"], 1)
                elif stage == "output":
                    e = int(step[3:])
                    if e == 0:
                        after(dve, enter, "dve", "acc", turn)
                    after(dve, output, "dve", f"weighed{e}", turn)
                    dve.tensor_tensor(acc[i][:, :], acc[i][:, :], weighed[:, :],
                                      ALU.add).then_inc(output["dve"], 1)

            run(dve, "dve", emit)

        @block.gpsimd
        def _(pool):
            advance(pool, "pool")
            pool.tensor_copy(select[:, :, :], rows["select"])
            pool.tensor_copy(gw[0][:, :], gate_w[:, :]).then_inc(small_hi, 1)
            pool.tensor_copy(bb[0][:, :], b2[:, :]).then_inc(small_hi, 1)

            def passed(*what):
                after(pool, *what)
                pool.sem_inc(pool_passed, 1)

            def binary(out, a, b, op, stage):
                pool.tensor_tensor(out, a, b, op).then_inc(stage["pool"], 1)

            def inverse_root(stage, mv, var, rs, names, turn):
                binary(var[:, :], mv[:, :, 1], pows["eps"][:, 0:1].broadcast_to([P, HQ]), ALU.add, stage)
                passed(stage, "pool", names, turn)
                binary(rs[:, :], var[:, :], pows["half"][:, 0:1].broadcast_to([P, HQ]), ALU.pow, stage)

            def emit(stage, step, turn):
                i = turn.side
                if (stage, step) == ("enter", "var"):
                    passed(enter, "dve", "mean", turn)
                    passed(enter, "dve", "centre", turn - 1)
                    inverse_root(enter, mean_var, var, rstd, "var", turn)
                elif (stage, step) == ("enter", "gain"):
                    passed(enter, "dve", "centre", turn)
                    binary(y[:, :, :], y[:, :, :], row(rows["ln1_g"]), ALU.mult, enter)
                elif (stage, step) == ("enter", "shift"):
                    passed(enter, "pool", "gain", turn)
                    binary(y[:, :, :], y[:, :, :], row(rows["ln1_b"]), ALU.add, enter)
                elif (stage, step) == ("enter", "w"):
                    passed(enter, "pool", "shift", turn)
                    passed(leave, "pool", "z", turn - 2)
                    passed(enter, "pe", "turn_w", turn - 2)
                    pool.wait_ge(in_sems[1][i], turn.landed())
                    pool.sem_inc(pool_passed, 1)
                    binary(w_tok[i][:, :, :], y[:, :, :], u_in[i][:, :, :], ALU.add, enter)
                elif (stage, step) == ("enter", "exp"):
                    passed(enter, "dve", "less_top", turn)
                    passed(enter, "dve", "probs", turn - 1)
                    binary(exped[:, :, :], pows["e"][:, 0:1, None].broadcast_to([P, HQ, E]), rest[:, :, :],
                           ALU.pow, enter)
                elif (stage, step) == ("leave", "var1"):
                    passed(leave, "dve", "mean1", turn)
                    passed(leave, "dve", "centre2", turn - 1)
                    inverse_root(leave, l_mv, l_var, l_rstd, "var1", turn)
                elif (stage, step) == ("leave", "gain"):
                    passed(leave, "dve", "centre1", turn)
                    binary(z[:, :, :], z[:, :, :], row(rows["ln2_g"]), ALU.mult, leave)
                elif (stage, step) == ("leave", "shift"):
                    passed(leave, "pool", "gain", turn)
                    binary(z[:, :, :], z[:, :, :], row(rows["ln2_b"]), ALU.add, leave)
                elif (stage, step) == ("leave", "z"):
                    passed(leave, "pool", "shift", turn)
                    binary(z[:, :, :], z[:, :, :], w_tok[i][:, :, :], ALU.add, leave)
                elif (stage, step) == ("leave", "var2"):
                    passed(leave, "dve", "mean2", turn)
                    inverse_root(leave, l_mv, l_var, l_rstd, "var2", turn)
                elif (stage, step) == ("leave", "out"):
                    passed(leave, "dve", "centre2", turn)
                    pool.wait_ge(in_sems[2][i], turn.landed())
                    pool.sem_inc(pool_passed, 1)
                    if not (type(turn.pair) is int and turn.c < 2):
                        pool.wait_ge(stored[i], (turn - 2).landed())
                        pool.sem_inc(pool_passed, 1)
                    binary(z_out[i][:, :, :], z[:, :, :], x_in[i][:, :, :], ALU.add, leave)
                elif stage == "hidden":
                    f, e = int(step[2]), int(step[4:])
                    before, p = (turn, e - 2) if e >= 2 else (turn - 1, E + e - 2)
                    passed(output, "pe", f"y{p}", before)
                    passed(hidden, "act", f"gelu{f}_{e}", turn)
                    binary(hid_hi[e % 2][:, f, :], hid[:, f, :],
                           pows["zero"][:, 0:1].broadcast_to([P, HALF]), ALU.add, hidden)

            run(pool, "pool", emit)


def build(nc, x, w, consts, out):
    with ExitStack() as ctx:
        def sb(name, shape, dt=F32):
            return ctx.enter_context(nc.sbuf_tensor(name, shape, dt))

        def sem(name):
            return ctx.enter_context(nc.semaphore(name))

        kept = nc.dram_tensor("kept", [P, NT, D], F32, kind="Internal").ap()
        kept_u = nc.dram_tensor("kept_u", [P, NT, D], F32, kind="Internal").ap()
        x_v = x.rearrange("b (t p) d -> p (b t) d", p=P)
        out_v = out.rearrange("b (t p) d -> p (b t) d", p=P)
        tokens = sb("tokens", [P, NT, D])
        ident = sb("ident", [P, P])
        rank = sb("rank", [P, E])
        ln_rows = {n: sb(n, [P, D]) for n in ("ln1_g", "ln1_b", "ln2_g", "ln2_b")}
        wo1 = sb("wo1", [P, D])
        bo1 = sb("bo1", [P, D])
        pow_cols = sb("pow_cols", [P, 4])
        early = ExitStack()

        def sb_early(name, shape, dt=F32):
            return early.enter_context(nc.sbuf_tensor(name, shape, dt))

        turned = [sb_early(f"turned_{k}", [P, NT * P], F32R) for k in ("hi", "lo")]
        split_sign = sb_early("split_sign", [P, 3])
        head_mask = sb_early("head_mask", [P, GH])
        ones_row = sb_early("ones_row", [1, P])
        slope_rows = sb_early("slope_rows", [6, G, P], BF16)
        iota_rows = sb_early("iota_rows", [6, T], BF16)
        ident16 = sb_early("ident16", [P, P], BF16)
        causal_mask = sb_early("causal_mask", [P, P], BF16)
        w3 = [[sb_early(f"w3_{k}{i}", [P, 2, G, P], F32R) for k in ("hi", "lo")] for i in range(2)]
        bias2 = [sb_early(f"bias2_{i}", [P, 2, G]) for i in range(2)]
        wv = [sb_early(f"wv{i}", [P, D]) for i in range(2)]
        wo = [sb_early("wo0", [P, D]), wo1]
        bv = [sb_early(f"bv{i}", [P, D]) for i in range(2)]
        bo0 = sb_early("bo0", [P, D])
        sides = ("L0_attn_", "L0_ffn_")

        with ExitStack() as c2:
            raw = [[c2.enter_context(nc.sbuf_tensor(f"raw{i}{m}", [P, D], F32)) for m in range(2)] for i in range(2)]
            raw_b = c2.enter_context(nc.sbuf_tensor("raw_b", [1, 2, 2, D], F32))
            row3 = c2.enter_context(nc.sbuf_tensor("row3", [1, 2, 2, G, P], F32))
            cols = c2.enter_context(nc.psum_tensor("cols", [P, 2 * 2 * G], F32))
            pads_landed = c2.enter_context(nc.semaphore("pads_landed"))
            others_landed = c2.enter_context(nc.semaphore("others_landed"))
            x_first = c2.enter_context(nc.sbuf_tensor("x_first", [P, NT, D], F32))
            w3_32 = [c2.enter_context(nc.sbuf_tensor(f"w3_32_{i}", [P, 2, G, P], F32)) for i in range(2)]
            padded = c2.enter_context(nc.semaphore("padded"))
            padded_hi = c2.enter_context(nc.semaphore("padded_hi"))
            zeroed = c2.enter_context(nc.semaphore("zeroed"))
            spread = c2.enter_context(nc.semaphore("spread"))
            turned_in = c2.enter_context(nc.semaphore("turned_in"))
            x_landed = [c2.enter_context(nc.semaphore(f"x_landed{b}")) for b in range(B)]
            first_landed = c2.enter_context(nc.semaphore("first_landed"))
            f32_slopes = c2.enter_context(nc.sbuf_tensor("f32_slopes", [6, G, P], F32))
            f32_iota = c2.enter_context(nc.sbuf_tensor("f32_iota", [6, T], F32))
            f32_mask = c2.enter_context(nc.sbuf_tensor("f32_mask", [P, P], F32))

            def across(name, n=D):
                return w[name].rearrange("(a d) -> a d", a=1).broadcast_to([P, n])

            first = [(pow_cols[:, :], consts["pow_cols"]), (ident[:, :], consts["ident"]),
                     (wv[0][:, :], w["L0_attn_Wv"]), (bv[0][:, :], across("L0_attn_bv"))]
            pads = [(raw[i][m][:, :], w[sides[i] + n]) for i in range(2) for m, n in ((0, "Wq"), (1, "Wk"))]
            pads += [(raw_b[0:1, i, m, :], w[sides[i] + n].rearrange("(a d) -> a d", a=1))
                     for i in range(2) for m, n in ((0, "bq"), (1, "bk"))]
            pads += [(f32_slopes[:, :, :], consts["slope_rows"]), (f32_iota[:, :], consts["iota_rows"]),
                     (f32_mask[:, :], consts["causal"]), (ones_row[:, :], consts["ones_row"])]
            others = [(wv[1][:, :], w["L0_ffn_Wv"]), (bv[1][:, :], across("L0_ffn_bv")),
                      (wo[0][:, :], w["L0_attn_Wo"]), (bo0[:, :], across("L0_attn_bo")),
                      (wo[1][:, :], w["L0_ffn_Wo"]), (bo1[:, :], across("L0_ffn_bo")),
                      (split_sign[:, :], consts["split_sign"]), (head_mask[:, :], consts["head_mask"]),
                      (rank[:, :], consts["rank"])]
            others += [(t[:, :], across("L0_ffn_" + n)) for n, t in ln_rows.items()]

            def sync(sp):
                for b in range(B):
                    sp.dma_start(x_first[:, b * TB:(b + 1) * TB, :],
                                 x_v[:, b * TB:(b + 1) * TB, :]).then_inc(x_landed[b], 16)
                for dst, src in pads[0::2]:
                    sp.dma_start(dst, src).then_inc(pads_landed, 16)
                for dst, src in others:
                    sp.dma_start(dst, src).then_inc(others_landed, 16)
                sp.wait_ge(others_landed, 16 * len(others))

            def scalar(act):
                for dst, src in first:
                    act.dma_start(dst, src).then_inc(first_landed, 16)
                for dst, src in pads[1::2]:
                    act.dma_start(dst, src).then_inc(pads_landed, 16)
                act.wait_ge(first_landed, 16 * len(first))

            def tensor(pe):
                pe.wait_ge(first_landed, 16 * len(first))

            def vector(dve):
                dve.wait_ge(first_landed, 16 * len(first))

            def gpsimd(pool):
                for i in range(2):
                    pool.memset(w3_32[i][:, :, :, :], 0.0)
                pool.memset(row3[:, :, :, :, :], 0.0).then_inc(zeroed, 1)
                pool.wait_ge(zeroed, 1)
                pool.wait_ge(pads_landed, 16 * len(pads))
                pool.wait_ge(first_landed, 16 * len(first))
                for i in range(2):
                    for m in range(2):
                        row = row3[0:1, i, m, :, :].rearrange("p g (j r) -> p (g j) r", j=GH)
                        for k in range(3):
                            src = raw_b[0:1, i, m, :].rearrange("p (h d) -> p h d", h=H)
                            if m == 0:
                                pool.tensor_scalar(row[:, :, k * DH:(k + 1) * DH], src, SCALE, None, ALU.mult)
                            else:
                                pool.tensor_copy(row[:, :, k * DH:(k + 1) * DH], src)
                        one, at = (1.0, ROW_BIAS) if m == 0 else (-1.0, ROW_MAX)
                        op = pool.memset(row[:, :, at:at + 2], one)
                op.then_inc(spread, 1)
                for i in range(2):
                    for m in range(2):
                        dst = w3_32[i][:, m, :, :].rearrange("p g (j r) -> p (g j) r", j=GH)
                        for k in range(3):
                            pool.tensor_copy(dst[:, :, k * DH:(k + 1) * DH],
                                             raw[i][m][:, :].rearrange("p (h d) -> p h d", h=H)).then_inc(padded, 1)
                for i in range(2):
                    pool.wait_ge(padded, 6 * (i + 1))
                    pool.tensor_tensor(w3[i][0][:, :, :, :], w3_32[i][:, :, :, :],
                                       pow_cols[:, 3:4, None, None].broadcast_to([P, 2, G, P]),
                                       ALU.add).then_inc(padded_hi, 1)

            def vector_end(dve):
                dve.wait_ge(pads_landed, 16 * len(pads))
                dve.tensor_copy(ident16[:, :], ident[:, :])
                dve.tensor_copy(causal_mask[:, :], f32_mask[:, :])
                dve.tensor_copy(slope_rows[:, :, :], f32_slopes[:, :, :])
                dve.tensor_copy(iota_rows[:, :], f32_iota[:, :])
                for i in range(2):
                    dve.wait_ge(padded_hi, i + 1)
                    dve.tensor_tensor(w3[i][1][:, :, :, :], w3_32[i][:, :, :, :],
                                      w3[i][0][:, :, :, :].bitcast(F32), ALU.subtract)

            def tensor_between(pe, n):
                columns = [(i, m, g) for i in range(2) for m in range(2) for g in range(G)]
                if n < 2:
                    return
                if n == 2:
                    pe.wait_ge(spread, 1)
                for i, m, g in columns[(n - 2) * 3:(n - 1) * 3]:
                    c = (i * 2 + m) * G + g
                    mm = pe.matmul(cols[:, c:c + 1], row3[0:1, i, m, g, :], ones_row[0:1, 0:1],
                                   start=True, stop=True)
                    if c == len(columns) - 1:
                        mm.then_inc(turned_in, 1)

            def scalar_end(act):
                act.wait_ge(turned_in, 1)
                v = cols[:, :].rearrange("p (i m g) -> p i m g", i=2, m=2)
                for i in range(2):
                    op = act.activation(bias2[i][:, :, :], v[:, i, :, :], ACT.Identity)
                op.then_inc(turned_in, 1)

            extra = dict(sync=sync, scalar=scalar, tensor=tensor, vector=vector, gpsimd=gpsimd,
                         tensor_between=tensor_between, vector_end=vector_end, scalar_end=scalar_end, x_landed=x_landed)
            rows_pass(nc, "first", None, x_first, turned, tokens, None, None, wv[0], bv[0], pow_cols[:, 0:1],
                      pow_cols[:, 3:4], ident, extra=extra)
        attention(nc, "at1", Plan(True), turned, tokens, tokens, w3[0], bias2[0], slope_rows, iota_rows,
                  split_sign, head_mask, ident, ident16, causal_mask)
        rows_pass(nc, "second", tokens, x_v, turned, tokens, wo[0], bo0, wv[1], bv[1], pow_cols[:, 0:1],
                  pow_cols[:, 3:4], ident, kept, kept_u)
        attention(nc, "at2", Plan(False), turned, tokens, tokens, w3[1], bias2[1], slope_rows, iota_rows,
                  split_sign, head_mask, ident, ident16, causal_mask)
        early.close()
        gate_w = sb("gate_w", [P, E])
        b2 = sb("b2", [E, D])
        b1t = sb("b1t", [P, FT, E])
        gate_row = sb("gate_row", [P, E])
        select = sb("select", [E, E, P])
        with ExitStack() as c2:
            b1 = c2.enter_context(nc.sbuf_tensor("b1", [E, FF], F32))
            cols = c2.enter_context(nc.psum_tensor("b1cols", [P, FT, E], F32))
            got = c2.enter_context(nc.semaphore("moe_got"))
            tr = c2.enter_context(nc.semaphore("moe_tr"))
            block = c2.enter_context(nc.Block())
            wanted = [(gate_w[:, :], w["L0_ffn_gate_w"]), (b2[:, :], w["L0_ffn_b2"]), (b1[:, :], w["L0_ffn_b1"]),
                      (gate_row[:, :], w["L0_ffn_gate_b"].rearrange("(a d) -> a d", a=1).broadcast_to([P, E])),
                      (select[:, :, :], consts["select"])]

            @block.sync
            def _(sp):
                for dst, src in wanted:
                    sp.dma_start(dst, src).then_inc(got, 16)

            @block.tensor
            def _(pe):
                pe.wait_ge(got, 16 * len(wanted))
                for f in range(FT):
                    mm = pe.transpose(cols[:, f, :], b1[:, f * P:(f + 1) * P], ident[0:E, 0:E])
                mm.then_inc(tr, 1)

            @block.vector
            def _(dve):
                dve.wait_ge(tr, 1)
                dve.tensor_copy(b1t[:, :, :], cols[:, :, :]).then_inc(tr, 1)
        rows = dict(ln_rows, bo=bo1, gate_b=gate_row, select=select[:, :, :])
        pows = {k: pow_cols[:, i:i + 1] for i, k in enumerate(("eps", "half", "e", "zero"))}
        tail(nc, tokens, kept_u, kept, out_v, wo[1], rows, gate_w, ident, rank, pows, b1t, b2,
             w["L0_ffn_W1"], w["L0_ffn_W2"])


_INS = ["L0_attn_x", "L0_attn_Wq", "L0_attn_bq", "L0_attn_Wk", "L0_attn_bk", "L0_attn_Wv", "L0_attn_bv",
        "L0_attn_Wo", "L0_attn_bo", "L0_ffn_Wq", "L0_ffn_bq", "L0_ffn_Wk", "L0_ffn_bk", "L0_ffn_Wv",
        "L0_ffn_bv", "L0_ffn_Wo", "L0_ffn_bo", "L0_ffn_ln1_g", "L0_ffn_ln1_b", "L0_ffn_ln2_g",
        "L0_ffn_ln2_b", "L0_ffn_gate_w", "L0_ffn_gate_b", "L0_ffn_W1", "L0_ffn_b1", "L0_ffn_W2",
        "L0_ffn_b2"]


def shape_constants():
    import numpy as np
    lane = np.arange(P)
    row = lane % HW
    query_lo = (row >= 2 * DH) & (row < 3 * DH)
    key_lo = ((row >= DH) & (row < 2 * DH)) | (row == ROW_BIAS + 1)
    slope = np.zeros((1, G, GH, HW), np.float32)
    slope[0, :, :, ROW_BIAS:ROW_BIAS + 2] = -np.array(slopes(), np.float32).reshape(G, GH, 1)
    parts, rest = [], slope.reshape(G, P)
    for _ in range(3):
        part = (rest.view(np.uint32) & np.uint32(0xFFFF0000)).view(np.float32)
        parts.append(part)
        rest = rest - part
    assert not rest.any()
    parts = np.stack(parts)
    return {
        "ident": np.eye(P, dtype=np.float32),
        "split_sign": -np.stack([query_lo, key_lo, 0 * lane], 1).astype(np.float32),
        "head_mask": (lane[:, None] // HW == np.arange(GH)).astype(np.float32),
        "rank": np.tile(np.arange(E, 0, -1, dtype=np.float32), (P, 1)),
        "ones_row": np.ones((1, P), np.float32),
        "pow_cols": np.tile(np.array([EPS, -0.5, np.e, 0.0], np.float32), (P, 1)),
        "select": np.repeat(np.eye(E, dtype=np.float32)[:, :, None], P, 2),
        "iota_rows": np.repeat(np.stack([np.arange(T) % 256, np.arange(T) // 256]), 3, 0).astype(np.float32),
        "slope_rows": np.concatenate([parts, 256 * parts]),
        "causal": np.where(lane[None, :] > lane[:, None], np.float32(BIG), np.float32(0)).astype(np.float32),
    }


def kernel(**inputs):
    import numpy as np
    import concourse.bacc as bacc
    from concourse.bass_utils import run_bass_kernel_spmd

    nc = bacc.Bacc("TRN2", target_bir_lowering=False, num_devices=1)
    nc.disable_value_cache = True
    arrays, aps = {}, {}
    for name in _INS:
        arrays[name] = np.ascontiguousarray(inputs[name])
    for name, a in shape_constants().items():
        arrays["const_" + name] = a
    for name, a in arrays.items():
        aps[name] = nc.dram_tensor(name, a.shape, mybir.dt.from_np(a.dtype), kind="ExternalInput").ap()
    out = nc.dram_tensor("out_0", (B, T, D), F32, kind="ExternalOutput").ap()
    consts = {k[6:]: v for k, v in aps.items() if k.startswith("const_")}
    build(nc, aps["L0_attn_x"], aps, consts, out)
    r = run_bass_kernel_spmd(nc, [arrays], core_ids=[0])
    return r.results[0]["out_0"]
```
